# Optimizing a Trainium2 kernel written in Bass

```python
import numpy as np
import jax
import jax.numpy as jnp

def _softmax(x, axis=-1):
    return jax.nn.softmax(x, axis=axis)

def _gelu(x):
    return jax.nn.gelu(x, approximate=True)

def _silu(x):
    return jax.nn.silu(x)

def _sigmoid(x):
    return jax.nn.sigmoid(x)

def _layernorm(x, axis=-1, eps=1e-05):
    m = jnp.mean(x, axis=axis, keepdims=True)
    v = jnp.var(x, axis=axis, keepdims=True)
    return (x - m) / jnp.sqrt(v + eps)

def _scatter_add(tgt, idx, src, axis=0):
    return tgt.at[idx].add(src)

def _segment_sum(src, seg, n):
    return jax.ops.segment_sum(src, seg, n)
kernel_name = 'mk_flamingo_gated_d2_seqx_r8_b7154d'

def setup_inputs(seed: int=0):
    np.random.seed(seed)
    _w = jnp.asarray

    def _rec_inputs():
        import jax
        import jax.numpy as jnp
        _rk = jax.random.key(seed)
        x = -0.000125 + 0.9999 * jax.random.normal(jax.random.fold_in(_rk, 1), (16, 128, 256), jnp.float32)
        _lenS = 128 - jax.random.randint(jax.random.fold_in(_rk, 7), (16,), 0, max(1, 128 // 4) + 1, jnp.int32)
        _lenS2 = 128 - jax.random.randint(jax.random.fold_in(_rk, 8), (16,), 0, max(1, 128 // 4) + 1, jnp.int32)
        _ctx_2048P = jax.random.normal(jax.random.fold_in(_rk, 11), (16, 16, 256), jnp.float32)
        _ctx_2048c = jax.random.dirichlet(jax.random.fold_in(_rk, 511), 0.3 * jnp.ones((16,), jnp.float32), (16, 128))
        _ctx_2048t = jnp.einsum('bsk,bkd->bsd', _ctx_2048c, _ctx_2048P)
        _ctx_2048t = _ctx_2048t * jax.lax.rsqrt(jnp.mean(jnp.square(_ctx_2048t)) + 1e-12) * 0.953939
        ctx_2048 = -1.52775e-05 + 0.999936 * (_ctx_2048t + 0.3 * jax.random.normal(jax.random.fold_in(_rk, 611), (16, 128, 256), jnp.float32))
        _validS = jnp.arange(128)[None, :] < _lenS[:, None]
        _validS2 = jnp.arange(128)[None, :] < _lenS2[:, None]
        _causal = jnp.tril(jnp.ones((128, 128), dtype=bool))
        mask_Bx1xSxS_fk0 = jnp.where(jnp.broadcast_to(_validS[:, None, None, :], (16, 1, 128, 128)), -1000000000.0, 0.0).astype(jnp.float32)
        _g = jax.random.normal(jax.random.fold_in(_rk, 9001), (2, 2), jnp.float32)
        _g = jnp.sign(_g) * jnp.maximum(jnp.abs(_g), 1.0) + (_g == 0) * 1.0
        g_xattn = _g[0]
        g_ffn = _g[1]
        return (x, ctx_2048, mask_Bx1xSxS_fk0, g_xattn, g_ffn)
    x, ctx_2048, mask_Bx1xSxS_fk0, g_xattn, g_ffn = _rec_inputs()

    def _L0_xattn_setup():
        import jax, jax.numpy as jnp
        import numpy as np
        B, DIM1, DIM2, LATENT, T = (16, 128, 128, 64, 256)
        LN_EPS = 1e-05
        key = jax.random.key(seed)
        ks = jax.random.split(key, 8)

        def xavier(k, shape):
            fan_out, fan_in = shape
            std = float(np.sqrt(2.0 / (fan_in + fan_out)))
            return jax.random.normal(k, shape, dtype=jnp.float32) * std
        return {'input1': jax.random.normal(ks[0], (B, DIM1, T), dtype=jnp.float32), 'input2': jax.random.normal(ks[1], (B, DIM2, T), dtype=jnp.float32), 'theta_w': xavier(ks[2], (LATENT, DIM2)), 'theta_b': jnp.zeros((LATENT,), jnp.float32), 'phi_w': xavier(ks[3], (LATENT, DIM1)), 'phi_b': jnp.zeros((LATENT,), jnp.float32), 'g_w': xavier(ks[4], (LATENT, DIM1)), 'g_b': jnp.zeros((LATENT,), jnp.float32), 'ln_gamma': jnp.ones((LATENT, T), jnp.float32), 'ln_beta': jnp.zeros((LATENT, T), jnp.float32), 'out_w': xavier(ks[5], (DIM2, LATENT)), 'out_b': jnp.zeros((DIM2,), jnp.float32)}
    _L0_xattn_all = _L0_xattn_setup()
    _L0_xattn_in = {k: v for k, v in _L0_xattn_all.items() if k in ('theta_w', 'theta_b', 'phi_w', 'phi_b', 'g_w', 'g_b', 'ln_gamma', 'ln_beta', 'out_w', 'out_b')}
    del _L0_xattn_all

    def _L0_ffn_setup():
        import jax, jax.numpy as jnp
        import numpy as np
        E, K, H, I = (64, 6, 256, 176)
        NS = 2
        IS = NS * I
        CAP = 32
        T_TOKENS = (1, 128)
        SCALE = 0.02

        def _moe_infer(x, gate_w, w_gate, w_up, w_down):
            T = x.shape[0]
            TK = T * K
            logits = x @ gate_w.T
            scores = jax.nn.softmax(logits, axis=-1)
            topk_w, topk_i = jax.lax.top_k(scores, K)
            flat_i = topk_i.reshape(-1)
            flat_w = topk_w.reshape(-1)
            token_ids = jnp.arange(TK, dtype=jnp.int32) // K
            order = jnp.argsort(flat_i)
            sorted_e = flat_i[order]
            counts = jnp.bincount(flat_i, length=E)
            starts = jnp.concatenate([jnp.zeros((1,), counts.dtype), jnp.cumsum(counts)[:-1]])
            pos_sorted = jnp.arange(TK) - starts[sorted_e]
            pos = jnp.zeros((TK,), jnp.int32).at[order].set(pos_sorted.astype(jnp.int32))
            valid = pos < CAP
            slot = jnp.where(valid, pos, CAP)
            buf = jnp.zeros((E, CAP + 1, H), x.dtype).at[flat_i, slot].set(x[token_ids])
            g = jnp.einsum('ech,ehi->eci', buf, w_gate)
            u = jnp.einsum('ech,ehi->eci', buf, w_up)
            y = jnp.einsum('eci,eih->ech', jax.nn.silu(g) * u, w_down)
            out_slots = y[flat_i, slot] * (flat_w * valid)[:, None]
            return out_slots.reshape(T, K, H).sum(axis=1)
        key = jax.random.key(seed)
        ks = jax.random.split(key, 8)
        f32 = jnp.float32
        return {'hidden_states': jax.random.normal(ks[0], (*T_TOKENS, H), f32), 'gate_w': jax.random.normal(ks[1], (E, H), f32) * SCALE, 'w_gate': jax.random.normal(ks[2], (E, H, I), f32) * SCALE, 'w_up': jax.random.normal(ks[3], (E, H, I), f32) * SCALE, 'w_down': jax.random.normal(ks[4], (E, I, H), f32) * SCALE, 'sw_gate': jax.random.normal(ks[5], (H, IS), f32) * SCALE, 'sw_up': jax.random.normal(ks[6], (H, IS), f32) * SCALE, 'sw_down': jax.random.normal(ks[7], (IS, H), f32) * SCALE}
    _L0_ffn_all = _L0_ffn_setup()
    _L0_ffn_in = {k: v for k, v in _L0_ffn_all.items() if k in ('gate_w', 'w_gate', 'w_up', 'w_down', 'sw_gate', 'sw_up', 'sw_down')}
    del _L0_ffn_all

    def _L1_xattn_setup():
        import jax, jax.numpy as jnp
        import numpy as np
        import math
        B, S, HID, H = (2, 256, 256, 32)
        D = HID // H
        AL = 10

        def _rope_tables(seq_len, dim, dtype):
            inv_freq = 1.0 / 10000.0 ** (np.arange(0, dim, 2, dtype=np.float32) / dim)
            t = np.arange(seq_len, dtype=np.float32)
            freqs = np.outer(t, inv_freq)
            emb = np.concatenate([freqs, freqs], -1)
            return (jnp.asarray(np.cos(emb), dtype), jnp.asarray(np.sin(emb), dtype))

        def _rotate_half(x):
            x1, x2 = jnp.split(x, 2, axis=-1)
            return jnp.concatenate([-x2, x1], axis=-1)
        key = jax.random.key(seed)
        ks = jax.random.split(key, 8)
        hidden_states = jax.random.normal(ks[0], (B, S, HID), dtype=jnp.float32)
        adapter = jax.random.normal(ks[1], (B, AL, HID), dtype=jnp.float32)
        causal = jnp.tril(jnp.ones((S, S), dtype=bool))
        attention_mask = jnp.broadcast_to(jnp.where(causal, 0.0, -1000000000.0).astype(jnp.float32)[None, None], (B, 1, S, S))
        scale = 0.02
        Wq = jax.random.normal(ks[2], (HID, HID), dtype=jnp.float32) * scale
        Wk = jax.random.normal(ks[3], (HID, HID), dtype=jnp.float32) * scale
        Wv = jax.random.normal(ks[4], (HID, HID), dtype=jnp.float32) * scale
        Wo = jax.random.normal(ks[5], (HID, HID), dtype=jnp.float32) * scale
        gate = jax.random.normal(ks[6], (1, H, 1, 1), dtype=jnp.float32) * 0.1
        return {'hidden_states': hidden_states, 'attention_mask': attention_mask, 'adapter': adapter, 'Wq': Wq, 'Wk': Wk, 'Wv': Wv, 'Wo': Wo, 'gate': gate}
    _L1_xattn_all = _L1_xattn_setup()
    _L1_xattn_in = {k: v for k, v in _L1_xattn_all.items() if k in ('Wq', 'Wk', 'Wv', 'Wo', 'gate')}
    del _L1_xattn_all

    def _L1_ffn_setup():
        import math
        import jax, jax.numpy as jnp
        import numpy as np
        CAPACITY_FACTOR = 1.25
        MIN_CAPACITY = 4

        def _capacity(num_tokens: int, num_experts: int) -> int:
            cap = math.floor(CAPACITY_FACTOR * num_tokens / num_experts)
            cap += cap % 2
            return max(cap, MIN_CAPACITY)
        key = jax.random.key(seed)
        k1, k2, k3, k4 = jax.random.split(key, 4)
        B, S, H, I, E = (2, 512, 256, 256, 8)
        inputs = jax.random.normal(k1, (B, S, H), dtype=jnp.float32)
        gate_weight = jax.random.normal(k2, (E, H), dtype=jnp.float32) * math.sqrt(0.1 / H)
        w1 = jax.random.normal(k3, (E, H, I), dtype=jnp.float32) * 0.02
        w2 = jax.random.normal(k4, (E, I, H), dtype=jnp.float32) * 0.02
        return {'inputs': inputs, 'gate_weight': gate_weight, 'w1': w1, 'w2': w2}
    _L1_ffn_all = _L1_ffn_setup()
    _L1_ffn_in = {k: v for k, v in _L1_ffn_all.items() if k in ('gate_weight', 'w1', 'w2')}
    del _L1_ffn_all
    return {'x': x, 'ctx_2048': ctx_2048, 'mask_Bx1xSxS_fk0': mask_Bx1xSxS_fk0, 'g_xattn': g_xattn, 'g_ffn': g_ffn, 'L0_xattn_theta_w': _L0_xattn_in['theta_w'], 'L0_xattn_theta_b': _L0_xattn_in['theta_b'], 'L0_xattn_phi_w': _L0_xattn_in['phi_w'], 'L0_xattn_phi_b': _L0_xattn_in['phi_b'], 'L0_xattn_g_w': _L0_xattn_in['g_w'], 'L0_xattn_g_b': _L0_xattn_in['g_b'], 'L0_xattn_ln_gamma': _L0_xattn_in['ln_gamma'], 'L0_xattn_ln_beta': _L0_xattn_in['ln_beta'], 'L0_xattn_out_w': _L0_xattn_in['out_w'], 'L0_xattn_out_b': _L0_xattn_in['out_b'], 'L0_ffn_gate_w': _L0_ffn_in['gate_w'], 'L0_ffn_w_gate': _L0_ffn_in['w_gate'], 'L0_ffn_w_up': _L0_ffn_in['w_up'], 'L0_ffn_w_down': _L0_ffn_in['w_down'], 'L0_ffn_sw_gate': _L0_ffn_in['sw_gate'], 'L0_ffn_sw_up': _L0_ffn_in['sw_up'], 'L0_ffn_sw_down': _L0_ffn_in['sw_down'], 'L1_xattn_Wq': _L1_xattn_in['Wq'], 'L1_xattn_Wk': _L1_xattn_in['Wk'], 'L1_xattn_Wv': _L1_xattn_in['Wv'], 'L1_xattn_Wo': _L1_xattn_in['Wo'], 'L1_xattn_gate': _L1_xattn_in['gate'], 'L1_ffn_gate_weight': _L1_ffn_in['gate_weight'], 'L1_ffn_w1': _L1_ffn_in['w1'], 'L1_ffn_w2': _L1_ffn_in['w2']}

def reference(x, ctx_2048, mask_Bx1xSxS_fk0, g_xattn, g_ffn, L0_xattn_theta_w, L0_xattn_theta_b, L0_xattn_phi_w, L0_xattn_phi_b, L0_xattn_g_w, L0_xattn_g_b, L0_xattn_ln_gamma, L0_xattn_ln_beta, L0_xattn_out_w, L0_xattn_out_b, L0_ffn_gate_w, L0_ffn_w_gate, L0_ffn_w_up, L0_ffn_w_down, L0_ffn_sw_gate, L0_ffn_sw_up, L0_ffn_sw_down, L1_xattn_Wq, L1_xattn_Wk, L1_xattn_Wv, L1_xattn_Wo, L1_xattn_gate, L1_ffn_gate_weight, L1_ffn_w1, L1_ffn_w2):
    import jax
    import jax.numpy as jnp

    def _L0_xattn_ref(input1, input2, theta_w, theta_b, phi_w, phi_b, g_w, g_b, ln_gamma, ln_beta, out_w, out_b):
        import jax, jax.numpy as jnp
        import numpy as np
        B, DIM1, DIM2, LATENT, T = (16, 128, 128, 64, 256)
        LN_EPS = 1e-05
        theta_x = jnp.einsum('ld,bdt->btl', theta_w, input2) + theta_b
        phi_x = jnp.einsum('ld,bdt->blt', phi_w, input1) + phi_b[:, None]
        scores = jnp.einsum('btl,bls->bts', theta_x, phi_x)
        p = jax.nn.softmax(scores, axis=-1)
        g_x = jnp.einsum('ld,bdt->btl', g_w, input1) + g_b
        t_x = jnp.einsum('bts,bsl->blt', p, g_x)
        mu = jnp.mean(t_x, axis=(1, 2), keepdims=True)
        var = jnp.var(t_x, axis=(1, 2), keepdims=True)
        h = (t_x - mu) * jax.lax.rsqrt(var + LN_EPS) * ln_gamma + ln_beta
        h = jax.nn.relu(h)
        w_t = jnp.einsum('ol,blt->bot', out_w, h) + out_b[None, :, None]
        return w_t + input2

    def _L0_ffn_ref(hidden_states, gate_w, w_gate, w_up, w_down, sw_gate, sw_up, sw_down):
        import jax, jax.numpy as jnp
        import numpy as np
        E, K, H, I = (64, 6, 256, 176)
        NS = 2
        IS = NS * I
        CAP = 32
        T_TOKENS = (1, 128)
        SCALE = 0.02

        def _moe_infer(x, gate_w, w_gate, w_up, w_down):
            T = x.shape[0]
            TK = T * K
            logits = x @ gate_w.T
            scores = jax.nn.softmax(logits, axis=-1)
            topk_w, topk_i = jax.lax.top_k(scores, K)
            flat_i = topk_i.reshape(-1)
            flat_w = topk_w.reshape(-1)
            token_ids = jnp.arange(TK, dtype=jnp.int32) // K
            order = jnp.argsort(flat_i)
            sorted_e = flat_i[order]
            counts = jnp.bincount(flat_i, length=E)
            starts = jnp.concatenate([jnp.zeros((1,), counts.dtype), jnp.cumsum(counts)[:-1]])
            pos_sorted = jnp.arange(TK) - starts[sorted_e]
            pos = jnp.zeros((TK,), jnp.int32).at[order].set(pos_sorted.astype(jnp.int32))
            valid = pos < CAP
            slot = jnp.where(valid, pos, CAP)
            buf = jnp.zeros((E, CAP + 1, H), x.dtype).at[flat_i, slot].set(x[token_ids])
            g = jnp.einsum('ech,ehi->eci', buf, w_gate)
            u = jnp.einsum('ech,ehi->eci', buf, w_up)
            y = jnp.einsum('eci,eih->ech', jax.nn.silu(g) * u, w_down)
            out_slots = y[flat_i, slot] * (flat_w * valid)[:, None]
            return out_slots.reshape(T, K, H).sum(axis=1)
        orig_shape = hidden_states.shape
        x = hidden_states.reshape(-1, orig_shape[-1])
        y = _moe_infer(x, gate_w, w_gate, w_up, w_down).reshape(orig_shape)
        shared = jax.nn.silu(hidden_states @ sw_gate) * (hidden_states @ sw_up) @ sw_down
        return y + shared

    def _L1_xattn_ref(hidden_states, attention_mask, adapter, Wq, Wk, Wv, Wo, gate):
        import jax, jax.numpy as jnp
        import numpy as np
        import math
        B, S, HID, H = (2, 256, 256, 32)
        D = HID // H
        AL = 10

        def _rope_tables(seq_len, dim, dtype):
            inv_freq = 1.0 / 10000.0 ** (np.arange(0, dim, 2, dtype=np.float32) / dim)
            t = np.arange(seq_len, dtype=np.float32)
            freqs = np.outer(t, inv_freq)
            emb = np.concatenate([freqs, freqs], -1)
            return (jnp.asarray(np.cos(emb), dtype), jnp.asarray(np.sin(emb), dtype))

        def _rotate_half(x):
            x1, x2 = jnp.split(x, 2, axis=-1)
            return jnp.concatenate([-x2, x1], axis=-1)
        bsz, q_len, hid = hidden_states.shape
        n_heads = gate.shape[1]
        head_dim = hid // n_heads
        inv_sqrt_d = 1.0 / math.sqrt(head_dim)

        def split_heads(x, length):
            return x.reshape(bsz, length, n_heads, head_dim).transpose(0, 2, 1, 3)
        q = split_heads(hidden_states @ Wq, q_len)
        k = split_heads(hidden_states @ Wk, q_len)
        v = split_heads(hidden_states @ Wv, q_len)
        cos, sin = _rope_tables(q_len, head_dim, q.dtype)
        q = q * cos + _rotate_half(q) * sin
        k = k * cos + _rotate_half(k) * sin
        scores = jnp.einsum('bhqd,bhkd->bhqk', q, k) * inv_sqrt_d
        scores = scores + attention_mask
        scores = jnp.maximum(scores, jnp.finfo(scores.dtype).min)
        w = jax.nn.softmax(scores.astype(jnp.float32), axis=-1).astype(q.dtype)
        attn_output = jnp.einsum('bhqk,bhkd->bhqd', w, v)
        adapter_len = adapter.shape[1]
        a_k = split_heads(adapter @ Wk, adapter_len)
        a_v = split_heads(adapter @ Wv, adapter_len)
        a_scores = jnp.einsum('bhqd,bhkd->bhqk', q, a_k) * inv_sqrt_d
        a_scores = jnp.tanh(gate) * jax.nn.softmax(a_scores.astype(jnp.float32), axis=-1).astype(q.dtype)
        attn_output = attn_output + jnp.einsum('bhqk,bhkd->bhqd', a_scores, a_v)
        attn_output = attn_output.transpose(0, 2, 1, 3).reshape(bsz, q_len, hid)
        return attn_output @ Wo

    def _L1_ffn_ref(inputs, gate_weight, w1, w2):
        import math
        import jax, jax.numpy as jnp
        import numpy as np
        CAPACITY_FACTOR = 1.25
        MIN_CAPACITY = 4

        def _capacity(num_tokens: int, num_experts: int) -> int:
            cap = math.floor(CAPACITY_FACTOR * num_tokens / num_experts)
            cap += cap % 2
            return max(cap, MIN_CAPACITY)
        B, S, H = inputs.shape
        E = gate_weight.shape[0]
        tokens = inputs.reshape(-1, H)
        T = tokens.shape[0]
        C = _capacity(T, E)
        logits = tokens.astype(jnp.float32) @ gate_weight.astype(jnp.float32).T
        probs = jax.nn.softmax(logits, axis=-1)
        top1 = jnp.argmax(logits, axis=-1)
        mask = jax.nn.one_hot(top1, E, dtype=jnp.int32)
        ranks = jnp.cumsum(mask, axis=0) - 1
        mask = mask * (ranks < C).astype(jnp.int32)
        rank1 = jnp.sum(mask * ranks, axis=-1)
        weight = mask.astype(probs.dtype) * probs
        rank_oh = jax.nn.one_hot(rank1, C, dtype=probs.dtype)
        combine_weights = weight[:, :, None] * rank_oh[:, None, :]
        sec_mask = (combine_weights != 0).astype(inputs.dtype)
        dispatch = jnp.einsum('tec,th->ech', sec_mask, tokens)
        hmid = jax.nn.gelu(jnp.einsum('ech,ehi->eci', dispatch, w1), approximate=False)
        expert_out = jnp.einsum('eci,eih->ech', hmid, w2)
        out = jnp.einsum('tec,ech->th', combine_weights.astype(inputs.dtype), expert_out)
        return out.reshape(B, S, H)
    x = x + jnp.tanh(g_xattn[0]) * _L0_xattn_ref(_layernorm(x, axis=-1), ctx_2048, L0_xattn_theta_w, L0_xattn_theta_b, L0_xattn_phi_w, L0_xattn_phi_b, L0_xattn_g_w, L0_xattn_g_b, L0_xattn_ln_gamma, L0_xattn_ln_beta, L0_xattn_out_w, L0_xattn_out_b)
    x = x + jnp.tanh(g_ffn[0]) * _L0_ffn_ref(_layernorm(x, axis=-1), L0_ffn_gate_w, L0_ffn_w_gate, L0_ffn_w_up, L0_ffn_w_down, L0_ffn_sw_gate, L0_ffn_sw_up, L0_ffn_sw_down)
    x = x + jnp.tanh(g_xattn[1]) * _L1_xattn_ref(_layernorm(x, axis=-1), mask_Bx1xSxS_fk0, ctx_2048, L1_xattn_Wq, L1_xattn_Wk, L1_xattn_Wv, L1_xattn_Wo, L1_xattn_gate)
    x = x + jnp.tanh(g_ffn[1]) * _L1_ffn_ref(_layernorm(x, axis=-1), L1_ffn_gate_weight, L1_ffn_w1, L1_ffn_w2)
    return x

_drawn_inputs = setup_inputs


def setup_inputs(seed=0):
    import zlib

    import numpy as np

    out = dict(_drawn_inputs(seed))
    spreads = {'g_ffn': (-1.0, 0.6),
     'L0_xattn_theta_b': (0.0, 0.1),
     'L0_xattn_phi_b': (0.0, 2.0),
     'L0_xattn_g_b': (0.0, 0.1),
     'L0_xattn_ln_gamma': (1.0, 0.2),
     'L0_xattn_ln_beta': (0.0, 0.1),
     'L0_xattn_out_b': (0.0, 0.463)}
    factors = {'L0_ffn_gate_w': 8.0,
     'L0_ffn_w_gate': 8.0,
     'L0_ffn_w_up': 8.0,
     'L0_ffn_w_down': 8.0,
     'L0_ffn_sw_gate': 5.107,
     'L0_ffn_sw_up': 5.026,
     'L0_ffn_sw_down': 5.039,
     'L1_xattn_Wq': 8.0,
     'L1_xattn_Wk': 8.0,
     'L1_xattn_gate': 8.0,
     'L1_ffn_gate_weight': 8.0,
     'L1_ffn_w1': 8.0,
     'L1_ffn_w2': 8.0}
    for name, (base, spread) in spreads.items():
        noise = np.random.default_rng([zlib.crc32(name.encode()), seed]).standard_normal(out[name].shape)
        drawn = base * np.exp(spread * noise) if base else spread * noise
        out[name] = jnp.asarray(drawn.astype(out[name].dtype))
    for name, factor in factors.items():
        out[name] = (out[name] * factor).astype(out[name].dtype)
    return out
```

```python
import concourse.bass as bass
from concourse import mybir
from contextlib import ExitStack
import numpy as np

F32 = mybir.dt.float32
BF16 = mybir.dt.bfloat16
U32 = mybir.dt.uint32
I32 = mybir.dt.int32
ACT = mybir.ActivationFunctionType
ALU = mybir.AluOpType
AX = mybir.AxisListType

P = 128
B, S, H = 16, 128, 256
TOK = B * S
HC = H // P
LAT = 64
E1, K1, I1, CAP1 = 64, 6, 176, 32
SLOTS1 = E1 * CAP1
I1H = I1 // 2
IS = 352
ISC = [(0, 128), (128, 128), (256, 96)]
ROW = H + E1
NH, HD = 32, 8
E2, CAP2 = 8, 320
SLOTS2 = E2 * CAP2
CH2 = [(0, 128), (128, 128), (256, 64)]
EPS = 1e-5
RSQRT_MAGIC = 0x5F3759DF
F32_MIN = float(np.finfo(np.float32).min)
SKIP = 1.0e6

W1 = 4
R2 = 4


class Count:

    def __init__(self):
        self.n = 0

    def one(self):
        self.n += 1
        return 1

    def restart(self):
        n, self.n = self.n, 0
        return n


def rsqrt(nc, dve, done, count, y, v, half, t):
    vec = nc.vector
    vec.tensor_scalar(t.bitcast(I32), v.bitcast(I32), 1, None, ALU.arith_shift_right).then_inc(done, count.one())
    dve.wait_ge(done, count.n)
    vec.tensor_scalar(y.bitcast(I32), t.bitcast(I32), -1.0, float(RSQRT_MAGIC), ALU.mult, ALU.add).then_inc(done, count.one())
    dve.wait_ge(done, count.n)
    for _ in range(3):
        vec.scalar_tensor_tensor(t, y, -0.5, y, ALU.mult, ALU.mult).then_inc(done, count.one())
        dve.wait_ge(done, count.n)
        vec.tensor_tensor(half, t, v, ALU.mult).then_inc(done, count.one())
        dve.wait_ge(done, count.n)
        vec.scalar_tensor_tensor(y, half, 1.5, y, ALU.add, ALU.mult).then_inc(done, count.one())
        dve.wait_ge(done, count.n)


def build(nc, x, ctx, ctxT, mask, gates, theta_w, theta_b, phi_w, phi_b, g_w, g_b, gamma, beta, out_w, out_b,
          gate1_w, w_gu, w_d, sw_gu, sw_d, wqkv, wo, hgate, gate2_w, w1, w2, ident, upper, cos, sin, group, quarter,
          out):
    rows1 = nc.dram_tensor("rows1", [TOK + 1, ROW], F32, kind="Internal").ap()
    rows2 = nc.dram_tensor("rows2", [SLOTS2, H], F32, kind="Internal").ap()
    youts = nc.dram_tensor("youts", [SLOTS2 + 1, H], F32, kind="Internal").ap()

    with ExitStack() as whole:
        def sb(name, shape, dt=F32, where=whole):
            return where.enter_context(nc.sbuf_tensor(name, shape, dt))

        def sem(name):
            return whole.enter_context(nc.semaphore(name))

        pb = [whole.enter_context(nc.psum_tensor(f"bank{i}", [P, 512], F32)) for i in range(8)]

        X = sb("X", [P, B, H])
        idn = sb("idn", [P, P])
        upr = sb("upr", [P, P], BF16)
        ones_b = sb("ones_b", [P, P], BF16)
        tanh_g = sb("tanh_g", [P, 4])
        iota_e = sb("iota_e", [P, E1])
        idx1f = sb("idx1f", [P, B])
        idx1 = sb("idx1", [P, B], U32)
        rs_t, rs_h = sb("rs_t", [P, W1]), sb("rs_h", [P, W1])
        zrow = sb("zrow", [P, ROW])
        shared = sb("shared", [P, B * 3 * H], BF16)
        parts = shared[:, :].rearrange("p (j k h) -> p j k h", k=3, h=H)
        slot_g = sb("slot_g", [P, B], U32)
        wt2 = sb("wt2", [P, B])

        dve_done, pool_done = sem("dve_done"), sem("pool_done")
        pe_passed, pool_passed = sem("pe_passed"), sem("pool_passed")
        consts_in, zero_made, zero_out = sem("consts_in"), sem("zero_made"), sem("zero_out")
        tanh_made, hgate_made = sem("tanh_made"), sem("hgate_made")

        phase12 = ExitStack()
        wgu_sb = [sb(f"wgu{r}", [P, 4, HC, 2 * I1], where=phase12) for r in range(R2)]
        wd_sb = [sb(f"wd{r}", [I1H, 4, 2, H], where=phase12) for r in range(R2)]
        experts_in = [sem(f"experts_in{r}") for r in range(R2)]
        experts_free = sem("experts_free")

        with ExitStack() as ph:
            CX = shared[:, 0:2 * B * H].bitcast(F32).rearrange("p (b h) -> p b h", h=H)
            G = [shared[:, (2 * B + 8 * i) * H:(2 * B + 8 * i + 8) * H].rearrange("p (e c) -> p e c", c=CAP1) for i in range(2)]
            thw, phw, gw = (sb(n, [P, LAT], where=ph) for n in ("thw", "phw", "gw"))
            thb, phb = (sb(n, [LAT, 1], where=ph) for n in ("thb", "phb"))
            gb = sb("gb", [P, 2, LAT], where=ph)
            gam, bet = (sb(n, [LAT, H], where=ph) for n in ("gam", "bet"))
            ow, ob = sb("ow", [LAT, P], where=ph), sb("ob", [P, 1], where=ph)
            mean64 = sb("mean64", [LAT, LAT], where=ph)
            g1w = sb("g1w", [P, HC, E1], where=ph)
            sgu = sb("sgu", [P, HC, 2 * IS], where=ph)
            sdn = sb("sdn", [P, 3, H], where=ph)
            iota_c = sb("iota_c", [P, CAP1], BF16, where=ph)
            xn = [sb(f"xn{p}", [P, H], where=ph) for p in range(W1)]
            th = [sb(f"th{p}", [LAT, 2 * H], where=ph) for p in range(W1)]
            gx = [sb(f"gx{p}", [P, 2, LAT], where=ph) for p in range(W1)]
            pr = [sb(f"pr{p}", [P, 2, H], where=ph) for p in range(W1)]
            prT = [sb(f"prT{p}", [P, 2, H], where=ph) for p in range(W1)]
            hh = [sb(f"hh{p}", [LAT, H], where=ph) for p in range(W1)]
            row = [sb(f"row{p}", [P, ROW], where=ph) for p in range(W1)]
            xT = [sb(f"xT{p}", [P, HC, P], where=ph) for p in range(W1)]
            sg = [sb(f"sg{p}", [P, 3, P], where=ph) for p in range(W1)]
            st = sb("st", [P, W1, 6], where=ph)
            mv = sb("mv", [P, W1, 2], where=ph)
            mvv = sb("mvv", [P, W1], where=ph)
            rstd = sb("rstd", [P, W1], where=ph)
            st2 = sb("st2", [LAT, W1, 2], where=ph)
            nmax = sb("nmax", [P, W1, 2], where=ph)
            psm = sb("psm", [P, W1, 2], where=ph)
            rin = sb("rin", [P, W1, 2], where=ph)
            t8 = sb("t8", [P, W1, 8], where=ph)
            i8 = sb("i8", [P, W1, 8], U32, where=ph)
            i8f = sb("i8f", [P, W1, 8], where=ph)
            ex = sb("ex", [P, W1, E1], where=ph)
            eq = sb("eq", [P, K1, E1], where=ph)
            mf = sb("mf", [P, E1], where=ph)
            mb = sb("mb", [P, W1, E1], BF16, where=ph)
            before = sb("before", [P, W1 + 1, E1], BF16, where=ph)
            cumc = sb("cumc", [P, E1], BF16, where=ph)

            names = ["x_in", "xn_ready", "pt_ready", "gxp_ready", "pt_sb", "gx_sb", "sc_ready", "nm_ready",
                     "p_ready", "pn_ready", "ptr_ready", "prT_sb", "tx_ready", "st2_ready", "mu_ready",
                     "hn_ready", "h_ready", "w_ready", "xn2_ready", "xt_ready", "xT_sb", "lg_ready", "gu_ready",
                     "lnm_ready", "e_ready", "mb_ready", "cum_ready", "G_ready", "ix_ready", "sg_ready",
                     "hs_ready", "dn_ready", "banks_free", "row_ready"]
            s = {n: sem(n) for n in names}
            row_out = [sem(f"row_out{p}") for p in range(W1)]
            bank_a = [pb[2 * p] for p in range(W1)]
            bank_b = [pb[2 * p + 1] for p in range(W1)]
            NIT = B // W1

            with nc.Block() as block:
                @block.sync
                def _(sp):
                    for dst, src in ((idn, ident), (upr, upper), (thw, theta_w), (phw, phi_w), (gw, g_w), (thb, theta_b),
                                     (phb, phi_b), (gam, gamma), (bet, beta), (ow, out_w), (ob, out_b)):
                        sp.dma_start(dst[:, :], src).then_inc(consts_in, 16)
                    sp.dma_start(gb[:, :, :], g_b.rearrange("(a c l) -> a c l", a=1, c=1).to_broadcast([P, 2, LAT])).then_inc(consts_in, 16)
                    sp.dma_start(tanh_g[:, :], gates.rearrange("(a n) -> a n", a=1).to_broadcast([P, 4])).then_inc(consts_in, 16)
                    sp.dma_start(g1w[:, :, :], gate1_w).then_inc(consts_in, 16)
                    sp.dma_start(sgu[:, :, :], sw_gu).then_inc(consts_in, 16)
                    sp.dma_start(sdn[:, 0:2, :], sw_d[0:2 * P, :].rearrange("(c p) n -> p c n", p=P)).then_inc(consts_in, 16)
                    sp.dma_start(sdn[0:IS - 2 * P, 2, :], sw_d[2 * P:IS, :]).then_inc(consts_in, 16)
                    def load_batches(it):
                        sp.dma_start(X[:, bass.ds(it * W1, W1), :], x[:, bass.ds(it * W1, W1), :]).then_inc(s["x_in"], 16)
                        sp.dma_start(CX[:, bass.ds(it * W1, W1), :], ctx[:, bass.ds(it * W1, W1), :]).then_inc(s["x_in"], 16)

                    def store_rows(it):
                        for p in range(W1):
                            sp.wait_ge(s["row_ready"], it * W1 + p + 1)
                            sp.dma_start(rows1[bass.ds((it * W1 + p) * P, P), :], row[p][:, :]).then_inc(row_out[p], 16)

                    load_batches(0)
                    for p in range(W1):
                        sp.sem_inc(row_out[p], 16)
                    for r in range(R2):
                        sp.dma_start(wgu_sb[r][:, :, :, :], w_gu[:, 4 * r:4 * r + 4, :, :]).then_inc(experts_in[r], 16)
                        sp.dma_start(wd_sb[r][:, :, :, :], w_d[:, 4 * r:4 * r + 4, :, :]).then_inc(experts_in[r], 16)
                    with sp.Fori(0, NIT - 1) as it:
                        sp.wait_ge(s["x_in"], it * 32 + 32)
                        load_batches(it + 1)
                        store_rows(it)
                    sp.wait_ge(zero_made, 2)
                    sp.dma_start(rows1[TOK:TOK + 1, :], zrow[0:1, :]).then_inc(zero_out, 16)
                    sp.dma_start(youts[SLOTS2:SLOTS2 + 1, :], zrow[0:1, 0:H]).then_inc(zero_out, 16)
                    for c in range(SLOTS2 // P):
                        sp.dma_start(rows2[c * P:(c + 1) * P, :], zrow[:, 0:H]).then_inc(zero_out, 16)
                    store_rows(NIT - 1)
                    sp.wait_ge(zero_out, 16 * (2 + SLOTS2 // P))
                    for p in range(W1):
                        sp.wait_ge(row_out[p], 16 * (NIT + 1))

                @block.gpsimd
                def _(pool):
                    gp, did = nc.gpsimd, Count()
                    gp.memset(zrow[:, :], 0.0).then_inc(zero_made, 1)
                    gp.iota(iota_e[:, :], [[1, E1]], base=0, channel_multiplier=0, allow_small_or_imprecise_dtypes=True).then_inc(pool_done, did.one())
                    pool.wait_ge(pool_done, did.n)
                    gp.iota(iota_c[:, :], [[1, CAP1]], base=0, channel_multiplier=0, allow_small_or_imprecise_dtypes=True).then_inc(pool_done, did.one())
                    pool.wait_ge(pool_done, did.n)
                    gp.memset(mean64[:, :], 1.0 / LAT).then_inc(pool_done, did.one())
                    pool.wait_ge(pool_done, did.n)
                    gp.memset(ones_b[:, :], 1.0).then_inc(pool_done, did.one())
                    pool.wait_ge(pool_done, did.n)
                    pool.wait_ge(pool_done, did.n)
                    pool.sem_inc(zero_made, 1)
                    pool.wait_ge(consts_in, 16 * 17)
                    pool.wait_ge(pool_done, did.n)
                    pool.sem_inc(pool_done, -did.restart())
                    with pool.Fori(0, NIT) as it:
                        for p in range(W1):
                            pool.wait_ge(s["hn_ready"], it * W1 + p + 1)
                            gp.tensor_tensor(hh[p][:, :], hh[p][:, :], gam[:, :], ALU.mult).then_inc(pool_done, did.one())
                            pool.wait_ge(pool_done, did.n)
                            gp.tensor_tensor(hh[p][:, :], hh[p][:, :], bet[:, :], ALU.add).then_inc(pool_done, did.one())
                            pool.wait_ge(pool_done, did.n)
                            gp.tensor_scalar(hh[p][:, :], hh[p][:, :], 0.0, None, ALU.max).then_inc(pool_done, did.one())
                            pool.wait_ge(pool_done, did.n)
                            pool.sem_inc(s["h_ready"], 1)
                        pool.wait_ge(pool_done, did.n)
                        pool.sem_inc(pool_done, -did.restart())

                @block.scalar
                def _(act):
                    sc = nc.scalar
                    act.wait_ge(consts_in, 16 * 17)
                    sc.activation(tanh_g[:, :], tanh_g[:, :], ACT.Tanh).then_inc(tanh_made, 1)
                    with act.Fori(0, NIT) as it:
                        for p in range(W1):
                            act.wait_ge(s["pt_ready"], it * W1 + p + 1)
                            sc.activation(th[p][:, 0:H], bank_a[p][0:LAT, 0:H], ACT.Identity, bias=phb[:, 0:1])
                            sc.activation(th[p][:, H:2 * H], bank_a[p][0:LAT, H:2 * H], ACT.Identity, bias=thb[:, 0:1]).then_inc(s["pt_sb"], 1)
                        for p in range(W1):
                            act.wait_ge(s["nm_ready"], it * W1 + p + 1)
                            for c in range(2):
                                last = sc.activation(pr[p][:, c, :], bank_a[p][:, c * H:(c + 1) * H], ACT.Exp,
                                                     bias=nmax[:, p, c:c + 1], accum_out=psm[:, p, c:c + 1])
                            last.then_inc(s["p_ready"], 1)
                        for p in range(W1):
                            act.wait_ge(s["ptr_ready"], it * W1 + p + 1)
                            sc.activation(prT[p][:, :, :], bank_b[p][:, :], ACT.Copy).then_inc(s["prT_sb"], 1)
                        for p in range(W1):
                            act.wait_ge(s["xt_ready"], it * W1 + p + 1)
                            sc.activation(xT[p][:, :, :], bank_a[p][:, 0:H], ACT.Copy).then_inc(s["xT_sb"], 1)
                        for p in range(W1):
                            act.wait_ge(s["lnm_ready"], it * W1 + p + 1)
                            sc.activation(ex[:, p, :], bank_b[p][:, 448:512], ACT.Exp, bias=nmax[:, p, 0:1],
                                          accum_out=psm[:, p, 0:1]).then_inc(s["e_ready"], 1)
                        for p in range(W1):
                            act.wait_ge(s["gu_ready"], it * W1 + p + 1)
                            sc.activation(sg[p][:, 0:2, :], bank_a[p][:, 0:256], ACT.Silu)
                            sc.activation(sg[p][0:96, 2, :], bank_a[p][0:96, 256:384], ACT.Silu).then_inc(s["sg_ready"], 1)

                @block.vector
                def _(dve):
                    v, did = nc.vector, Count()

                    def norm_stats(src, p):
                        v.bn_stats(st[:, p, :], src).then_inc(dve_done, did.one())
                        dve.wait_ge(dve_done, did.n)
                        v.bn_aggr(mv[:, p, :], st[:, p, :]).then_inc(dve_done, did.one())
                        dve.wait_ge(dve_done, did.n)
                        v.tensor_scalar(mvv[:, p:p + 1], mv[:, p, 1:2], EPS, None, ALU.add).then_inc(dve_done, did.one())

                    v.memset(idx1f[:, :], 0.0).then_inc(dve_done, did.one())
                    dve.wait_ge(dve_done, did.n)
                    v.memset(before[:, 0, :], 0.0).then_inc(dve_done, did.one())
                    dve.wait_ge(dve_done, did.n)
                    for _ in range(W1):
                        dve.sem_inc(s["banks_free"], 1)
                    dve.wait_ge(zero_made, 2)
                    dve.wait_ge(tanh_made, 1)
                    dve.wait_ge(consts_in, 16 * 17)
                    dve.wait_ge(dve_done, did.n)
                    dve.sem_inc(dve_done, -did.restart())
                    with dve.Fori(0, NIT) as it:
                        dve.wait_ge(s["x_in"], it * 32 + 32)
                        for p in range(W1):
                            norm_stats(X[:, bass.ds(it * W1 + p, 1), :], p)
                        dve.wait_ge(dve_done, did.n)
                        rsqrt(nc, dve, dve_done, did, rstd[:, :], mvv[:, :], rs_h[:, :], rs_t[:, :])
                        for p in range(W1):
                            v.tensor_scalar(xn[p][:, :], X[:, bass.ds(it * W1 + p, 1), :], mv[:, p, 0:1], rstd[:, p:p + 1],
                                                    ALU.subtract, ALU.mult).then_inc(dve_done, did.one())
                            dve.wait_ge(dve_done, did.n)
                            dve.sem_inc(s["xn_ready"], 1)
                        for p in range(W1):
                            dve.wait_ge(s["gxp_ready"], it * W1 + p + 1)
                            v.tensor_tensor(gx[p][:, :, :], bank_b[p][:, 0:2 * LAT].rearrange("p (c l) -> p c l", c=2), gb[:, :, :], ALU.add).then_inc(dve_done, did.one())
                            dve.wait_ge(dve_done, did.n)
                            dve.sem_inc(s["gx_sb"], 1)
                        for p in range(W1):
                            dve.wait_ge(s["sc_ready"], it * W1 + p + 1)
                            v.tensor_reduce(nmax[:, p, :], bank_a[p][:, :].rearrange("p (c t) -> p c t", c=2), axis=AX.X, op=ALU.max, negate=True).then_inc(dve_done, did.one())
                            dve.wait_ge(dve_done, did.n)
                            dve.sem_inc(s["nm_ready"], 1)
                        for p in range(W1):
                            dve.wait_ge(s["p_ready"], it * W1 + p + 1)
                            v.reciprocal(rin[:, p, :], psm[:, p, :]).then_inc(dve_done, did.one())
                            dve.wait_ge(dve_done, did.n)
                            for c in range(2):
                                v.tensor_scalar(pr[p][:, c, :], pr[p][:, c, :], rin[:, p, c:c + 1], None, ALU.mult).then_inc(dve_done, did.one())
                            dve.wait_ge(dve_done, did.n)
                            dve.sem_inc(s["pn_ready"], 1)
                        for p in range(W1):
                            dve.wait_ge(s["tx_ready"], it * W1 + p + 1)
                            v.bn_stats(st[0:LAT, p, :], bank_a[p][0:LAT, 0:H]).then_inc(dve_done, did.one())
                            dve.wait_ge(dve_done, did.n)
                            v.bn_aggr(st2[:, p, :], st[0:LAT, p, :]).then_inc(dve_done, did.one())
                            dve.wait_ge(dve_done, did.n)
                            v.scalar_tensor_tensor(st2[:, p, 1:2], st2[:, p, 0:1], st2[:, p, 0:1], st2[:, p, 1:2], ALU.mult, ALU.add).then_inc(dve_done, did.one())
                            dve.wait_ge(dve_done, did.n)
                            dve.sem_inc(s["st2_ready"], 1)
                        for p in range(W1):
                            dve.wait_ge(s["mu_ready"], it * W1 + p + 1)
                            v.tensor_copy(mv[0:LAT, p, :], bank_a[p][0:LAT, H:H + 2]).then_inc(dve_done, did.one())
                            dve.wait_ge(dve_done, did.n)
                            v.scalar_tensor_tensor(mvv[0:LAT, p:p + 1], mv[0:LAT, p, 0:1], mv[0:LAT, p, 0:1], mv[0:LAT, p, 1:2], ALU.mult, ALU.subtract).then_inc(dve_done, did.one())
                            dve.wait_ge(dve_done, did.n)
                            v.tensor_scalar(mvv[0:LAT, p:p + 1], mvv[0:LAT, p:p + 1], -1.0, EPS, ALU.mult, ALU.add).then_inc(dve_done, did.one())
                        dve.wait_ge(dve_done, did.n)
                        rsqrt(nc, dve, dve_done, did, rstd[0:LAT, :], mvv[0:LAT, :], rs_h[0:LAT, :], rs_t[0:LAT, :])
                        for p in range(W1):
                            v.tensor_scalar(hh[p][:, :], bank_a[p][0:LAT, 0:H], mv[0:LAT, p, 0:1], rstd[0:LAT, p:p + 1], ALU.subtract, ALU.mult).then_inc(dve_done, did.one())
                            dve.wait_ge(dve_done, did.n)
                            dve.sem_inc(s["hn_ready"], 1)
                        for p in range(W1):
                            dve.wait_ge(s["w_ready"], it * W1 + p + 1)
                            xb = X[:, bass.ds(it * W1 + p, 1), :]
                            v.scalar_tensor_tensor(xn[p][:, :], bank_b[p][:, 0:H], ob[:, 0:1], CX[:, bass.ds(it * W1 + p, 1), :].rearrange("p a h -> p (a h)"), ALU.add, ALU.add).then_inc(dve_done, did.one())
                            dve.wait_ge(dve_done, did.n)
                            v.scalar_tensor_tensor(xb.rearrange("p a h -> p (a h)"), xn[p][:, :], tanh_g[:, 0:1], xb.rearrange("p a h -> p (a h)"), ALU.mult, ALU.add).then_inc(dve_done, did.one())
                            dve.wait_ge(dve_done, did.n)
                            norm_stats(xb, p)
                        dve.wait_ge(dve_done, did.n)
                        rsqrt(nc, dve, dve_done, did, rstd[:, :], mvv[:, :], rs_h[:, :], rs_t[:, :])
                        for p in range(W1):
                            dve.wait_ge(row_out[p], it * 16 + 16)
                            v.tensor_scalar(row[p][:, 0:H], X[:, bass.ds(it * W1 + p, 1), :], mv[:, p, 0:1], rstd[:, p:p + 1],
                                                    ALU.subtract, ALU.mult).then_inc(dve_done, did.one())
                            dve.wait_ge(dve_done, did.n)
                            dve.sem_inc(s["xn2_ready"], 1)
                        for p in range(W1):
                            dve.wait_ge(s["lg_ready"], it * W1 + p + 1)
                            v.tensor_reduce(nmax[:, p, 0:1], bank_b[p][:, 448:512], axis=AX.X, op=ALU.max, negate=True).then_inc(dve_done, did.one())
                            dve.wait_ge(dve_done, did.n)
                            dve.sem_inc(s["lnm_ready"], 1)
                        for p in range(W1):
                            dve.wait_ge(s["e_ready"], it * W1 + p + 1)
                            v.reciprocal(rin[:, p, 0:1], psm[:, p, 0:1]).then_inc(dve_done, did.one())
                            dve.wait_ge(dve_done, did.n)
                            v.tensor_scalar(ex[:, p, :], ex[:, p, :], rin[:, p, 0:1], None, ALU.mult).then_inc(dve_done, did.one())
                            dve.wait_ge(dve_done, did.n)
                            v.max(t8[:, p, :], ex[:, p, :]).then_inc(dve_done, did.one())
                            dve.wait_ge(dve_done, did.n)
                            v.max_index(i8[:, p, :], t8[:, p, :], ex[:, p, :]).then_inc(dve_done, did.one())
                            dve.wait_ge(dve_done, did.n)
                            v.tensor_copy(i8f[:, p, :], i8[:, p, :]).then_inc(dve_done, did.one())
                            dve.wait_ge(dve_done, did.n)
                            v.tensor_tensor(eq[:, :, :], iota_e[:, :].unsqueeze(1).to_broadcast([P, K1, E1]),
                                                    i8f[:, p, 0:K1].unsqueeze(2).to_broadcast([P, K1, E1]), ALU.is_equal).then_inc(dve_done, did.one())
                            dve.wait_ge(dve_done, did.n)
                            v.tensor_reduce(mf[:, :], eq[:, :, :].rearrange("p k e -> p e k"), axis=AX.X, op=ALU.add).then_inc(dve_done, did.one())
                            dve.wait_ge(dve_done, did.n)
                            v.tensor_tensor(row[p][:, H:ROW], ex[:, p, :], mf[:, :], ALU.mult).then_inc(dve_done, did.one())
                            v.tensor_copy(mb[:, p, :], mf[:, :]).then_inc(dve_done, did.one())
                            dve.wait_ge(dve_done, did.n)
                            v.tensor_tensor(before[:, p + 1, :], before[:, p, :], mb[:, p, :], ALU.add).then_inc(dve_done, did.one())
                            dve.wait_ge(dve_done, did.n)
                            dve.sem_inc(s["mb_ready"], 1)
                            dve.sem_inc(s["row_ready"], 1)
                        for p in range(W1):
                            dve.wait_ge(s["sg_ready"], it * W1 + p + 1)
                            v.tensor_tensor(sg[p][:, 0:2, :], sg[p][:, 0:2, :], bank_b[p][:, 0:256].rearrange("p (c t) -> p c t", c=2), ALU.mult).then_inc(dve_done, did.one())
                            v.tensor_tensor(sg[p][0:96, 2, :], sg[p][0:96, 2, :], bank_b[p][0:96, 256:384], ALU.mult).then_inc(dve_done, did.one())
                            dve.wait_ge(dve_done, did.n)
                            dve.sem_inc(s["hs_ready"], 1)
                        for p in range(W1):
                            dve.wait_ge(s["cum_ready"], it * W1 + p + 1)
                            v.tensor_scalar(cumc[:, :], bank_b[p][:, 448:512], 2.0 * CAP1, None, ALU.min).then_inc(dve_done, did.one())
                            dve.wait_ge(dve_done, did.n)
                            if p >= 2:
                                dve.wait_ge(s["ix_ready"], it * W1 + p - 1)
                            v.tensor_tensor(G[p % 2][:, :, :], cumc[:, :].unsqueeze(2).to_broadcast([P, E1, CAP1]),
                                                    iota_c[:, :].unsqueeze(1).to_broadcast([P, E1, CAP1]), ALU.is_le).then_inc(dve_done, did.one())
                            dve.wait_ge(dve_done, did.n)
                            dve.sem_inc(s["G_ready"], 1)
                        for p in range(W1):
                            dve.wait_ge(s["ix_ready"], it * W1 + p + 1)
                            v.tensor_tensor(idx1f[:, :], idx1f[:, :], bank_b[p][:, 384:400], ALU.add).then_inc(dve_done, did.one())
                            dve.wait_ge(dve_done, did.n)
                        v.tensor_copy(before[:, 0, :], before[:, W1, :]).then_inc(dve_done, did.one())
                        dve.wait_ge(dve_done, did.n)
                        for p in range(W1):
                            dve.wait_ge(s["dn_ready"], it * W1 + p + 1)
                            xb = X[:, bass.ds(it * W1 + p, 1), :].rearrange("p a h -> p (a h)")
                            v.scalar_tensor_tensor(xb, bank_a[p][:, 0:H], tanh_g[:, 2:3], xb, ALU.mult, ALU.add).then_inc(dve_done, did.one())
                            dve.wait_ge(dve_done, did.n)
                            dve.sem_inc(s["banks_free"], 1)
                        dve.wait_ge(dve_done, did.n)
                        dve.sem_inc(dve_done, -did.restart())
                    v.tensor_copy(idx1[:, :], idx1f[:, :]).then_inc(dve_done, did.one())
                    dve.wait_ge(dve_done, did.n)
                    dve.wait_ge(dve_done, did.n)
                    dve.sem_inc(dve_done, -did.restart())

                @block.tensor
                def _(pe):
                    t = nc.tensor
                    pe.wait_ge(consts_in, 16 * 17)
                    pe.wait_ge(zero_made, 2)
                    with pe.Fori(0, NIT) as it:
                        for p in range(W1):
                            pe.wait_ge(s["banks_free"], it * W1 + p + 1)
                            pe.wait_ge(s["xn_ready"], it * W1 + p + 1)
                            t.matmul(bank_a[p][0:LAT, 0:H], phw[:, :], xn[p][:, :], start=True, stop=True)
                            t.matmul(bank_a[p][0:LAT, H:2 * H], thw[:, :], CX[:, bass.ds(it * W1 + p, 1), :].rearrange("p a h -> p (a h)"),
                                     start=True, stop=True).then_inc(s["pt_ready"], 1)
                            for c in range(2):
                                last = t.matmul(bank_b[p][:, c * LAT:(c + 1) * LAT], xn[p][:, c * P:(c + 1) * P], gw[:, :], start=True, stop=True)
                            last.then_inc(s["gxp_ready"], 1)
                        for p in range(W1):
                            pe.wait_ge(s["pt_sb"], it * W1 + p + 1)
                            for c in range(2):
                                last = t.matmul(bank_a[p][:, c * H:(c + 1) * H], th[p][:, H + c * P:H + (c + 1) * P], th[p][:, 0:H], start=True, stop=True)
                            last.then_inc(s["sc_ready"], 1)
                        for p in range(W1):
                            pe.wait_ge(s["gx_sb"], it * W1 + p + 1)
                            pe.wait_ge(s["pn_ready"], it * W1 + p + 1)
                            for c in range(2):
                                for tc in range(2):
                                    last = t.transpose(bank_b[p][:, c * H + tc * P:c * H + (tc + 1) * P], pr[p][:, tc, c * P:(c + 1) * P], idn[:, :])
                            last.then_inc(s["ptr_ready"], 1)
                        for p in range(W1):
                            pe.wait_ge(s["prT_sb"], it * W1 + p + 1)
                            for c in range(2):
                                last = t.matmul(bank_a[p][0:LAT, 0:H], gx[p][:, c, :], prT[p][:, c, :], start=c == 0, stop=c == 1)
                            last.then_inc(s["tx_ready"], 1)
                        for p in range(W1):
                            pe.wait_ge(s["st2_ready"], it * W1 + p + 1)
                            pe.sem_inc(pe_passed, 1)
                            t.matmul(bank_a[p][0:LAT, H:H + 2], mean64[:, :], st2[:, p, :], start=True, stop=True).then_inc(s["mu_ready"], 1)
                        for p in range(W1):
                            pe.wait_ge(s["h_ready"], it * W1 + p + 1)
                            t.matmul(bank_b[p][:, 0:H], ow[:, :], hh[p][:, :], start=True, stop=True).then_inc(s["w_ready"], 1)
                        for p in range(W1):
                            pe.wait_ge(s["xn2_ready"], it * W1 + p + 1)
                            for c in range(HC):
                                last = t.transpose(bank_a[p][:, c * P:(c + 1) * P], row[p][:, c * P:(c + 1) * P], idn[:, :])
                            last.then_inc(s["xt_ready"], 1)
                        for p in range(W1):
                            pe.wait_ge(s["xT_sb"], it * W1 + p + 1)
                            for c in range(HC):
                                last = t.matmul(bank_b[p][:, 448:512], xT[p][:, c, :], g1w[:, c, :], start=c == 0, stop=c == HC - 1)
                            last.then_inc(s["lg_ready"], 1)
                        for k, banks in enumerate((bank_a, bank_b)):
                            for p in range(W1):
                                if k == 1:
                                    pe.wait_ge(s["e_ready"], it * W1 + p + 1)
                                for j, (o, m) in enumerate(ISC):
                                    for c in range(HC):
                                        last = t.matmul(banks[p][0:m, j * P:(j + 1) * P], sgu[:, c, k * IS + o:k * IS + o + m], xT[p][:, c, :],
                                                        start=c == 0, stop=c == HC - 1)
                                if k == 1:
                                    last.then_inc(s["gu_ready"], 1)
                        for p in range(W1):
                            pe.wait_ge(s["hs_ready"], it * W1 + p + 1)
                            pe.wait_ge(s["mb_ready"], it * W1 + p + 1)
                            t.matmul(bank_b[p][:, 448:512], upr[:, :], mb[:, p, :], start=True, stop=False)
                            t.matmul(bank_b[p][:, 448:512], ones_b[:, :], before[:, p, :], start=False, stop=True).then_inc(s["cum_ready"], 1)
                            for j, (o, m) in enumerate(ISC):
                                last = t.matmul(bank_a[p][:, 0:H], sg[p][0:m, j, :], sdn[0:m, j, :], start=j == 0, stop=j == 2)
                            last.then_inc(s["dn_ready"], 1)
                        for p in range(W1):
                            pe.wait_ge(s["G_ready"], it * W1 + p + 1)
                            gf = G[p % 2][:, :, :].rearrange("p e c -> p (e c)")
                            for j in range(SLOTS1 // P):
                                last = t.matmul(bank_b[p][:, 384 + j:385 + j], gf[:, j * P:(j + 1) * P], ones_b[:, 0:1], start=True, stop=True)
                            last.then_inc(s["ix_ready"], 1)

        N2 = SLOTS1 // P
        with ExitStack() as ph:
            qrt = sb("qrt", [P, 4], where=ph)
            idxc = [sb(f"idxc{q}", [P, 1], U32, where=ph) for q in range(2)]
            xs = [sb(f"xs{q}", [P, ROW], where=ph) for q in range(2)]
            xsT = [sb(f"xsT{q}", [P, HC, P], where=ph) for q in range(2)]
            hm = [sb(f"hm{q}", [P, I1], where=ph) for q in range(2)]
            hT = [sb(f"hT{q}", [I1H, 2, P], where=ph) for q in range(2)]
            w4 = sb("w4", [P, 2, 4], where=ph)
            ws = sb("ws", [P, 2], where=ph)
            yy = [sb(f"yy{q}", [P, H], where=ph) for q in range(2)]
            slots_in = [sem(f"slots_in{q}") for q in range(2)]
            names = ["slots_free", "st_ready", "xsT_sb", "ug_ready", "silu_ready", "hm_ready", "ht_ready", "hT_sb", "y_ready", "y_taken"]
            s = {n: sem("e_" + n) for n in names}
            with nc.Block() as block:
                @block.sync
                def _(sp):
                    sp.dma_start(qrt[:, :], quarter).then_inc(consts_in, 16)
                    with sp.Fori(1, N2 // R2) as it:
                        for r in range(R2):
                            sp.wait_ge(experts_free, (it - 1) * R2 + r + 1)
                            sp.dma_start(wgu_sb[r][:, :, :, :], w_gu[:, bass.ds((it * R2 + r) * 4, 4), :, :]).then_inc(experts_in[r], 16)
                            sp.dma_start(wd_sb[r][:, :, :, :], w_d[:, bass.ds((it * R2 + r) * 4, 4), :, :]).then_inc(experts_in[r], 16)

                @block.gpsimd
                def _(pool):
                    gp, did = nc.gpsimd, Count()
                    for _ in range(2):
                        pool.sem_inc(s["slots_free"], 1)
                    with pool.Fori(0, N2 // R2) as it:
                        for r in range(R2):
                            q = r % 2
                            pool.wait_ge(s["slots_free"], it * R2 + r + 1)
                            gp.tensor_copy(idxc[q][:, :], idx1[:, bass.ds(it * R2 + r, 1)]).then_inc(pool_done, did.one())
                            pool.wait_ge(pool_done, did.n)
                            pool.indirect_dma_start(xs[q][:, :], None, rows1, bass.IndirectOffsetOnAxis(ap=idxc[q][:, :], axis=0),
                                                    bounds_check=TOK, oob_is_err=False).then_inc(slots_in[q], 16)
                        pool.wait_ge(pool_done, did.n)
                        pool.sem_inc(pool_done, -did.restart())

                @block.scalar
                def _(act):
                    sc = nc.scalar
                    with act.Fori(0, N2 // R2) as it:
                        for r in range(R2):
                            q, n = r % 2, it * R2 + r + 1
                            act.wait_ge(s["st_ready"], n)
                            sc.activation(xsT[q][:, :, :], pb[q][:, 0:H], ACT.Copy).then_inc(s["xsT_sb"], 1)
                            act.wait_ge(s["ug_ready"], n)
                            sc.activation(hm[q][:, :], pb[2 + q][:, 0:I1], ACT.Silu).then_inc(s["silu_ready"], 1)
                            act.wait_ge(s["ht_ready"], n)
                            sc.activation(hT[q][:, :, :], pb[4 + q][0:I1H, 0:2 * P], ACT.Copy).then_inc(s["hT_sb"], 1)

                @block.vector
                def _(dve):
                    v, did = nc.vector, Count()
                    dve.wait_ge(consts_in, 16 * 18)
                    with dve.Fori(0, N2 // R2) as it:
                        for r in range(R2):
                            q, n = r % 2, it * R2 + r + 1
                            dve.wait_ge(slots_in[q], it * 32 + (r // 2 + 1) * 16)
                            v.tensor_tensor(w4[:, q, :], xs[q][:, bass.ds(H + (it * R2 + r) * 4, 4)], qrt[:, :], ALU.mult).then_inc(dve_done, did.one())
                            dve.wait_ge(dve_done, did.n)
                            v.tensor_reduce(ws[:, q:q + 1], w4[:, q, :], axis=AX.X, op=ALU.add).then_inc(dve_done, did.one())
                            dve.wait_ge(dve_done, did.n)
                            dve.wait_ge(s["xsT_sb"], n)
                            dve.sem_inc(s["slots_free"], 1)
                            dve.wait_ge(s["silu_ready"], n)
                            v.tensor_tensor(hm[q][:, :], hm[q][:, :], pb[2 + q][:, I1:2 * I1], ALU.mult).then_inc(dve_done, did.one())
                            dve.wait_ge(dve_done, did.n)
                            dve.sem_inc(s["hm_ready"], 1)
                            dve.wait_ge(s["y_ready"], n)
                            v.tensor_scalar(yy[q][:, :], pb[6 + q][:, 0:H], ws[:, q:q + 1], None, ALU.mult).then_inc(dve_done, did.one())
                            dve.wait_ge(dve_done, did.n)
                            for k in range(3):
                                part = parts[:, bass.ds(it * R2 + r, 1), k, :].rearrange("p a h -> p (a h)")
                                v.tensor_copy(part, yy[q][:, :]).then_inc(dve_done, did.one())
                                dve.wait_ge(dve_done, did.n)
                                if k < 2:
                                    v.tensor_tensor(yy[q][:, :], yy[q][:, :], part, ALU.subtract).then_inc(dve_done, did.one())
                                    dve.wait_ge(dve_done, did.n)
                            dve.sem_inc(s["y_taken"], 1)
                        dve.wait_ge(dve_done, did.n)
                        dve.sem_inc(dve_done, -did.restart())

                @block.tensor
                def _(pe):
                    t = nc.tensor
                    with pe.Fori(0, N2 // R2) as it:
                        for r in range(R2):
                            q, n = r % 2, it * R2 + r + 1
                            pe.wait_ge(slots_in[q], it * 32 + (r // 2 + 1) * 16)
                            for c in range(HC):
                                last = t.transpose(pb[q][:, c * P:(c + 1) * P], xs[q][:, c * P:(c + 1) * P], idn[:, :])
                            last.then_inc(s["st_ready"], 1)
                            pe.wait_ge(experts_in[r], it * 32 + 32)
                            pe.wait_ge(s["xsT_sb"], n)
                            for c in range(HC):
                                for e in range(4):
                                    last = t.matmul(pb[2 + q][32 * e:32 * e + 32, 0:2 * I1], xsT[q][:, c, 32 * e:32 * e + 32],
                                                    wgu_sb[r][:, e, c, :], start=c == 0, stop=c == HC - 1)
                            last.then_inc(s["ug_ready"], 1)
                            pe.wait_ge(s["hm_ready"], n)
                            for c in range(2):
                                last = t.transpose(pb[4 + q][0:I1H, c * P:(c + 1) * P], hm[q][:, c * I1H:(c + 1) * I1H], idn[:, :])
                            last.then_inc(s["ht_ready"], 1)
                            pe.wait_ge(s["hT_sb"], n)
                            for c in range(2):
                                for e in range(4):
                                    last = t.matmul(pb[6 + q][32 * e:32 * e + 32, 0:H], hT[q][:, c, 32 * e:32 * e + 32],
                                                    wd_sb[r][:, e, c, :], start=c == 0, stop=c == 1)
                            last.then_inc(s["y_ready"], 1)
                            pe.wait_ge(s["y_taken"], n)
                            pe.sem_inc(experts_free, 1)
        phase12.close()

        with ExitStack() as ph:
            wq = sb("wq", [P, HC, 3 * H], where=ph)
            wo_sb = sb("wo_sb", [P, HC, H], where=ph)
            g2w = sb("g2w", [P, HC, E2], where=ph)
            cosv, sinv = (sb(n, [P, HD], where=ph) for n in ("cosv", "sinv"))
            grp = sb("grp", [P, 4], where=ph)
            hg = sb("hg", [P, NH], where=ph)
            iota_t = sb("iota_t", [P, P], where=ph)
            onehot = sb("onehot", [P, N2, P], BF16, where=ph)
            cT = [sb(f"cT{p}", [P, HC, P], where=ph) for p in range(2)]
            mk = [sb(f"mk{p}", [P, P], where=ph) for p in range(2)]
            xn = [sb(f"xc{p}", [P, H], where=ph) for p in range(2)]
            xT = sb("xcT", [P, HC, P], where=ph)
            qk = sb("qk", [P, 2, NH, HD], where=ph)
            rot = sb("rot", [P, 2, NH, HD], where=ph)
            ak = sb("ak", [P, H], where=ph)
            kT = sb("kT", [P, 2, HC, P], where=ph)
            vv = [[sb(f"vv{p}{a}", [P, NH, 32], where=ph) for a in range(2)] for p in range(2)]
            qT = [sb(f"qT{p}", [P, HC, P], where=ph) for p in range(2)]
            kd = [[sb(f"kd{p}{a}", [P, HC, 4, P], where=ph) for a in range(2)] for p in range(2)]
            pr = [sb(f"pc{i}", [P, 4, P], where=ph) for i in range(3)] + [sb("pc3", [P, 4, P], where=ph)]
            prT = [sb(f"pcT{i}", [P, 4, P], where=ph) for i in range(2)]
            ots = [sb(f"ots{i}", [P, 4, P], where=ph) for i in range(2)]
            nm = sb("nm", [P, 4, 4], where=ph)
            oa = sb("oa", [P, 2, NH, HD + 1], where=ph)
            rr = sb("rr", [P, 2, NH], where=ph)
            at = sb("at", [P, NH, HD], where=ph)
            at2 = sb("at2", [P, NH, HD], where=ph)
            atT = sb("atT", [P, HC, P], where=ph)
            xn4 = [sb(f"xn4{p}", [P, H], where=ph) for p in range(2)]
            x4T = sb("x4T", [P, HC, P], where=ph)
            st = sb("stc", [P, 6], where=ph)
            mv = sb("mvc", [P, 2], where=ph)
            mvv, rstd = sb("mvvc", [P, 1], where=ph), sb("rstdc", [P, 1], where=ph)
            t8 = sb("t8c", [P, 8], where=ph)
            i8 = sb("i8c", [P, 8], U32, where=ph)
            sm = sb("sm", [P, 16], where=ph)
            e8, m8, c8, pe8 = (sb(n, [P, E2], where=ph) for n in ("e8", "m8", "c8", "pe8"))
            m8b = sb("m8b", [P, E2], BF16, where=ph)
            before2 = sb("before2", [P, E2], BF16, where=ph)
            sl = [sb(f"sl{p}", [P, 1], U32, where=ph) for p in range(2)]
            names = ["one_ready", "comb_ready", "xc_ready", "xcT_ready", "xcT_sb", "qk_ready", "qk_sb", "ka_ready", "ka_sb",
                     "v_ready", "v_sb", "rope_ready", "qkT_ready", "qkT_sb", "aT2_ready", "aT2_sb", "kd_ready", "mask_ready",
                     "at_ready", "aT_ready", "aT_sb", "wo_ready", "x4_ready", "x4T_ready", "x4T_sb", "lg_ready", "ln_ready",
                     "e8_ready", "m_ready", "cum_ready", "cum_taken", "sl_ready", "cin_free", "x4_free", "buffers_made",
                     "sc_ready", "nm_ready", "p_ready", "tr_ready", "evac_main", "evac_ad", "pv_done",
                     "ot_ready", "ot_sb", "ob_ready", "o_taken"]
            s = {n: sem("c_" + n) for n in names}
            ctx_in = [sem(f"ctx_in{p}") for p in range(2)]
            xn4_out = [sem(f"xn4_out{p}") for p in range(2)]
            score = pb[0:4]
            trp, otb, mb_ = pb[4], pb[5:7], pb[7]
            U, NM = 16, 8
            CONSTS3 = 16 * 25

            FIRST, LASTS = [(0, True, False, True)], [(13, True, True, True), (14, True, True, False), (15, False, True, False)]
            LOOP = (1, 13, 2)

            with nc.Block() as block:
                @block.sync
                def _(sp):
                    for dst, src in ((wq, wqkv), (wo_sb, wo), (g2w, gate2_w)):
                        sp.dma_start(dst[:, :, :], src).then_inc(consts_in, 16)
                    for dst, src in ((cosv, cos), (sinv, sin), (grp, group)):
                        sp.dma_start(dst[:, :], src).then_inc(consts_in, 16)
                    sp.dma_start(hg[:, :], hgate.rearrange("(a n) -> a n", a=1).to_broadcast([P, NH])).then_inc(consts_in, 16)
                    for p in range(2):
                        sp.sem_inc(s["cin_free"], 1)
                    with sp.Fori(0, B // 2) as it:
                        for p in range(2):
                            sp.wait_ge(s["cin_free"], it * 2 + p + 1)
                            sp.dma_start(cT[p][:, :, :], ctxT[bass.ds(it * 2 + p, 1), :, :, :].rearrange("a p c t -> p (a c) t")).then_inc(ctx_in[p], 16)
                            sp.dma_start(mk[p][:, :], mask[bass.ds(it * 2 + p, 1), :, :].rearrange("a p k -> p (a k)")).then_inc(ctx_in[p], 16)

                @block.gpsimd
                def _(pool):
                    gp, did = nc.gpsimd, Count()
                    gp.iota(iota_t[:, :], [[1, P]], base=0, channel_multiplier=0, allow_small_or_imprecise_dtypes=True).then_inc(pool_done, did.one())
                    for p in range(2):
                        for a in range(2):
                            gp.memset(vv[p][a][:, :, :], 0.0).then_inc(pool_done, did.one())
                    pool.wait_ge(pool_done, did.n)
                    for p in range(2):
                        for a in range(2):
                            gp.memset(vv[p][a][:, :, HD:HD + 1], 1.0).then_inc(pool_done, did.one())
                        pool.sem_inc(s["x4_free"], 1)
                    pool.wait_ge(pool_done, did.n)
                    pool.sem_inc(s["buffers_made"], 1)
                    pool.wait_ge(consts_in, CONSTS3)

                    def which_slots():
                        for j in range(N2):
                            gp.tensor_scalar(onehot[:, j, :], iota_t[:, :], idx1f[:, j:j + 1], None, ALU.is_equal).then_inc(pool_done, did.one())
                        pool.wait_ge(pool_done, did.n)
                        gp.tensor_scalar(iota_t[:, :], iota_t[:, :], float(P), None, ALU.add).then_inc(pool_done, did.one())
                        pool.wait_ge(pool_done, did.n)
                        pool.sem_inc(s["one_ready"], 1)

                    def rope_and_keys(b, p):
                        pool.wait_ge(s["qk_sb"], b + 1)
                        q4 = qk[:, :, :, :].rearrange("p a h d -> p (a h) d")
                        r4 = rot[:, :, :, :].rearrange("p a h d -> p (a h) d")
                        hf = HD // 2
                        gp.tensor_tensor(r4[:, :, 0:hf], q4[:, :, hf:HD], sinv[:, 0:hf].unsqueeze(1).to_broadcast([P, 2 * NH, hf]), ALU.mult).then_inc(pool_done, did.one())
                        gp.tensor_tensor(r4[:, :, hf:HD], q4[:, :, 0:hf], sinv[:, hf:HD].unsqueeze(1).to_broadcast([P, 2 * NH, hf]), ALU.mult).then_inc(pool_done, did.one())
                        pool.wait_ge(pool_done, did.n)
                        gp.tensor_tensor(q4, q4, cosv[:, :].unsqueeze(1).to_broadcast([P, 2 * NH, HD]), ALU.mult).then_inc(pool_done, did.one())
                        pool.wait_ge(pool_done, did.n)
                        gp.tensor_tensor(q4, q4, r4, ALU.add).then_inc(pool_done, did.one())
                        pool.wait_ge(pool_done, did.n)
                        pool.sem_inc(s["rope_ready"], 1)
                        pool.wait_ge(s["aT2_sb"], b + 1)
                        for a in range(2):
                            for c in range(HC):
                                gp.tensor_tensor(kd[p][a][:, c, :, :], kT[:, a, c, :].unsqueeze(1).to_broadcast([P, 4, P]),
                                                 grp[:, :].unsqueeze(2).to_broadcast([P, 4, P]), ALU.mult).then_inc(pool_done, did.one())
                        pool.wait_ge(pool_done, did.n)
                        pool.sem_inc(s["kd_ready"], 1)

                    def scatter(b, p):
                        pool.wait_ge(s["sl_ready"], b + 1)
                        pool.sem_inc(pool_passed, 1)
                        pool.indirect_dma_start(rows2, bass.IndirectOffsetOnAxis(ap=sl[p][:, :], axis=0), xn4[p][:, :], None,
                                                bounds_check=SLOTS2 - 1, oob_is_err=False).then_inc(xn4_out[p], 16)

                    def turn(b, p, proj, end, comb, scattered):
                        if comb:
                            pool.wait_ge(s["comb_ready"], b + 2)
                            pool.sem_inc(pool_passed, 1)
                            which_slots()
                        if proj:
                            rope_and_keys(b + 1, 1 - p)
                        if end:
                            scatter(b - 1, 1 - p)
                            pool.wait_ge(xn4_out[1 - p], scattered)
                            pool.sem_inc(s["x4_free"], 1)

                    which_slots()
                    rope_and_keys(0, 0)
                    pool.wait_ge(s["comb_ready"], 1)
                    which_slots()
                    for b, proj, end, comb in FIRST:
                        turn(b, b % 2, proj, end, comb, 0)
                    pool.wait_ge(pool_done, did.n)
                    pool.sem_inc(pool_done, -did.restart())
                    with pool.Fori(*LOOP) as b:
                        turn(b, 1, True, True, True, b * 8 + 8)
                        turn(b + 1, 0, True, True, True, b * 8 + 8)
                        pool.wait_ge(pool_done, did.n)
                        pool.sem_inc(pool_done, -did.restart())
                    for b, proj, end, comb in LASTS:
                        turn(b, b % 2, proj, end, comb, 16 * ((b - 1) // 2 + 1))
                    scatter(B - 1, 1)
                    pool.wait_ge(xn4_out[1], 16 * (B // 2))
                    pool.wait_ge(pool_done, did.n)
                    pool.sem_inc(pool_done, -did.restart())

                @block.scalar
                def _(act):
                    sc = nc.scalar
                    act.wait_ge(consts_in, CONSTS3)
                    sc.activation(hg[:, :], hg[:, :], ACT.Tanh).then_inc(hgate_made, 1)
                    act.wait_ge(s["buffers_made"], 1)

                    def hook(k, b, p, proj, end):
                        if proj and k == 1:
                            act.wait_ge(s["xcT_ready"], b + 2)
                            sc.activation(xT[:, :, :], mb_[:, 0:H], ACT.Copy).then_inc(s["xcT_sb"], 1)
                        if proj and k == 2:
                            act.wait_ge(s["qk_ready"], b + 2)
                            sc.activation(qk[:, :, :, :], mb_[:, :], ACT.Copy).then_inc(s["qk_sb"], 1)
                        if proj and k == 3:
                            act.wait_ge(s["ka_ready"], b + 2)
                            sc.activation(ak[:, :], mb_[:, 0:H], ACT.Copy)
                            sc.activation(vv[1 - p][1][:, :, 0:HD], mb_[:, H:2 * H].rearrange("p (h d) -> p h d", d=HD), ACT.Copy).then_inc(s["ka_sb"], 1)
                        if proj and k == 4:
                            act.wait_ge(s["v_ready"], b + 2)
                            sc.activation(vv[1 - p][0][:, :, 0:HD], mb_[:, 0:H].rearrange("p (h d) -> p h d", d=HD), ACT.Copy).then_inc(s["v_sb"], 1)
                        if proj and k == 5:
                            act.wait_ge(s["qkT_ready"], b + 2)
                            sc.activation(qT[1 - p][:, :, :], mb_[:, 0:H], ACT.Copy, scale=float(HD) ** -0.5)
                            sc.activation(kT[:, 0, :, :], mb_[:, H:2 * H], ACT.Copy).then_inc(s["qkT_sb"], 1)
                        if proj and k == 6:
                            act.wait_ge(s["aT2_ready"], b + 2)
                            sc.activation(kT[:, 1, :, :], mb_[:, 0:H], ACT.Copy).then_inc(s["aT2_sb"], 1)
                        if end and k == 7:
                            act.wait_ge(s["aT_ready"], b)
                            sc.activation(atT[:, :, :], mb_[:, 0:H], ACT.Copy).then_inc(s["aT_sb"], 1)
                        if end and k == 10:
                            act.wait_ge(s["x4T_ready"], b)
                            sc.activation(x4T[:, :, :], mb_[:, 0:H], ACT.Copy).then_inc(s["x4T_sb"], 1)
                        if end and k == 11:
                            act.wait_ge(s["ln_ready"], b)
                            sc.activation(e8[:, :], mb_[:, 0:E2], ACT.Exp, bias=sm[:, 0:1], accum_out=sm[:, 1:2]).then_inc(s["e8_ready"], 1)

                    def evacuate(b, w):
                        if w < NM:
                            act.wait_ge(s["tr_ready"], b * U + w + 1)
                            sc.activation(prT[w % 2][:, :, :], trp[:, :], ACT.Copy).then_inc(s["evac_main"], 1)

                    def outputs(b, w):
                        act.wait_ge(s["ot_ready"], b * 4 + w // 4 + 1)
                        sc.activation(ots[w // 4 % 2][:, :, :], otb[w // 4 % 2][:, :], ACT.Copy).then_inc(s["ot_sb"], 1)

                    def turn(b, p, proj, end, first=False):
                        for u in range(U):
                            if u >= 2:
                                evacuate(b, u - 2)
                            elif not first:
                                evacuate(b - 1, U + u - 2)
                            act.wait_ge(s["nm_ready"], b * U + u + 1)
                            if u >= 4 or not first:
                                act.wait_ge(s["tr_ready"], b * U + u - 3)
                            for h in range(4):
                                last = sc.activation(pr[u % 4][:, h, :], score[u % 4][:, h * P:(h + 1) * P], ACT.Exp, bias=nm[:, u % 4, h:h + 1])
                            last.then_inc(s["p_ready"], 1)
                            if u == 3 and not first:
                                outputs(b - 1, 15)
                            if u in (7, 11, 15):
                                outputs(b, u - 4)
                            hook(u, b, p, proj, end)

                    for k in range(7):
                        hook(k, -1, 1, True, False)
                    for b, proj, end, comb in FIRST:
                        turn(b, b % 2, proj, end, True)
                    with act.Fori(*LOOP) as b:
                        turn(b, 1, True, True)
                        turn(b + 1, 0, True, True)
                    for b, proj, end, comb in LASTS:
                        turn(b, b % 2, proj, end)
                    outputs(B - 1, 15)
                    for k in range(7, 12):
                        hook(k, B, 0, False, True)

                @block.vector
                def _(dve):
                    v, did = nc.vector, Count()
                    v.memset(before2[:, :], 0.0).then_inc(dve_done, did.one())
                    dve.wait_ge(s["buffers_made"], 1)
                    dve.wait_ge(hgate_made, 1)
                    dve.wait_ge(consts_in, CONSTS3)
                    dve.wait_ge(dve_done, did.n)

                    def batch(b):
                        return X[:, bass.ds(b, 1), :].rearrange("p a h -> p (a h)")

                    def normalise(dst, src):
                        v.bn_stats(st[:, :], src).then_inc(dve_done, did.one())
                        dve.wait_ge(dve_done, did.n)
                        v.bn_aggr(mv[:, :], st[:, :]).then_inc(dve_done, did.one())
                        dve.wait_ge(dve_done, did.n)
                        v.tensor_scalar(mvv[:, :], mv[:, 1:2], EPS, None, ALU.add).then_inc(dve_done, did.one())
                        dve.wait_ge(dve_done, did.n)
                        rsqrt(nc, dve, dve_done, did, rstd[:, :], mvv[:, :], rs_h[:, 0:1], rs_t[:, 0:1])
                        v.tensor_scalar(dst, src, mv[:, 0:1], rstd[:, 0:1], ALU.subtract, ALU.mult).then_inc(dve_done, did.one())
                        dve.wait_ge(dve_done, did.n)

                    def combined(b, p):
                        dve.wait_ge(s["comb_ready"], b + 1)
                        v.scalar_tensor_tensor(batch(b), mb_[:, 0:H], tanh_g[:, 2:3], batch(b), ALU.mult, ALU.add).then_inc(dve_done, did.one())
                        dve.wait_ge(dve_done, did.n)
                        normalise(xn[p][:, :], batch(b))
                        dve.sem_inc(s["xc_ready"], 1)

                    def mask_floor(b, p, loads):
                        dve.wait_ge(ctx_in[p], loads)
                        v.tensor_scalar(mk[p][:, :], mk[p][:, :], F32_MIN, None, ALU.max).then_inc(dve_done, did.one())
                        dve.wait_ge(dve_done, did.n)

                    def attended(b):
                        v.reciprocal(rr[:, :, :], oa[:, :, :, HD]).then_inc(dve_done, did.one())
                        dve.wait_ge(dve_done, did.n)
                        v.tensor_tensor(rr[:, 1, :], rr[:, 1, :], hg[:, :], ALU.mult).then_inc(dve_done, did.one())
                        dve.wait_ge(dve_done, did.n)
                        v.tensor_tensor(at[:, :, :], oa[:, 0, :, 0:HD], rr[:, 0, :].unsqueeze(2).to_broadcast([P, NH, HD]), ALU.mult).then_inc(dve_done, did.one())
                        v.tensor_tensor(at2[:, :, :], oa[:, 1, :, 0:HD], rr[:, 1, :].unsqueeze(2).to_broadcast([P, NH, HD]), ALU.mult).then_inc(dve_done, did.one())
                        dve.wait_ge(dve_done, did.n)
                        v.tensor_tensor(at[:, :, :], at[:, :, :], at2[:, :, :], ALU.add).then_inc(dve_done, did.one())
                        dve.wait_ge(dve_done, did.n)
                        dve.sem_inc(s["at_ready"], 1)

                    def projected(b, p):
                        dve.wait_ge(s["wo_ready"], b + 1)
                        v.scalar_tensor_tensor(batch(b), mb_[:, 0:H], tanh_g[:, 1:2], batch(b), ALU.mult, ALU.add).then_inc(dve_done, did.one())
                        dve.wait_ge(dve_done, did.n)
                        dve.wait_ge(s["x4_free"], b + 1)
                        normalise(xn4[p][:, :], batch(b))
                        dve.sem_inc(s["x4_ready"], 1)

                    def choose(b):
                        dve.wait_ge(s["lg_ready"], b + 1)
                        v.tensor_copy(c8[:, :], mb_[:, 0:E2]).then_inc(dve_done, did.one())
                        dve.wait_ge(dve_done, did.n)
                        v.max(t8[:, :], c8[:, :]).then_inc(dve_done, did.one())
                        dve.wait_ge(dve_done, did.n)
                        v.tensor_scalar(sm[:, 0:1], t8[:, 0:1], -1.0, None, ALU.mult).then_inc(dve_done, did.one())
                        dve.wait_ge(dve_done, did.n)
                        dve.sem_inc(s["ln_ready"], 1)
                        v.max_index(i8[:, :], t8[:, :], c8[:, :]).then_inc(dve_done, did.one())
                        dve.wait_ge(dve_done, did.n)
                        v.tensor_copy(sm[:, 2:3], i8[:, 0:1]).then_inc(dve_done, did.one())
                        dve.wait_ge(dve_done, did.n)
                        v.tensor_scalar(m8[:, :], iota_e[:, 0:E2], sm[:, 2:3], None, ALU.is_equal).then_inc(dve_done, did.one())
                        dve.wait_ge(dve_done, did.n)
                        v.tensor_copy(m8b[:, :], m8[:, :]).then_inc(dve_done, did.one())
                        dve.wait_ge(dve_done, did.n)
                        dve.sem_inc(s["m_ready"], 1)

                    def place(b, p):
                        dve.wait_ge(s["e8_ready"], b + 1)
                        v.reciprocal(sm[:, 3:4], sm[:, 1:2]).then_inc(dve_done, did.one())
                        dve.wait_ge(dve_done, did.n)
                        v.scalar_tensor_tensor(pe8[:, :], e8[:, :], sm[:, 3:4], m8[:, :], ALU.mult, ALU.mult).then_inc(dve_done, did.one())
                        dve.wait_ge(dve_done, did.n)
                        v.tensor_reduce(sm[:, 4:5], pe8[:, :], axis=AX.X, op=ALU.add).then_inc(dve_done, did.one())
                        dve.wait_ge(s["cum_ready"], b + 1)
                        v.tensor_tensor(c8[:, :], mb_[:, 0:E2], m8[:, :], ALU.mult).then_inc(dve_done, did.one())
                        dve.wait_ge(dve_done, did.n)
                        dve.sem_inc(s["cum_taken"], 1)
                        v.tensor_tensor(before2[:, :], before2[:, :], m8b[:, :], ALU.add).then_inc(dve_done, did.one())
                        v.tensor_reduce(sm[:, 5:6], c8[:, :], axis=AX.X, op=ALU.add).then_inc(dve_done, did.one())
                        dve.wait_ge(dve_done, did.n)
                        v.tensor_scalar(sm[:, 6:7], sm[:, 5:6], float(CAP2), None, ALU.is_le).then_inc(dve_done, did.one())
                        v.scalar_tensor_tensor(sm[:, 8:9], sm[:, 2:3], float(CAP2), sm[:, 5:6], ALU.mult, ALU.add).then_inc(dve_done, did.one())
                        dve.wait_ge(dve_done, did.n)
                        v.tensor_tensor(wt2[:, bass.ds(b, 1)], sm[:, 4:5], sm[:, 6:7], ALU.mult).then_inc(dve_done, did.one())
                        v.tensor_scalar(sm[:, 7:8], sm[:, 6:7], -SKIP, SKIP - 1.0, ALU.mult, ALU.add).then_inc(dve_done, did.one())
                        dve.wait_ge(dve_done, did.n)
                        v.tensor_tensor(sm[:, 8:9], sm[:, 8:9], sm[:, 7:8], ALU.add).then_inc(dve_done, did.one())
                        dve.wait_ge(dve_done, did.n)
                        v.tensor_copy(sl[p][:, :], sm[:, 8:9]).then_inc(dve_done, did.one())
                        v.tensor_scalar(slot_g[:, bass.ds(b, 1)], sm[:, 8:9], float(SLOTS2), None, ALU.min).then_inc(dve_done, did.one())
                        dve.wait_ge(dve_done, did.n)
                        dve.sem_inc(s["sl_ready"], 1)

                    def evacuate(b, w):
                        if w >= NM:
                            dve.wait_ge(s["tr_ready"], b * U + w + 1)
                            v.tensor_copy(prT[w % 2][:, :, :], trp[:, :]).then_inc(s["evac_ad"], 1)

                    def outputs(b, w):
                        a, half = w // 8, w // 4 % 2
                        dve.wait_ge(s["ob_ready"], b * 4 + w // 4 + 1)
                        v.tensor_copy(oa[:, a, 16 * half:16 * half + 16, :], otb[w // 4 % 2][:, :].rearrange("p (h d) -> p h d", d=32)[:, :, 0:HD + 1]).then_inc(dve_done, did.one())
                        dve.wait_ge(dve_done, did.n)
                        dve.sem_inc(s["o_taken"], 1)

                    def turn(b, p, loads, proj, end, comb, first=False):
                        mask_floor(b, p, loads)
                        for u in range(U):
                            dve.wait_ge(s["sc_ready"], b * U + u + 1)
                            sp4 = score[u % 4][:, :].rearrange("p (h t) -> p h t", h=4)
                            if u < NM:
                                v.tensor_tensor(sp4, sp4, mk[p][:, :].unsqueeze(1).to_broadcast([P, 4, P]), ALU.add).then_inc(dve_done, did.one())
                                dve.wait_ge(dve_done, did.n)
                            if u >= 4 or not first:
                                dve.wait_ge(s["p_ready"], b * U + u - 3)
                            v.tensor_reduce(nm[:, u % 4, :], sp4, axis=AX.X, op=ALU.max, negate=True).then_inc(s["nm_ready"], 1)
                            if u >= 2:
                                evacuate(b, u - 2)
                            elif not first:
                                evacuate(b - 1, U + u - 2)
                            if u == NM:
                                dve.wait_ge(dve_done, did.n)
                                dve.sem_inc(s["cin_free"], 1)
                            if u in (1, 5) and not first:
                                outputs(b - 1, 8 + 4 * (u // 4))
                            if u in (9, 13):
                                outputs(b, 4 * ((u - 9) // 4))
                            if end and u == 5:
                                attended(b - 1)
                            if end and u == 8:
                                projected(b - 1, 1 - p)
                            if end and u == 11:
                                choose(b - 1)
                            if end and u == 12:
                                place(b - 1, 1 - p)
                            if comb and u == 15:
                                combined(b + 2, p)

                    combined(0, 0)
                    combined(1, 1)
                    for b, proj, end, comb in FIRST:
                        turn(b, b % 2, 32, proj, end, comb, True)
                    dve.wait_ge(dve_done, did.n)
                    dve.sem_inc(dve_done, -did.restart())
                    with dve.Fori(*LOOP) as b:
                        turn(b, 1, b * 16 + 16, True, True, True)
                        turn(b + 1, 0, b * 16 + 48, True, True, True)
                        dve.wait_ge(dve_done, did.n)
                        dve.sem_inc(dve_done, -did.restart())
                    for b, proj, end, comb in LASTS:
                        turn(b, b % 2, 32 * (b // 2 + 1), proj, end, comb)
                    for w in (14, 15):
                        evacuate(B - 1, w)
                    outputs(B - 1, 8)
                    outputs(B - 1, 12)
                    attended(B - 1)
                    projected(B - 1, 1)
                    choose(B - 1)
                    place(B - 1, 1)
                    dve.wait_ge(dve_done, did.n)
                    dve.sem_inc(dve_done, -did.restart())

                @block.tensor
                def _(pe):
                    t = nc.tensor
                    pe.wait_ge(consts_in, CONSTS3)
                    pe.wait_ge(s["buffers_made"], 1)

                    def combine(b, j0, j1):
                        if j0 == 0:
                            pe.wait_ge(s["one_ready"], b + 1)
                        for j in range(j0, j1):
                            for k in range(3):
                                last = t.matmul(mb_[:, 0:H], onehot[:, j, :], parts[:, j, k, :], start=j == 0 and k == 0, stop=j == N2 - 1 and k == 2)
                        if j1 == N2:
                            last.then_inc(s["comb_ready"], 1)

                    def hook(k, b, p, loads, proj, end, comb):
                        if proj and k == 1:
                            pe.wait_ge(s["xc_ready"], b + 2)
                            for c in range(HC):
                                last = t.transpose(mb_[:, c * P:(c + 1) * P], xn[1 - p][:, c * P:(c + 1) * P], idn[:, :])
                            last.then_inc(s["xcT_ready"], 1)
                        if proj and k == 2:
                            pe.wait_ge(s["xcT_sb"], b + 2)
                            for c in range(HC):
                                last = t.matmul(mb_[:, :], xT[:, c, :], wq[:, c, 0:2 * H], start=c == 0, stop=c == HC - 1)
                            last.then_inc(s["qk_ready"], 1)
                        if proj and k == 3:
                            pe.wait_ge(s["qk_sb"], b + 2)
                            pe.wait_ge(ctx_in[1 - p], loads)
                            for c in range(HC):
                                last = t.matmul(mb_[:, :], cT[1 - p][:, c, :], wq[:, c, H:3 * H], start=c == 0, stop=c == HC - 1)
                            last.then_inc(s["ka_ready"], 1)
                        if proj and k == 4:
                            pe.wait_ge(s["ka_sb"], b + 2)
                            for c in range(HC):
                                last = t.matmul(mb_[:, 0:H], xT[:, c, :], wq[:, c, 2 * H:3 * H], start=c == 0, stop=c == HC - 1)
                            last.then_inc(s["v_ready"], 1)
                        if proj and k == 5:
                            pe.wait_ge(s["v_sb"], b + 2)
                            pe.wait_ge(s["rope_ready"], b + 2)
                            for a in range(2):
                                for c in range(HC):
                                    src = qk[:, a, c * (NH // 2):(c + 1) * (NH // 2), :].rearrange("p h d -> p (h d)")
                                    last = t.transpose(mb_[:, a * H + c * P:a * H + (c + 1) * P], src, idn[:, :])
                            last.then_inc(s["qkT_ready"], 1)
                        if proj and k == 6:
                            pe.wait_ge(s["qkT_sb"], b + 2)
                            for c in range(HC):
                                last = t.transpose(mb_[:, c * P:(c + 1) * P], ak[:, c * P:(c + 1) * P], idn[:, :])
                            last.then_inc(s["aT2_ready"], 1)
                        if end and k == 7:
                            if proj:
                                pe.wait_ge(s["aT2_sb"], b + 2)
                            pe.wait_ge(s["at_ready"], b)
                            for c in range(HC):
                                last = t.transpose(mb_[:, c * P:(c + 1) * P], at[:, c * (NH // 2):(c + 1) * (NH // 2), :].rearrange("p h d -> p (h d)"), idn[:, :])
                            last.then_inc(s["aT_ready"], 1)
                        if end and k == 8:
                            pe.wait_ge(s["aT_sb"], b)
                            for c in range(HC):
                                last = t.matmul(mb_[:, 0:H], atT[:, c, :], wo_sb[:, c, :], start=c == 0, stop=c == HC - 1)
                            last.then_inc(s["wo_ready"], 1)
                        if end and k == 10:
                            pe.wait_ge(s["x4_ready"], b)
                            for c in range(HC):
                                last = t.transpose(mb_[:, c * P:(c + 1) * P], xn4[1 - p][:, c * P:(c + 1) * P], idn[:, :])
                            last.then_inc(s["x4T_ready"], 1)
                        if end and k == 11:
                            pe.wait_ge(s["x4T_sb"], b)
                            for c in range(HC):
                                last = t.matmul(mb_[:, 0:E2], x4T[:, c, :], g2w[:, c, :], start=c == 0, stop=c == HC - 1)
                            last.then_inc(s["lg_ready"], 1)
                        if end and k == 12:
                            pe.wait_ge(s["m_ready"], b)
                            pe.wait_ge(s["e8_ready"], b)
                            t.matmul(mb_[:, 0:E2], upr[:, :], m8b[:, :], start=True, stop=False)
                            t.matmul(mb_[:, 0:E2], ones_b[:, :], before2[:, :], start=False, stop=True).then_inc(s["cum_ready"], 1)
                        if comb and k == 13:
                            if end:
                                pe.wait_ge(s["cum_taken"], b)
                            combine(b + 2, 0, 6)
                        if comb and k == 14:
                            combine(b + 2, 6, 11)
                        if comb and k == 15:
                            combine(b + 2, 11, N2)

                    def transposes(b, w, first=False):
                        pe.wait_ge(s["p_ready"], b * U + w + 1)
                        if w == 0 and not first:
                            pe.wait_ge(s["evac_ad"], b * NM)
                        if 1 <= w <= NM:
                            pe.wait_ge(s["evac_main"], b * NM + w)
                        if w > NM:
                            pe.wait_ge(s["evac_ad"], b * NM + w - NM)
                        for h in range(4):
                            last = t.transpose(trp[:, h * P:(h + 1) * P], pr[w % 4][:, h, :], idn[:, :])
                        last.then_inc(s["tr_ready"], 1)

                    def values(b, p, w, first=False):
                        if w < NM:
                            pe.wait_ge(s["evac_main"], b * NM + w + 1)
                        else:
                            pe.wait_ge(s["evac_ad"], b * NM + w - NM + 1)
                        if w % 4 == 0 and not (first and w < 8):
                            pe.wait_ge(s["o_taken"], b * 4 + w // 4 - 1)
                        for h in range(4):
                            last = t.matmul(otb[w // 4 % 2][32 * h:32 * h + 32, w % 4 * P:(w % 4 + 1) * P], vv[p][w // NM][:, 4 * (w % NM) + h, :],
                                            prT[w % 2][:, h, :], start=True, stop=True)
                        if w % 4 == 3:
                            last.then_inc(s["ot_ready"], 1)

                    def outputs(b, w):
                        pe.wait_ge(s["ot_sb"], b * 4 + w // 4 + 1)
                        for k in range(4):
                            last = t.transpose(otb[w // 4 % 2][:, k * P:(k + 1) * P], ots[w // 4 % 2][:, k, :], idn[:, :])
                        last.then_inc(s["ob_ready"], 1)

                    def turn(b, p, loads, proj, end, comb, first=False):
                        pe.wait_ge(s["kd_ready"], b + 1)
                        for u in range(U):
                            if u >= 4 or not first:
                                pe.wait_ge(s["p_ready"], b * U + u - 3)
                            a, c, i = u // NM, u % NM // 4, u % 4
                            t.matmul(score[u % 4][:, :], qT[p][32 * i:32 * i + 32, c, :], kd[p][a][32 * i:32 * i + 32, c, :, :],
                                     start=True, stop=True).then_inc(s["sc_ready"], 1)
                            if u >= 2:
                                transposes(b, u - 2, first)
                            elif not first:
                                transposes(b - 1, U + u - 2)
                            if u >= 3:
                                values(b, p, u - 3, first)
                            elif not first:
                                values(b - 1, 1 - p, U + u - 3)
                            if u in (0, 4) and not first:
                                outputs(b - 1, 8 + u)
                            if u in (8, 12):
                                outputs(b, u - 8)
                            hook(u, b, p, loads, proj, end, comb)

                    combine(0, 0, N2)
                    for k in range(7):
                        hook(k, -1, 1, 32, True, False, False)
                    pe.wait_ge(s["aT2_sb"], 1)
                    combine(1, 0, N2)
                    for b, proj, end, comb in FIRST:
                        turn(b, b % 2, 32, proj, end, comb, True)
                    with pe.Fori(*LOOP) as b:
                        turn(b, 1, b * 16 + 48, True, True, True)
                        turn(b + 1, 0, b * 16 + 48, True, True, True)
                    for b, proj, end, comb in LASTS:
                        turn(b, b % 2, 32 * ((b + 1) // 2 + 1), proj, end, comb)
                    for w in (14, 15):
                        transposes(B - 1, w)
                        values(B - 1, 1, w - 1)
                    values(B - 1, 1, 15)
                    outputs(B - 1, 8)
                    outputs(B - 1, 12)
                    for k in range(7, 13):
                        hook(k, B, 0, 0, False, True, False)

        with ExitStack() as ph:
            w1s = [sb(f"w1s{q}", [P, HC, H], where=ph) for q in range(2)]
            w2s = [sb(f"w2s{q}", [P, HC, H], where=ph) for q in range(2)]
            xe = [sb(f"xe{q}", [P, 3, H], where=ph) for q in range(2)]
            xeT = [sb(f"xeT{q}", [P, HC, CAP2], where=ph) for q in range(2)]
            mid = [sb(f"mid{q}", [P, HC, CAP2], where=ph) for q in range(2)]
            ye = [sb(f"ye{q}", [P, 3, H], where=ph) for q in range(2)]
            sgc = [sb(f"sgc{q}", [P, 1], U32, where=ph) for q in range(2)]
            yg = [sb(f"yg{q}", [P, H], where=ph) for q in range(2)]
            res = [sb(f"res{q}", [P, H], where=ph) for q in range(2)]
            names = ["in_free", "xt_ready", "xt_sb", "h_ready", "h_sb", "y_ready", "y_sb", "yg_free", "res_ready"]
            s = {n: sem("d_" + n) for n in names}
            e_in = [sem(f"e_in{q}") for q in range(2)]
            y_out = [sem(f"y_out{q}") for q in range(2)]
            yg_in = [sem(f"yg_in{q}") for q in range(2)]
            res_out = [sem(f"res_out{q}") for q in range(2)]
            with nc.Block() as block:
                @block.sync
                def _(sp):
                    for q in range(2):
                        sp.sem_inc(s["in_free"], 1)
                    with sp.Fori(0, E2 // 2) as it:
                        for q in range(2):
                            e = it * 2 + q
                            sp.wait_ge(s["in_free"], e + 1)
                            sp.dma_start(w1s[q][:, :, :], w1[:, bass.ds(e, 1), :, :].rearrange("p a c n -> p (a c) n")).then_inc(e_in[q], 16)
                            sp.dma_start(w2s[q][:, :, :], w2[:, bass.ds(e, 1), :, :].rearrange("p a c n -> p (a c) n")).then_inc(e_in[q], 16)
                            sp.dma_start(xe[q][:, 0:2, :], rows2[bass.ds(e * CAP2, 2 * P), :].rearrange("(c p) n -> p c n", p=P)).then_inc(e_in[q], 16)
                            sp.dma_start(xe[q][0:64, 2, :], rows2[bass.ds(e * CAP2 + 2 * P, 64), :]).then_inc(e_in[q], 16)

                @block.scalar
                def _(act):
                    sc = nc.scalar
                    for q in range(2):
                        act.sem_inc(y_out[q], 32)
                    with act.Fori(0, E2 // 2) as it:
                        for q in range(2):
                            n = it * 2 + q + 1
                            act.wait_ge(s["h_ready"], n)
                            for m in range(HC):
                                last = sc.activation(mid[q][:, m, :], pb[2 + m][:, 0:CAP2], ACT.Gelu)
                            last.then_inc(s["h_sb"], 1)
                            act.wait_ge(s["y_sb"], n)
                            act.dma_start(youts[bass.ds((it * 2 + q) * CAP2, 2 * P), :].rearrange("(c p) n -> p c n", p=P), ye[q][:, 0:2, :]).then_inc(y_out[q], 16)
                            act.dma_start(youts[bass.ds((it * 2 + q) * CAP2 + 2 * P, 64), :], ye[q][0:64, 2, :]).then_inc(y_out[q], 16)
                    for q in range(2):
                        act.sem_inc(res_out[q], 16)
                    with act.Fori(0, B // 2) as it:
                        for q in range(2):
                            act.wait_ge(s["res_ready"], it * 2 + q + 1)
                            act.dma_start(out[:, bass.ds(it * 2 + q, 1), :].rearrange("p a h -> p (a h)"), res[q][:, :]).then_inc(res_out[q], 16)
                    for q in range(2):
                        act.wait_ge(res_out[q], 16 * (B // 2 + 1))

                @block.gpsimd
                def _(pool):
                    gp, did = nc.gpsimd, Count()
                    for q in range(2):
                        pool.sem_inc(s["yg_free"], 1)
                        pool.wait_ge(y_out[q], 32 * (E2 // 2 + 1))
                    with pool.Fori(0, B // 2) as it:
                        for q in range(2):
                            pool.wait_ge(s["yg_free"], it * 2 + q + 1)
                            gp.tensor_copy(sgc[q][:, :], slot_g[:, bass.ds(it * 2 + q, 1)]).then_inc(pool_done, did.one())
                            pool.wait_ge(pool_done, did.n)
                            pool.indirect_dma_start(yg[q][:, :], None, youts, bass.IndirectOffsetOnAxis(ap=sgc[q][:, :], axis=0),
                                                    bounds_check=SLOTS2, oob_is_err=False).then_inc(yg_in[q], 16)
                        pool.wait_ge(pool_done, did.n)
                        pool.sem_inc(pool_done, -did.restart())

                @block.vector
                def _(dve):
                    v, did = nc.vector, Count()
                    with dve.Fori(0, E2 // 2) as it:
                        for q in range(2):
                            n = it * 2 + q + 1
                            dve.wait_ge(s["xt_ready"], n)
                            for c in range(HC):
                                v.tensor_copy(xeT[q][:, c, :], pb[c][:, 0:CAP2]).then_inc(dve_done, did.one())
                            dve.wait_ge(dve_done, did.n)
                            dve.sem_inc(s["xt_sb"], 1)
                            dve.wait_ge(s["y_ready"], n)
                            dve.wait_ge(y_out[q], it * 32 + 32)
                            v.tensor_copy(ye[q][:, 0:2, :], pb[4][:, :]).then_inc(dve_done, did.one())
                            v.tensor_copy(ye[q][0:64, 2, :], pb[5][0:64, 0:H]).then_inc(dve_done, did.one())
                            dve.wait_ge(dve_done, did.n)
                            dve.sem_inc(s["y_sb"], 1)
                        dve.wait_ge(dve_done, did.n)
                        dve.sem_inc(dve_done, -did.restart())
                    with dve.Fori(0, B // 2) as it:
                        for q in range(2):
                            dve.wait_ge(yg_in[q], it * 16 + 16)
                            v.tensor_scalar(yg[q][:, :], yg[q][:, :], wt2[:, bass.ds(it * 2 + q, 1)], tanh_g[:, 3:4], ALU.mult, ALU.mult).then_inc(dve_done, did.one())
                            dve.wait_ge(dve_done, did.n)
                            dve.wait_ge(res_out[q], it * 16 + 16)
                            v.tensor_tensor(res[q][:, :], yg[q][:, :], X[:, bass.ds(it * 2 + q, 1), :].rearrange("p a h -> p (a h)"), ALU.add).then_inc(dve_done, did.one())
                            dve.wait_ge(dve_done, did.n)
                            dve.sem_inc(s["res_ready"], 1)
                            dve.sem_inc(s["yg_free"], 1)
                        dve.wait_ge(dve_done, did.n)
                        dve.sem_inc(dve_done, -did.restart())

                @block.tensor
                def _(pe):
                    t = nc.tensor
                    with pe.Fori(0, E2 // 2) as it:
                        for q in range(2):
                            n = it * 2 + q + 1
                            pe.wait_ge(e_in[q], it * 64 + 64)
                            for c in range(HC):
                                for o, m in CH2:
                                    last = t.transpose(pb[c][:, o:o + m], xe[q][0:m, o // P, c * P:(c + 1) * P], idn[0:m, 0:m])
                            last.then_inc(s["xt_ready"], 1)
                            pe.wait_ge(s["xt_sb"], n)
                            for m in range(HC):
                                for c in range(HC):
                                    last = t.matmul(pb[2 + m][:, 0:CAP2], w1s[q][:, c, m * P:(m + 1) * P], xeT[q][:, c, :], start=c == 0, stop=c == HC - 1)
                            last.then_inc(s["h_ready"], 1)
                            pe.wait_ge(s["h_sb"], n)
                            for j, (o, m) in enumerate(CH2):
                                for c in range(HC):
                                    last = t.matmul(pb[4 + j // 2][0:m, (j % 2) * H:(j % 2) * H + H], mid[q][:, c, o:o + m], w2s[q][:, c, :], start=c == 0, stop=c == HC - 1)
                            last.then_inc(s["y_ready"], 1)
                            pe.wait_ge(s["y_sb"], n)
                            pe.sem_inc(s["in_free"], 1)


def kernel(**a):
    import concourse.bacc as bacc
    from concourse import mybir as _mb
    from concourse.bass_utils import run_bass_kernel_spmd
    import ml_dtypes

    g = {k: np.asarray(v) for k, v in a.items()}
    f = np.float32
    inv = 1.0 / 10000.0 ** (np.arange(0, HD, 2, dtype=f) / HD)
    emb = np.outer(np.arange(S, dtype=f), inv)
    emb = np.concatenate([emb, emb], -1)
    cosv, sinv = np.cos(emb).astype(f), np.sin(emb).astype(f)
    sinv[:, :HD // 2] *= -1
    rows = np.arange(P)
    wgu = np.concatenate([g["L0_ffn_w_gate"], g["L0_ffn_w_up"]], -1)
    ins = {
        "x": g["x"].transpose(1, 0, 2), "ctx": g["ctx_2048"].transpose(1, 0, 2),
        "ctxT": g["ctx_2048"].transpose(0, 2, 1).reshape(B, HC, P, S).transpose(0, 2, 1, 3),
        "mask": g["mask_Bx1xSxS_fk0"][:, 0],
        "gates": np.concatenate([g["g_xattn"], g["g_ffn"]]),
        "theta_w": g["L0_xattn_theta_w"].T, "theta_b": g["L0_xattn_theta_b"][:, None],
        "phi_w": g["L0_xattn_phi_w"].T, "phi_b": g["L0_xattn_phi_b"][:, None],
        "g_w": g["L0_xattn_g_w"].T, "g_b": g["L0_xattn_g_b"],
        "gamma": g["L0_xattn_ln_gamma"], "beta": g["L0_xattn_ln_beta"],
        "out_w": g["L0_xattn_out_w"].T, "out_b": g["L0_xattn_out_b"][:, None],
        "gate1_w": g["L0_ffn_gate_w"].T.reshape(HC, P, E1).transpose(1, 0, 2),
        "w_gu": wgu.reshape(E1, HC, P, 2 * I1).transpose(2, 0, 1, 3),
        "w_d": g["L0_ffn_w_down"].reshape(E1, 2, I1H, H).transpose(2, 0, 1, 3),
        "sw_gu": np.concatenate([g["L0_ffn_sw_gate"], g["L0_ffn_sw_up"]], -1).reshape(HC, P, 2 * IS).transpose(1, 0, 2),
        "sw_d": g["L0_ffn_sw_down"],
        "wqkv": np.concatenate([g["L1_xattn_Wq"], g["L1_xattn_Wk"], g["L1_xattn_Wv"]], -1).reshape(HC, P, 3 * H).transpose(1, 0, 2),
        "wo": g["L1_xattn_Wo"].reshape(HC, P, H).transpose(1, 0, 2),
        "hgate": g["L1_xattn_gate"].reshape(NH),
        "gate2_w": g["L1_ffn_gate_weight"].T.reshape(HC, P, E2).transpose(1, 0, 2),
        "w1": g["L1_ffn_w1"].reshape(E2, HC, P, H).transpose(2, 0, 1, 3),
        "w2": g["L1_ffn_w2"].reshape(E2, HC, P, H).transpose(2, 0, 1, 3),
        "ident": np.eye(P, dtype=f), "upper": np.triu(np.ones((P, P), f)).astype(ml_dtypes.bfloat16),
        "cos": cosv, "sin": sinv,
        "group": (rows[:, None] % 32 // 8 == np.arange(4)).astype(f),
        "quarter": (rows[:, None] // 32 == np.arange(4)).astype(f),
    }
    nc = bacc.Bacc("TRN2", target_bir_lowering=False, num_devices=1)
    arrays, args = {}, []
    for name, v in ins.items():
        arrays[f"in_{name}"] = v = np.ascontiguousarray(v)
        args.append(nc.dram_tensor(f"in_{name}", v.shape, _mb.dt.from_np(v.dtype), kind="ExternalInput").ap())
    args.append(nc.dram_tensor("out_x", (P, B, H), _mb.dt.float32, kind="ExternalOutput").ap())
    build(nc, *args)
    r = run_bass_kernel_spmd(nc, [arrays], core_ids=[0])
    return r.results[0]["out_x"].transpose(1, 0, 2)
```

```python
import concourse.bass as bass
from concourse import mybir
from contextlib import ExitStack
import numpy as np

F32 = mybir.dt.float32
BF16 = mybir.dt.bfloat16
U32 = mybir.dt.uint32
I32 = mybir.dt.int32
ACT = mybir.ActivationFunctionType
ALU = mybir.AluOpType
AX = mybir.AxisListType

P = 128
B, S, H = 16, 128, 256
TOK = B * S
HC = H // P
LAT = 64
E1, K1, I1, CAP1 = 64, 6, 176, 32
SLOTS1 = E1 * CAP1
I1H = I1 // 2
IS = 352
ISC = [(0, 128), (128, 128), (256, 96)]
ROW = H + E1
NH, HD = 32, 8
E2, CAP2 = 8, 320
SLOTS2 = E2 * CAP2
CH2 = [(0, 128), (128, 128), (256, 64)]
EPS = 1e-5
RSQRT_MAGIC = 0x5F3759DF
F32_MIN = float(np.finfo(np.float32).min)
SKIP = 1.0e6

W1 = 4
R2 = 4


class Count:

    def __init__(self):
        self.n = 0

    def one(self):
        self.n += 1
        return 1

    def restart(self):
        n, self.n = self.n, 0
        return n


def rsqrt(nc, dve, done, count, y, v, half, t):
    vec = nc.vector
    vec.tensor_scalar(t.bitcast(I32), v.bitcast(I32), 1, None, ALU.arith_shift_right).then_inc(done, count.one())
    dve.wait_ge(done, count.n)
    vec.tensor_scalar(y.bitcast(I32), t.bitcast(I32), -1.0, float(RSQRT_MAGIC), ALU.mult, ALU.add).then_inc(done, count.one())
    dve.wait_ge(done, count.n)
    for _ in range(3):
        vec.scalar_tensor_tensor(t, y, -0.5, y, ALU.mult, ALU.mult).then_inc(done, count.one())
        dve.wait_ge(done, count.n)
        vec.tensor_tensor(half, t, v, ALU.mult).then_inc(done, count.one())
        dve.wait_ge(done, count.n)
        vec.scalar_tensor_tensor(y, half, 1.5, y, ALU.add, ALU.mult).then_inc(done, count.one())
        dve.wait_ge(done, count.n)


def build(nc, x, ctx, ctxT, mask, gates, theta_w, theta_b, phi_w, phi_b, g_w, g_b, gamma, beta, out_w, out_b,
          gate1_w, w_gu, w_d, sw_gu, sw_d, wqkv, wo, hgate, gate2_w, w1, w2, ident, upper, cos, sin, group, quarter,
          out):
    rows1 = nc.dram_tensor("rows1", [TOK + 1, ROW], F32, kind="Internal").ap()
    rows2 = nc.dram_tensor("rows2", [SLOTS2, H], F32, kind="Internal").ap()
    youts = nc.dram_tensor("youts", [SLOTS2 + 1, H], F32, kind="Internal").ap()

    with ExitStack() as whole:
        def sb(name, shape, dt=F32, where=whole):
            return where.enter_context(nc.sbuf_tensor(name, shape, dt))

        def sem(name):
            return whole.enter_context(nc.semaphore(name))

        pb = [whole.enter_context(nc.psum_tensor(f"bank{i}", [P, 512], F32)) for i in range(8)]

        X = sb("X", [P, B, H])
        idn = sb("idn", [P, P])
        upr = sb("upr", [P, P], BF16)
        ones_b = sb("ones_b", [P, P], BF16)
        tanh_g = sb("tanh_g", [P, 4])
        iota_e = sb("iota_e", [P, E1])
        idx1f = sb("idx1f", [P, B])
        idx1 = sb("idx1", [P, B], U32)
        rs_t, rs_h = sb("rs_t", [P, W1]), sb("rs_h", [P, W1])
        zrow = sb("zrow", [P, ROW])
        shared = sb("shared", [P, B * 3 * H], BF16)
        parts = shared[:, :].rearrange("p (j k h) -> p j k h", k=3, h=H)
        slot_g = sb("slot_g", [P, B], U32)
        wt2 = sb("wt2", [P, B])

        dve_done, pool_done = sem("dve_done"), sem("pool_done")
        pe_passed, pool_passed = sem("pe_passed"), sem("pool_passed")
        consts_in, zero_made, zero_out = sem("consts_in"), sem("zero_made"), sem("zero_out")
        tanh_made, hgate_made = sem("tanh_made"), sem("hgate_made")

        phase12 = ExitStack()
        wgu_sb = [sb(f"wgu{r}", [P, 4, HC, 2 * I1], where=phase12) for r in range(R2)]
        wd_sb = [sb(f"wd{r}", [I1H, 4, 2, H], where=phase12) for r in range(R2)]
        experts_in = [sem(f"experts_in{r}") for r in range(R2)]
        experts_free = sem("experts_free")

        with ExitStack() as ph:
            CX = shared[:, 0:2 * B * H].bitcast(F32).rearrange("p (b h) -> p b h", h=H)
            G = [shared[:, (2 * B + 8 * i) * H:(2 * B + 8 * i + 8) * H].rearrange("p (e c) -> p e c", c=CAP1) for i in range(2)]
            G += [sb(f"G{i}", [P, E1, CAP1], BF16, where=ph) for i in range(2, W1)]
            thw, phw, gw = (sb(n, [P, LAT], where=ph) for n in ("thw", "phw", "gw"))
            thb, phb = (sb(n, [LAT, 1], where=ph) for n in ("thb", "phb"))
            gb = sb("gb", [P, 2, LAT], where=ph)
            gam, bet = (sb(n, [LAT, H], where=ph) for n in ("gam", "bet"))
            ow, ob = sb("ow", [LAT, P], where=ph), sb("ob", [P, 1], where=ph)
            mean64 = sb("mean64", [LAT, LAT], where=ph)
            g1w = sb("g1w", [P, HC, E1], where=ph)
            sgu = sb("sgu", [P, HC, 2 * IS], where=ph)
            sdn = sb("sdn", [P, 3, H], where=ph)
            iota_c = sb("iota_c", [P, CAP1], BF16, where=ph)
            xn = [sb(f"xn{p}", [P, H], where=ph) for p in range(W1)]
            wx = [sb(f"wx{p}", [P, H], where=ph) for p in range(2)]
            th = [sb(f"th{p}", [LAT, 2 * H], where=ph) for p in range(W1)]
            gx = [sb(f"gx{p}", [P, 2, LAT], where=ph) for p in range(W1)]
            pr = [sb(f"pr{p}", [P, 2, H], where=ph) for p in range(W1)]
            prT = [sb(f"prT{p}", [P, 2, H], where=ph) for p in range(W1)]
            hh = [sb(f"hh{p}", [LAT, H], where=ph) for p in range(W1)]
            row = sb("row", [P, W1, ROW], where=ph)
            xT = [sb(f"xT{p}", [P, HC, P], where=ph) for p in range(W1)]
            sg = [sb(f"sg{p}", [P, 3, P], where=ph) for p in range(W1)]
            st = sb("st", [P, W1, 6], where=ph)
            mv = sb("mv", [P, W1, 2], where=ph)
            mvv = sb("mvv", [P, W1], where=ph)
            rstd = sb("rstd", [P, W1], where=ph)
            st2 = sb("st2", [LAT, W1, 2], where=ph)
            nmax = sb("nmax", [P, W1, 2], where=ph)
            psm = sb("psm", [P, W1, 2], where=ph)
            rin = sb("rin", [P, W1, 2], where=ph)
            t8 = sb("t8", [P, W1, 8], where=ph)
            i8 = sb("i8", [P, W1, 8], U32, where=ph)
            i8f = sb("i8f", [P, W1, 8], where=ph)
            ex = sb("ex", [P, W1, E1], where=ph)
            eq = sb("eq", [P, 2, K1, E1], where=ph)
            mf = sb("mf", [P, 2, E1], where=ph)
            mb = sb("mb", [P, W1, E1], BF16, where=ph)
            before = sb("before", [P, W1 + 1, E1], BF16, where=ph)
            cumc = sb("cumc", [P, W1, E1], BF16, where=ph)

            names = ["x_in", "xn_ready", "pt_ready", "gxp_ready", "pt_sb", "gx_sb", "sc_ready", "nm_ready",
                     "p_ready", "pn_ready", "ptr_ready", "prT_sb", "tx_ready", "st2_ready", "mu_ready",
                     "hn_ready", "h_ready", "w_ready", "xn2_ready", "xt_ready", "xT_sb", "lg_ready", "gu_ready",
                     "lnm_ready", "e_ready", "mb_ready", "cum_ready", "G_ready", "ix_ready", "sg_ready",
                     "hs_ready", "dn_ready", "banks_free", "row_ready"]
            s = {n: sem(n) for n in names}
            row_out = [sem(f"row_out{p}") for p in range(W1)]
            bank_a = [pb[2 * p] for p in range(W1)]
            bank_b = [pb[2 * p + 1] for p in range(W1)]
            NIT = B // W1

            with nc.Block() as block:
                @block.sync
                def _(sp):
                    for dst, src in ((idn, ident), (upr, upper), (thw, theta_w), (phw, phi_w), (gw, g_w), (thb, theta_b),
                                     (phb, phi_b), (gam, gamma), (bet, beta), (ow, out_w), (ob, out_b)):
                        sp.dma_start(dst[:, :], src).then_inc(consts_in, 16)
                    sp.dma_start(gb[:, :, :], g_b.rearrange("(a c l) -> a c l", a=1, c=1).to_broadcast([P, 2, LAT])).then_inc(consts_in, 16)
                    sp.dma_start(tanh_g[:, :], gates.rearrange("(a n) -> a n", a=1).to_broadcast([P, 4])).then_inc(consts_in, 16)
                    sp.dma_start(g1w[:, :, :], gate1_w).then_inc(consts_in, 16)
                    sp.dma_start(sgu[:, :, :], sw_gu).then_inc(consts_in, 16)
                    sp.dma_start(sdn[:, 0:2, :], sw_d[0:2 * P, :].rearrange("(c p) n -> p c n", p=P)).then_inc(consts_in, 16)
                    sp.dma_start(sdn[0:IS - 2 * P, 2, :], sw_d[2 * P:IS, :]).then_inc(consts_in, 16)
                    def load_batches(it):
                        sp.dma_start(X[:, bass.ds(it * W1, W1), :], x[:, bass.ds(it * W1, W1), :]).then_inc(s["x_in"], 16)
                        sp.dma_start(CX[:, bass.ds(it * W1, W1), :], ctx[:, bass.ds(it * W1, W1), :]).then_inc(s["x_in"], 16)

                    def store_rows(it):
                        for p in range(W1):
                            sp.wait_ge(s["row_ready"], it * W1 + p + 1)
                            sp.dma_start(rows1[bass.ds((it * W1 + p) * P, P), :], row[:, p, :]).then_inc(row_out[p], 16)

                    load_batches(0)
                    for p in range(W1):
                        sp.sem_inc(row_out[p], 16)
                    for r in range(R2):
                        sp.dma_start(wgu_sb[r][:, :, :, :], w_gu[:, 4 * r:4 * r + 4, :, :]).then_inc(experts_in[r], 16)
                        sp.dma_start(wd_sb[r][:, :, :, :], w_d[:, 4 * r:4 * r + 4, :, :]).then_inc(experts_in[r], 16)
                    with sp.Fori(0, NIT - 1) as it:
                        sp.wait_ge(s["x_in"], it * 32 + 32)
                        load_batches(it + 1)
                        store_rows(it)
                    sp.wait_ge(zero_made, 2)
                    sp.dma_start(rows1[TOK:TOK + 1, :], zrow[0:1, :]).then_inc(zero_out, 16)
                    sp.dma_start(youts[SLOTS2:SLOTS2 + 1, :], zrow[0:1, 0:H]).then_inc(zero_out, 16)
                    for c in range(SLOTS2 // P):
                        sp.dma_start(rows2[c * P:(c + 1) * P, :], zrow[:, 0:H]).then_inc(zero_out, 16)
                    store_rows(NIT - 1)
                    sp.wait_ge(zero_out, 16 * (2 + SLOTS2 // P))
                    for p in range(W1):
                        sp.wait_ge(row_out[p], 16 * (NIT + 1))

                @block.gpsimd
                def _(pool):
                    gp, did = nc.gpsimd, Count()
                    gp.memset(zrow[:, :], 0.0).then_inc(zero_made, 1)
                    gp.iota(iota_e[:, :], [[1, E1]], base=0, channel_multiplier=0, allow_small_or_imprecise_dtypes=True).then_inc(pool_done, did.one())
                    pool.wait_ge(pool_done, did.n)
                    gp.iota(iota_c[:, :], [[1, CAP1]], base=0, channel_multiplier=0, allow_small_or_imprecise_dtypes=True).then_inc(pool_done, did.one())
                    pool.wait_ge(pool_done, did.n)
                    gp.memset(mean64[:, :], 1.0 / LAT).then_inc(pool_done, did.one())
                    pool.wait_ge(pool_done, did.n)
                    gp.memset(ones_b[:, :], 1.0).then_inc(pool_done, did.one())
                    pool.wait_ge(pool_done, did.n)
                    pool.sem_inc(zero_made, 1)
                    pool.sem_inc(pool_done, -did.restart())

                @block.scalar
                def _(act):
                    sc = nc.scalar
                    act.wait_ge(consts_in, 16 * 17)
                    sc.activation(tanh_g[:, :], tanh_g[:, :], ACT.Tanh).then_inc(tanh_made, 1)
                    with act.Fori(0, NIT) as it:
                        for p in range(W1):
                            act.wait_ge(s["pt_ready"], it * W1 + p + 1)
                            sc.activation(th[p][:, 0:H], bank_a[p][0:LAT, 0:H], ACT.Identity, bias=phb[:, 0:1])
                            sc.activation(th[p][:, H:2 * H], bank_a[p][0:LAT, H:2 * H], ACT.Identity, bias=thb[:, 0:1]).then_inc(s["pt_sb"], 1)
                        for p in range(W1):
                            act.wait_ge(s["nm_ready"], it * W1 + p + 1)
                            for c in range(2):
                                last = sc.activation(pr[p][:, c, :], bank_a[p][:, c * H:(c + 1) * H], ACT.Exp,
                                                     bias=nmax[:, p, c:c + 1], accum_out=psm[:, p, c:c + 1])
                            last.then_inc(s["p_ready"], 1)
                        for p in range(W1):
                            act.wait_ge(s["ptr_ready"], it * W1 + p + 1)
                            sc.activation(prT[p][:, :, :], bank_b[p][:, :], ACT.Copy).then_inc(s["prT_sb"], 1)
                        for p in range(W1):
                            act.wait_ge(s["hn_ready"], it * W1 + p + 1)
                            sc.activation(hh[p][:, :], hh[p][:, :], ACT.Relu).then_inc(s["h_ready"], 1)
                        for p in range(W1):
                            act.wait_ge(s["xt_ready"], it * W1 + p + 1)
                            sc.activation(xT[p][:, :, :], bank_a[p][:, 0:H], ACT.Copy).then_inc(s["xT_sb"], 1)
                        for p in range(W1):
                            act.wait_ge(s["lnm_ready"], it * W1 + p + 1)
                            sc.activation(ex[:, p, :], bank_b[p][:, 448:512], ACT.Exp, bias=nmax[:, p, 0:1],
                                          accum_out=psm[:, p, 0:1]).then_inc(s["e_ready"], 1)
                        for p in range(W1):
                            act.wait_ge(s["gu_ready"], it * W1 + p + 1)
                            sc.activation(sg[p][:, 0:2, :], bank_a[p][:, 0:256], ACT.Silu)
                            sc.activation(sg[p][0:96, 2, :], bank_a[p][0:96, 256:384], ACT.Silu).then_inc(s["sg_ready"], 1)

                @block.vector
                def _(dve):
                    v, did = nc.vector, Count()

                    def norm_stats(src, p):
                        v.bn_stats(st[:, p, :], src).then_inc(dve_done, did.one())
                        dve.wait_ge(dve_done, did.n)
                        v.bn_aggr(mv[:, p, :], st[:, p, :]).then_inc(dve_done, did.one())
                        dve.wait_ge(dve_done, did.n)
                        v.tensor_scalar(mvv[:, p:p + 1], mv[:, p, 1:2], EPS, None, ALU.add).then_inc(dve_done, did.one())

                    v.memset(idx1f[:, :], 0.0).then_inc(dve_done, did.one())
                    dve.wait_ge(dve_done, did.n)
                    v.memset(cumc[:, :, :], 2.0 * CAP1).then_inc(dve_done, did.one())
                    dve.wait_ge(dve_done, did.n)
                    v.memset(before[:, 0, :], 0.0).then_inc(dve_done, did.one())
                    dve.wait_ge(dve_done, did.n)
                    for _ in range(W1):
                        dve.sem_inc(s["banks_free"], 1)
                    dve.wait_ge(zero_made, 2)
                    dve.wait_ge(tanh_made, 1)
                    dve.wait_ge(consts_in, 16 * 17)
                    dve.wait_ge(dve_done, did.n)
                    dve.sem_inc(dve_done, -did.restart())

                    def norm_x(it):
                        dve.wait_ge(s["x_in"], it * 32 + 32)
                        for p in range(W1):
                            norm_stats(X[:, bass.ds(it * W1 + p, 1), :], p)
                        dve.wait_ge(dve_done, did.n)
                        rsqrt(nc, dve, dve_done, did, rstd[:, :], mvv[:, :], rs_h[:, :], rs_t[:, :])
                        for p in range(W1):
                            v.tensor_scalar(xn[p][:, :], X[:, bass.ds(it * W1 + p, 1), :], mv[:, p, 0:1], rstd[:, p:p + 1],
                                            ALU.subtract, ALU.mult).then_inc(s["xn_ready"], 1)

                    def slots_of(it, p):
                        v.tensor_tensor(G[p][:, :, :], cumc[:, p, :].unsqueeze(2).to_broadcast([P, E1, CAP1]),
                                        iota_c[:, :].unsqueeze(1).to_broadcast([P, E1, CAP1]), ALU.is_le).then_inc(s["G_ready"], 1)

                    def add_slots(it, p):
                        dve.wait_ge(s["ix_ready"], it * W1 + p + 1)
                        dve.wait_ge(dve_done, did.n)
                        v.tensor_tensor(idx1f[:, :], idx1f[:, :], bank_b[p][:, 384:400], ALU.add).then_inc(dve_done, did.one())

                    def step(it, more):
                        for p in range(W1):
                            dve.wait_ge(s["gxp_ready"], it * W1 + p + 1)
                            v.tensor_tensor(gx[p][:, :, :], bank_b[p][:, 0:2 * LAT].rearrange("p (c l) -> p c l", c=2), gb[:, :, :], ALU.add).then_inc(s["gx_sb"], 1)
                            slots_of(it, p)
                        for p in range(W1):
                            dve.wait_ge(s["sc_ready"], it * W1 + p + 1)
                            v.tensor_reduce(nmax[:, p, :], bank_a[p][:, :].rearrange("p (c t) -> p c t", c=2), axis=AX.X, op=ALU.max, negate=True).then_inc(s["nm_ready"], 1)
                            add_slots(it, p)
                        for p in range(W1):
                            dve.wait_ge(s["p_ready"], it * W1 + p + 1)
                            v.reciprocal(rin[:, p, :], psm[:, p, :]).then_inc(dve_done, did.one())
                            dve.wait_ge(dve_done, did.n)
                            for c in range(2):
                                v.tensor_scalar(pr[p][:, c, :], pr[p][:, c, :], rin[:, p, c:c + 1], None, ALU.mult).then_inc(dve_done, did.one())
                            dve.wait_ge(dve_done, did.n)
                            dve.sem_inc(s["pn_ready"], 1)
                        if more:
                            norm_x(it + 1)
                        for p in range(W1):
                            dve.wait_ge(s["tx_ready"], it * W1 + p + 1)
                            v.bn_stats(st[0:LAT, p, :], bank_a[p][0:LAT, 0:H]).then_inc(dve_done, did.one())
                            dve.wait_ge(dve_done, did.n)
                            v.bn_aggr(st2[:, p, :], st[0:LAT, p, :]).then_inc(dve_done, did.one())
                            dve.wait_ge(dve_done, did.n)
                            v.scalar_tensor_tensor(st2[:, p, 1:2], st2[:, p, 0:1], st2[:, p, 0:1], st2[:, p, 1:2], ALU.mult, ALU.add).then_inc(dve_done, did.one())
                            dve.wait_ge(dve_done, did.n)
                            dve.sem_inc(s["st2_ready"], 1)
                        for p in range(W1):
                            dve.wait_ge(s["mu_ready"], it * W1 + p + 1)
                            v.tensor_copy(mv[0:LAT, p, :], bank_a[p][0:LAT, H:H + 2]).then_inc(dve_done, did.one())
                        dve.wait_ge(dve_done, did.n)
                        v.tensor_tensor(mvv[0:LAT, :], mv[0:LAT, :, 0], mv[0:LAT, :, 0], ALU.mult).then_inc(dve_done, did.one())
                        dve.wait_ge(dve_done, did.n)
                        v.scalar_tensor_tensor(mvv[0:LAT, :], mv[0:LAT, :, 1], EPS, mvv[0:LAT, :], ALU.add, ALU.subtract).then_inc(dve_done, did.one())
                        dve.wait_ge(dve_done, did.n)
                        rsqrt(nc, dve, dve_done, did, rstd[0:LAT, :], mvv[0:LAT, :], rs_h[0:LAT, :], rs_t[0:LAT, :])
                        for p in range(W1):
                            v.scalar_tensor_tensor(hh[p][:, :], bank_a[p][0:LAT, 0:H], mv[0:LAT, p, 0:1], gam[:, :], ALU.subtract, ALU.mult).then_inc(dve_done, did.one())
                            if p:
                                v.scalar_tensor_tensor(hh[p - 1][:, :], hh[p - 1][:, :], rstd[0:LAT, p - 1:p], bet[:, :], ALU.mult, ALU.add).then_inc(s["hn_ready"], 1)
                            dve.wait_ge(dve_done, did.n)
                        v.scalar_tensor_tensor(hh[W1 - 1][:, :], hh[W1 - 1][:, :], rstd[0:LAT, W1 - 1:W1], bet[:, :], ALU.mult, ALU.add).then_inc(s["hn_ready"], 1)
                        for p in range(W1):
                            dve.wait_ge(s["w_ready"], it * W1 + p + 1)
                            xb = X[:, bass.ds(it * W1 + p, 1), :]
                            v.scalar_tensor_tensor(wx[p % 2][:, :], bank_b[p][:, 0:H], ob[:, 0:1], CX[:, bass.ds(it * W1 + p, 1), :].rearrange("p a h -> p (a h)"), ALU.add, ALU.add).then_inc(dve_done, did.one())
                            dve.wait_ge(dve_done, did.n)
                            v.scalar_tensor_tensor(xb.rearrange("p a h -> p (a h)"), wx[p % 2][:, :], tanh_g[:, 0:1], xb.rearrange("p a h -> p (a h)"), ALU.mult, ALU.add).then_inc(dve_done, did.one())
                            dve.wait_ge(dve_done, did.n)
                            norm_stats(xb, p)
                        dve.wait_ge(dve_done, did.n)
                        rsqrt(nc, dve, dve_done, did, rstd[:, :], mvv[:, :], rs_h[:, :], rs_t[:, :])
                        for p in range(W1):
                            dve.wait_ge(row_out[p], it * 16 + 16)
                            v.tensor_scalar(row[:, p, 0:H], X[:, bass.ds(it * W1 + p, 1), :], mv[:, p, 0:1], rstd[:, p:p + 1],
                                                    ALU.subtract, ALU.mult).then_inc(s["xn2_ready"], 1)
                        for p in range(W1):
                            dve.wait_ge(s["lg_ready"], it * W1 + p + 1)
                            v.tensor_reduce(nmax[:, p, 0:1], bank_b[p][:, 448:512], axis=AX.X, op=ALU.max, negate=True).then_inc(s["lnm_ready"], 1)
                        for p in range(0, W1, 2):
                            two = slice(p, p + 2)
                            dve.wait_ge(s["e_ready"], it * W1 + p + 2)
                            v.reciprocal(rin[:, two, 0], psm[:, two, 0]).then_inc(dve_done, did.one())
                            dve.wait_ge(dve_done, did.n)
                            v.tensor_tensor(ex[:, two, :], ex[:, two, :], rin[:, two, 0:1].to_broadcast([P, 2, E1]), ALU.mult).then_inc(dve_done, did.one())
                            dve.wait_ge(dve_done, did.n)
                            v.max(t8[:, p, :], ex[:, p, :]).then_inc(dve_done, did.one())
                            v.max(t8[:, p + 1, :], ex[:, p + 1, :]).then_inc(dve_done, did.one())
                            dve.wait_ge(dve_done, did.n)
                            v.max_index(i8[:, p, :], t8[:, p, :], ex[:, p, :]).then_inc(dve_done, did.one())
                            v.max_index(i8[:, p + 1, :], t8[:, p + 1, :], ex[:, p + 1, :]).then_inc(dve_done, did.one())
                            dve.wait_ge(dve_done, did.n)
                            v.tensor_copy(i8f[:, two, :], i8[:, two, :]).then_inc(dve_done, did.one())
                            dve.wait_ge(dve_done, did.n)
                            for q in range(2):
                                v.tensor_tensor(eq[:, q, :, :], iota_e[:, :].unsqueeze(1).to_broadcast([P, K1, E1]),
                                                i8f[:, p + q, 0:K1].unsqueeze(2).to_broadcast([P, K1, E1]), ALU.is_equal).then_inc(dve_done, did.one())
                            dve.wait_ge(dve_done, did.n)
                            v.tensor_reduce(mf[:, :, :], eq[:, :, :, :].rearrange("p q k e -> p q e k"), axis=AX.X, op=ALU.add).then_inc(dve_done, did.one())
                            dve.wait_ge(dve_done, did.n)
                            v.tensor_tensor(row[:, two, H:ROW], ex[:, two, :], mf[:, :, :], ALU.mult).then_inc(dve_done, did.one())
                            v.tensor_copy(mb[:, two, :], mf[:, :, :]).then_inc(dve_done, did.one())
                            dve.wait_ge(dve_done, did.n)
                            for q in range(p, p + 2):
                                v.tensor_tensor(before[:, q + 1, :], before[:, q, :], mb[:, q, :], ALU.add).then_inc(dve_done, did.one())
                                dve.wait_ge(dve_done, did.n)
                            dve.sem_inc(s["mb_ready"], 2)
                            dve.sem_inc(s["row_ready"], 2)
                        for p in range(W1):
                            dve.wait_ge(s["sg_ready"], it * W1 + p + 1)
                            v.tensor_tensor(sg[p][:, 0:2, :], sg[p][:, 0:2, :], bank_b[p][:, 0:256].rearrange("p (c t) -> p c t", c=2), ALU.mult).then_inc(dve_done, did.one())
                            v.tensor_tensor(sg[p][0:96, 2, :], sg[p][0:96, 2, :], bank_b[p][0:96, 256:384], ALU.mult).then_inc(dve_done, did.one())
                            dve.wait_ge(dve_done, did.n)
                            dve.sem_inc(s["hs_ready"], 1)
                        for p in range(W1):
                            dve.wait_ge(s["cum_ready"], it * W1 + p + 1)
                            v.tensor_scalar(cumc[:, p, :], bank_b[p][:, 448:512], 2.0 * CAP1, None, ALU.min).then_inc(dve_done, did.one())
                        v.tensor_copy(before[:, 0, :], before[:, W1, :]).then_inc(dve_done, did.one())
                        for p in range(W1):
                            dve.wait_ge(s["dn_ready"], it * W1 + p + 1)
                            xb = X[:, bass.ds(it * W1 + p, 1), :].rearrange("p a h -> p (a h)")
                            v.scalar_tensor_tensor(xb, bank_a[p][:, 0:H], tanh_g[:, 2:3], xb, ALU.mult, ALU.add).then_inc(dve_done, did.one())
                            dve.wait_ge(dve_done, did.n)
                            dve.sem_inc(s["banks_free"], 1)
                        dve.wait_ge(dve_done, did.n)
                        dve.sem_inc(dve_done, -did.restart())

                    norm_x(0)
                    dve.wait_ge(dve_done, did.n)
                    dve.sem_inc(dve_done, -did.restart())
                    with dve.Fori(0, NIT - 1) as it:
                        step(it, True)
                    step(NIT - 1, False)
                    for p in range(W1):
                        slots_of(NIT, p)
                    for p in range(W1):
                        add_slots(NIT, p)
                    dve.wait_ge(dve_done, did.n)
                    v.tensor_copy(idx1[:, :], idx1f[:, :]).then_inc(dve_done, did.one())
                    dve.wait_ge(dve_done, did.n)
                    dve.wait_ge(dve_done, did.n)
                    dve.sem_inc(dve_done, -did.restart())

                @block.tensor
                def _(pe):
                    t = nc.tensor
                    pe.wait_ge(consts_in, 16 * 17)
                    pe.wait_ge(zero_made, 2)

                    def slots(it, p):
                        pe.wait_ge(s["G_ready"], it * W1 + p + 1)
                        gf = G[p][:, :, :].rearrange("p e c -> p (e c)")
                        for j in range(SLOTS1 // P):
                            last = t.matmul(bank_b[p][:, 384 + j:385 + j], gf[:, j * P:(j + 1) * P], ones_b[:, 0:1], start=True, stop=True)
                        last.then_inc(s["ix_ready"], 1)

                    with pe.Fori(0, NIT) as it:
                        for p in range(W1):
                            pe.wait_ge(s["banks_free"], it * W1 + p + 1)
                            pe.wait_ge(s["xn_ready"], it * W1 + p + 1)
                            t.matmul(bank_a[p][0:LAT, 0:H], phw[:, :], xn[p][:, :], start=True, stop=True)
                            t.matmul(bank_a[p][0:LAT, H:2 * H], thw[:, :], CX[:, bass.ds(it * W1 + p, 1), :].rearrange("p a h -> p (a h)"),
                                     start=True, stop=True).then_inc(s["pt_ready"], 1)
                            for c in range(2):
                                last = t.matmul(bank_b[p][:, c * LAT:(c + 1) * LAT], xn[p][:, c * P:(c + 1) * P], gw[:, :], start=True, stop=True)
                            last.then_inc(s["gxp_ready"], 1)
                        for p in range(W1):
                            pe.wait_ge(s["pt_sb"], it * W1 + p + 1)
                            for c in range(2):
                                last = t.matmul(bank_a[p][:, c * H:(c + 1) * H], th[p][:, H + c * P:H + (c + 1) * P], th[p][:, 0:H], start=True, stop=True)
                            last.then_inc(s["sc_ready"], 1)
                        for p in range(W1):
                            slots(it, p)
                        for p in range(W1):
                            pe.wait_ge(s["gx_sb"], it * W1 + p + 1)
                            pe.wait_ge(s["pn_ready"], it * W1 + p + 1)
                            for c in range(2):
                                for tc in range(2):
                                    last = t.transpose(bank_b[p][:, c * H + tc * P:c * H + (tc + 1) * P], pr[p][:, tc, c * P:(c + 1) * P], idn[:, :])
                            last.then_inc(s["ptr_ready"], 1)
                        for p in range(W1):
                            pe.wait_ge(s["prT_sb"], it * W1 + p + 1)
                            for c in range(2):
                                last = t.matmul(bank_a[p][0:LAT, 0:H], gx[p][:, c, :], prT[p][:, c, :], start=c == 0, stop=c == 1)
                            last.then_inc(s["tx_ready"], 1)
                        for p in range(W1):
                            pe.wait_ge(s["st2_ready"], it * W1 + p + 1)
                            pe.sem_inc(pe_passed, 1)
                            t.matmul(bank_a[p][0:LAT, H:H + 2], mean64[:, :], st2[:, p, :], start=True, stop=True).then_inc(s["mu_ready"], 1)
                        for p in range(W1):
                            pe.wait_ge(s["h_ready"], it * W1 + p + 1)
                            t.matmul(bank_b[p][:, 0:H], ow[:, :], hh[p][:, :], start=True, stop=True).then_inc(s["w_ready"], 1)
                        for p in range(W1):
                            pe.wait_ge(s["xn2_ready"], it * W1 + p + 1)
                            for c in range(HC):
                                last = t.transpose(bank_a[p][:, c * P:(c + 1) * P], row[:, p, c * P:(c + 1) * P], idn[:, :])
                            last.then_inc(s["xt_ready"], 1)
                        for p in range(W1):
                            pe.wait_ge(s["xT_sb"], it * W1 + p + 1)
                            for c in range(HC):
                                last = t.matmul(bank_b[p][:, 448:512], xT[p][:, c, :], g1w[:, c, :], start=c == 0, stop=c == HC - 1)
                            last.then_inc(s["lg_ready"], 1)
                        for k, banks in enumerate((bank_a, bank_b)):
                            for p in range(W1):
                                if k == 1:
                                    pe.wait_ge(s["e_ready"], it * W1 + p + 1)
                                for j, (o, m) in enumerate(ISC):
                                    for c in range(HC):
                                        last = t.matmul(banks[p][0:m, j * P:(j + 1) * P], sgu[:, c, k * IS + o:k * IS + o + m], xT[p][:, c, :],
                                                        start=c == 0, stop=c == HC - 1)
                                if k == 1:
                                    last.then_inc(s["gu_ready"], 1)
                        for p in range(W1):
                            pe.wait_ge(s["hs_ready"], it * W1 + p + 1)
                            pe.wait_ge(s["mb_ready"], it * W1 + p + 1)
                            t.matmul(bank_b[p][:, 448:512], upr[:, :], mb[:, p, :], start=True, stop=False)
                            t.matmul(bank_b[p][:, 448:512], ones_b[:, :], before[:, p, :], start=False, stop=True).then_inc(s["cum_ready"], 1)
                            for j, (o, m) in enumerate(ISC):
                                last = t.matmul(bank_a[p][:, 0:H], sg[p][0:m, j, :], sdn[0:m, j, :], start=j == 0, stop=j == 2)
                            last.then_inc(s["dn_ready"], 1)
                    for p in range(W1):
                        slots(NIT, p)

        N2 = SLOTS1 // P
        with ExitStack() as ph:
            qrt = sb("qrt", [P, 4], where=ph)
            idxc = [sb(f"idxc{q}", [P, 1], U32, where=ph) for q in range(2)]
            xs = [sb(f"xs{q}", [P, ROW], where=ph) for q in range(2)]
            xsT = [sb(f"xsT{q}", [P, HC, P], where=ph) for q in range(2)]
            hm = [sb(f"hm{q}", [P, I1], where=ph) for q in range(2)]
            hT = [sb(f"hT{q}", [I1H, 2, P], where=ph) for q in range(2)]
            w4 = sb("w4", [P, 2, 4], where=ph)
            ws = sb("ws", [P, 2], where=ph)
            yy = [sb(f"yy{q}", [P, H], where=ph) for q in range(2)]
            slots_in = [sem(f"slots_in{q}") for q in range(2)]
            names = ["slots_free", "st_ready", "xsT_sb", "ug_ready", "silu_ready", "hm_ready", "ht_ready", "hT_sb", "y_ready", "y_taken"]
            s = {n: sem("e_" + n) for n in names}
            with nc.Block() as block:
                @block.sync
                def _(sp):
                    sp.dma_start(qrt[:, :], quarter).then_inc(consts_in, 16)
                    with sp.Fori(1, N2 // R2) as it:
                        for r in range(R2):
                            sp.wait_ge(experts_free, (it - 1) * R2 + r + 1)
                            sp.dma_start(wgu_sb[r][:, :, :, :], w_gu[:, bass.ds((it * R2 + r) * 4, 4), :, :]).then_inc(experts_in[r], 16)
                            sp.dma_start(wd_sb[r][:, :, :, :], w_d[:, bass.ds((it * R2 + r) * 4, 4), :, :]).then_inc(experts_in[r], 16)

                @block.gpsimd
                def _(pool):
                    gp, did = nc.gpsimd, Count()
                    for _ in range(2):
                        pool.sem_inc(s["slots_free"], 1)
                    with pool.Fori(0, N2 // R2) as it:
                        for r in range(R2):
                            q = r % 2
                            pool.wait_ge(s["slots_free"], it * R2 + r + 1)
                            gp.tensor_copy(idxc[q][:, :], idx1[:, bass.ds(it * R2 + r, 1)]).then_inc(pool_done, did.one())
                            pool.wait_ge(pool_done, did.n)
                            pool.indirect_dma_start(xs[q][:, :], None, rows1, bass.IndirectOffsetOnAxis(ap=idxc[q][:, :], axis=0),
                                                    bounds_check=TOK, oob_is_err=False).then_inc(slots_in[q], 16)
                        pool.wait_ge(pool_done, did.n)
                        pool.sem_inc(pool_done, -did.restart())

                @block.scalar
                def _(act):
                    sc = nc.scalar
                    with act.Fori(0, N2 // R2) as it:
                        for r in range(R2):
                            q, n = r % 2, it * R2 + r + 1
                            act.wait_ge(s["st_ready"], n)
                            sc.activation(xsT[q][:, :, :], pb[q][:, 0:H], ACT.Copy).then_inc(s["xsT_sb"], 1)
                            act.wait_ge(s["ug_ready"], n)
                            sc.activation(hm[q][:, :], pb[2 + q][:, 0:I1], ACT.Silu).then_inc(s["silu_ready"], 1)
                            act.wait_ge(s["ht_ready"], n)
                            sc.activation(hT[q][:, :, :], pb[4 + q][0:I1H, 0:2 * P], ACT.Copy).then_inc(s["hT_sb"], 1)

                @block.vector
                def _(dve):
                    v, did = nc.vector, Count()
                    dve.wait_ge(consts_in, 16 * 18)
                    with dve.Fori(0, N2 // R2) as it:
                        for r in range(R2):
                            q, n = r % 2, it * R2 + r + 1
                            dve.wait_ge(slots_in[q], it * 32 + (r // 2 + 1) * 16)
                            v.tensor_tensor(w4[:, q, :], xs[q][:, bass.ds(H + (it * R2 + r) * 4, 4)], qrt[:, :], ALU.mult).then_inc(dve_done, did.one())
                            dve.wait_ge(dve_done, did.n)
                            v.tensor_reduce(ws[:, q:q + 1], w4[:, q, :], axis=AX.X, op=ALU.add).then_inc(dve_done, did.one())
                            dve.wait_ge(dve_done, did.n)
                            dve.wait_ge(s["xsT_sb"], n)
                            dve.sem_inc(s["slots_free"], 1)
                            dve.wait_ge(s["silu_ready"], n)
                            v.tensor_tensor(hm[q][:, :], hm[q][:, :], pb[2 + q][:, I1:2 * I1], ALU.mult).then_inc(dve_done, did.one())
                            dve.wait_ge(dve_done, did.n)
                            dve.sem_inc(s["hm_ready"], 1)
                            dve.wait_ge(s["y_ready"], n)
                            v.tensor_scalar(yy[q][:, :], pb[6 + q][:, 0:H], ws[:, q:q + 1], None, ALU.mult).then_inc(dve_done, did.one())
                            dve.wait_ge(dve_done, did.n)
                            for k in range(3):
                                part = parts[:, bass.ds(it * R2 + r, 1), k, :].rearrange("p a h -> p (a h)")
                                v.tensor_copy(part, yy[q][:, :]).then_inc(dve_done, did.one())
                                dve.wait_ge(dve_done, did.n)
                                if k < 2:
                                    v.tensor_tensor(yy[q][:, :], yy[q][:, :], part, ALU.subtract).then_inc(dve_done, did.one())
                                    dve.wait_ge(dve_done, did.n)
                            dve.sem_inc(s["y_taken"], 1)
                        dve.wait_ge(dve_done, did.n)
                        dve.sem_inc(dve_done, -did.restart())

                @block.tensor
                def _(pe):
                    t = nc.tensor
                    with pe.Fori(0, N2 // R2) as it:
                        for r in range(R2):
                            q, n = r % 2, it * R2 + r + 1
                            pe.wait_ge(slots_in[q], it * 32 + (r // 2 + 1) * 16)
                            for c in range(HC):
                                last = t.transpose(pb[q][:, c * P:(c + 1) * P], xs[q][:, c * P:(c + 1) * P], idn[:, :])
                            last.then_inc(s["st_ready"], 1)
                            pe.wait_ge(experts_in[r], it * 32 + 32)
                            pe.wait_ge(s["xsT_sb"], n)
                            for c in range(HC):
                                for e in range(4):
                                    last = t.matmul(pb[2 + q][32 * e:32 * e + 32, 0:2 * I1], xsT[q][:, c, 32 * e:32 * e + 32],
                                                    wgu_sb[r][:, e, c, :], start=c == 0, stop=c == HC - 1)
                            last.then_inc(s["ug_ready"], 1)
                            pe.wait_ge(s["hm_ready"], n)
                            for c in range(2):
                                last = t.transpose(pb[4 + q][0:I1H, c * P:(c + 1) * P], hm[q][:, c * I1H:(c + 1) * I1H], idn[:, :])
                            last.then_inc(s["ht_ready"], 1)
                            pe.wait_ge(s["hT_sb"], n)
                            for c in range(2):
                                for e in range(4):
                                    last = t.matmul(pb[6 + q][32 * e:32 * e + 32, 0:H], hT[q][:, c, 32 * e:32 * e + 32],
                                                    wd_sb[r][:, e, c, :], start=c == 0, stop=c == 1)
                            last.then_inc(s["y_ready"], 1)
                            pe.wait_ge(s["y_taken"], n)
                            pe.sem_inc(experts_free, 1)
        phase12.close()
        phase34 = ExitStack()
        w1s = [sb(f"w1s{q}", [P, HC, H], where=phase34) for q in range(2)]
        w2s = [sb(f"w2s{q}", [P, HC, H], where=phase34) for q in range(2)]
        w1_in, w2_in = [sem(f"w1_in{q}") for q in range(2)], [sem(f"w2_in{q}") for q in range(2)]

        with ExitStack() as ph:
            wq = sb("wq", [P, HC, 3 * H], where=ph)
            wo_sb = sb("wo_sb", [P, HC, H], where=ph)
            g2w = sb("g2w", [P, HC, E2], where=ph)
            cosv, sinv = (sb(n, [P, HD], where=ph) for n in ("cosv", "sinv"))
            grp = sb("grp", [P, 4], where=ph)
            hg = sb("hg", [P, NH], where=ph)
            iota_t = sb("iota_t", [P, P], where=ph)
            onehot = sb("onehot", [P, N2, P], BF16, where=ph)
            cT = [sb(f"cT{p}", [P, HC, P], where=ph) for p in range(2)]
            mk = [sb(f"mk{p}", [P, P], where=ph) for p in range(2)]
            xn = sb("xc", [P, H], where=ph)
            xT = sb("xcT", [P, H + E2], where=ph)
            qk = sb("qk", [P, 2, NH, HD], where=ph)
            rot = sb("rot", [P, 2, NH, HD], where=ph)
            ak = sb("ak", [P, H], where=ph)
            kT = sb("kT", [P, 2, HC, P], where=ph)
            vv = [[sb(f"vv{p}{a}", [P, NH, 32], where=ph) for a in range(2)] for p in range(2)]
            qT = [sb(f"qT{p}", [P, HC, P], where=ph) for p in range(2)]
            kb = [sb(f"kb{a}", [P, HC, 4, P], where=ph) for a in range(2)]
            kd = [[sb(f"kd{p}{a}", [P, HC, 16, P], where=ph) for a in range(2)] for p in range(2)]
            pr = [sb(f"pc{i}", [P, 4, P], where=ph) for i in range(3)] + [sb("pc3", [P, 4, P], where=ph)]
            prT = [sb(f"pcT{i}", [P, 4, P], where=ph) for i in range(2)]
            ots = [sb(f"ots{i}", [P, 4, P], where=ph) for i in range(2)]
            nm = sb("nm", [P, 4, 4], where=ph)
            oa = sb("oa", [P, 2, NH, HD + 1], where=ph)
            rr = sb("rr", [P, 2, NH], where=ph)
            at = sb("at", [P, NH, HD], where=ph)
            at2 = sb("at2", [P, NH, HD], where=ph)
            atT = sb("atT", [P, HC, P], where=ph)
            xn4 = [sb(f"xn4{p}", [P, H], where=ph) for p in range(2)]
            x4T = sb("x4T", [P, HC, P], where=ph)
            st = sb("stc", [P, 2, 6], where=ph)
            mv = sb("mvc", [P, 2, 2], where=ph)
            mvv, rstd = sb("mvvc", [P, 2], where=ph), sb("rstdc", [P, 2], where=ph)
            t8 = sb("t8c", [P, 8], where=ph)
            i8 = sb("i8c", [P, 8], U32, where=ph)
            sm = sb("sm", [P, 16], where=ph)
            e8, m8, c8, pe8, n8 = (sb(n, [P, E2], where=ph) for n in ("e8", "m8", "c8", "pe8", "n8"))
            m8b = sb("m8b", [P, E2], BF16, where=ph)
            before2 = sb("before2", [P, E2], BF16, where=ph)
            sl = [sb(f"sl{p}", [P, 1], U32, where=ph) for p in range(2)]
            names = ["one_ready", "comb_ready", "comb_taken", "xc_ready", "xcT_ready", "xcT_sb", "qk_ready", "qk_sb", "ka_ready",
                     "ka_sb", "v_ready", "v_sb", "rope_ready", "qkT_ready", "qkT_sb", "kb_ready", "kd_zero", "at_ready", "aT_ready", "aT_sb",
                     "wo_ready", "wo_taken", "x4_ready", "x4T_ready", "x4T_sb", "lg_ready", "ln_ready", "e8_ready", "m_ready",
                     "sl_ready", "cin_free", "x4_free", "buffers_made",
                     "norm_done", "end_done", "att_done",
                     "sc_ready", "nm_ready", "p_ready", "tr_ready", "evac_main", "evac_ad", "pv_done",
                     "ot_ready", "ot_sb", "ob_ready", "o_taken"]
            s = {n: sem("c_" + n) for n in names}
            ctx_in = [sem(f"ctx_in{p}") for p in range(2)]
            xn4_out = [sem(f"xn4_out{p}") for p in range(2)]
            kd_in = [sem(f"kd_in{p}") for p in range(2)]
            score = pb[0:4]
            trp, otb, mb_ = pb[4], pb[5:7], pb[7]
            U, NM = 16, 8
            CONSTS3 = 16 * 25

            FIRST = [(0, True, True, False, False), (1, True, True, True, False)]
            LASTS = [(14, True, False, True, True), (15, False, False, True, True)]
            ENDS = [(16, False, False, True, True), (17, False, False, False, True)]
            LOOP = (2, 14, 2)

            with nc.Block() as block:
                @block.sync
                def _(sp):
                    for dst, src in ((wq, wqkv), (wo_sb, wo), (g2w, gate2_w)):
                        sp.dma_start(dst[:, :, :], src).then_inc(consts_in, 16)
                    for dst, src in ((cosv, cos), (sinv, sin), (grp, group)):
                        sp.dma_start(dst[:, :], src).then_inc(consts_in, 16)
                    sp.dma_start(hg[:, :], hgate.rearrange("(a n) -> a n", a=1).to_broadcast([P, NH])).then_inc(consts_in, 16)
                    for p in range(2):
                        sp.sem_inc(s["cin_free"], 1)

                    def load(b, p):
                        sp.wait_ge(s["cin_free"], b + 1)
                        sp.dma_start(cT[p][:, :, :], ctxT[bass.ds(b, 1), :, :, :].rearrange("a p c t -> p (a c) t")).then_inc(ctx_in[p], 16)
                        sp.dma_start(mk[p][:, :], mask[bass.ds(b, 1), :, :].rearrange("a p k -> p (a k)")).then_inc(ctx_in[p], 16)

                    def spread_keys(b, p):
                        for a in (1, 0):
                            sp.wait_ge(s["kb_ready"], b * 2 + 2 - a)
                            for g in range(4):
                                sp.dma_start(kd[p][a][32 * g:32 * g + 32, :, 4 * g:4 * g + 4, :], kb[a][32 * g:32 * g + 32, :, :, :]).then_inc(kd_in[p], 16)

                    load(0, 0)
                    load(1, 1)
                    for q in range(2):
                        sp.dma_start(w1s[q][:, :, :], w1[:, q, :, :]).then_inc(w1_in[q], 16)
                        sp.dma_start(w2s[q][:, :, :], w2[:, q, :, :]).then_inc(w2_in[q], 16)
                    sp.wait_ge(s["kd_zero"], 4)
                    spread_keys(0, 0)
                    with sp.Fori(1, B // 2) as it:
                        load(it * 2, 0)
                        spread_keys(it * 2 - 1, 1)
                        load(it * 2 + 1, 1)
                        spread_keys(it * 2, 0)
                    spread_keys(B - 1, 1)

                @block.gpsimd
                def _(pool):
                    gp, did = nc.gpsimd, Count()
                    gp.iota(iota_t[:, :], [[1, P]], base=0, channel_multiplier=0, allow_small_or_imprecise_dtypes=True).then_inc(pool_done, did.one())
                    for p in range(2):
                        for a in range(2):
                            gp.memset(vv[p][a][:, :, :], 0.0).then_inc(pool_done, did.one())
                    pool.wait_ge(pool_done, did.n)
                    for p in range(2):
                        for a in range(2):
                            gp.memset(vv[p][a][:, :, HD:HD + 1], 1.0).then_inc(pool_done, did.one())
                        pool.sem_inc(s["x4_free"], 1)
                    pool.wait_ge(pool_done, did.n)
                    pool.sem_inc(s["buffers_made"], 1)
                    pool.wait_ge(consts_in, CONSTS3)

                    def which_slots():
                        for j in range(N2):
                            gp.tensor_scalar(onehot[:, j, :], iota_t[:, :], idx1f[:, j:j + 1], None, ALU.is_equal).then_inc(pool_done, did.one())
                        pool.wait_ge(pool_done, did.n)
                        gp.tensor_scalar(iota_t[:, :], iota_t[:, :], float(P), None, ALU.add).then_inc(pool_done, did.one())
                        pool.wait_ge(pool_done, did.n)
                        pool.sem_inc(s["one_ready"], 1)

                    def rope(b):
                        pool.wait_ge(s["qk_sb"], b + 1)
                        q4 = qk[:, :, :, :].rearrange("p a h d -> p (a h) d")
                        r4 = rot[:, :, :, :].rearrange("p a h d -> p (a h) d")
                        hf = HD // 2
                        gp.tensor_tensor(r4[:, :, 0:hf], q4[:, :, hf:HD], sinv[:, 0:hf].unsqueeze(1).to_broadcast([P, 2 * NH, hf]), ALU.mult).then_inc(pool_done, did.one())
                        gp.tensor_tensor(r4[:, :, hf:HD], q4[:, :, 0:hf], sinv[:, hf:HD].unsqueeze(1).to_broadcast([P, 2 * NH, hf]), ALU.mult).then_inc(pool_done, did.one())
                        pool.wait_ge(pool_done, did.n)
                        gp.tensor_tensor(q4, q4, cosv[:, :].unsqueeze(1).to_broadcast([P, 2 * NH, HD]), ALU.mult).then_inc(pool_done, did.one())
                        pool.wait_ge(pool_done, did.n)
                        gp.tensor_tensor(q4, q4, r4, ALU.add).then_inc(pool_done, did.one())
                        pool.wait_ge(pool_done, did.n)
                        pool.sem_inc(s["rope_ready"], 1)
                    def keys(b, a, spread):
                        if a == 0:
                            pool.wait_ge(s["qkT_sb"], b + 1)
                        else:
                            pool.wait_ge(s["v_sb"], b + 1)
                            pool.sem_inc(pool_passed, 1)
                            for p, n in spread:
                                pool.wait_ge(kd_in[p], n)
                        for c in range(HC):
                            gp.tensor_tensor(kb[a][:, c, :, :], kT[:, a, c, :].unsqueeze(1).to_broadcast([P, 4, P]),
                                             grp[:, :].unsqueeze(2).to_broadcast([P, 4, P]), ALU.mult).then_inc(pool_done, did.one())
                        pool.wait_ge(pool_done, did.n)
                        pool.sem_inc(s["kb_ready"], 1)

                    def scatter(b, p):
                        pool.wait_ge(s["sl_ready"], b + 1)
                        pool.sem_inc(pool_passed, 1)
                        pool.indirect_dma_start(rows2, bass.IndirectOffsetOnAxis(ap=sl[p][:, :], axis=0), xn4[p][:, :], None,
                                                bounds_check=SLOTS2 - 1, oob_is_err=False).then_inc(xn4_out[p], 16)

                    def turn(b, p, has1, has2, end2, scattered, spread):
                        if has2:
                            pool.wait_ge(s["comb_ready"], b + 2)
                            pool.sem_inc(pool_passed, 1)
                            which_slots()
                        if has1:
                            rope(b + 1)
                        if end2:
                            scatter(b - 2, p)
                        if has1:
                            keys(b + 1, 1, [(p, spread)])
                            keys(b + 1, 0, [])
                        if end2:
                            pool.wait_ge(xn4_out[p], scattered)
                            pool.sem_inc(s["x4_free"], 1)

                    which_slots()
                    rope(0)
                    keys(0, 1, [])
                    keys(0, 0, [])
                    pool.wait_ge(s["comb_ready"], 1)
                    which_slots()
                    for b, has1, has2, end1, end2 in FIRST:
                        turn(b, b % 2, has1, has2, end2, 0, 128)
                    pool.wait_ge(pool_done, did.n)
                    pool.sem_inc(pool_done, -did.restart())
                    with pool.Fori(*LOOP) as b:
                        turn(b, 0, True, True, True, b * 8, b * 64 + 128)
                        turn(b + 1, 1, True, True, True, b * 8, b * 64 + 128)
                        pool.wait_ge(pool_done, did.n)
                        pool.sem_inc(pool_done, -did.restart())
                    for b, has1, has2, end1, end2 in LASTS + ENDS:
                        turn(b, b % 2, has1, has2, end2, 16 * (b // 2), 128 * (b // 2 + 1))
                    pool.wait_ge(pool_done, did.n)
                    pool.sem_inc(pool_done, -did.restart())

                @block.scalar
                def _(act):
                    sc = nc.scalar
                    act.wait_ge(consts_in, CONSTS3)
                    sc.activation(hg[:, :], hg[:, :], ACT.Tanh).then_inc(hgate_made, 1)
                    act.wait_ge(s["buffers_made"], 1)

                    def hook(k, b, p, has1, end1, end2):
                        if end2 and k == 2:
                            act.wait_ge(s["x4T_ready"], b - 1)
                            sc.activation(x4T[:, :, :], mb_[:, 0:H], ACT.Copy).then_inc(s["x4T_sb"], 1)
                        if end2 and k == 5:
                            act.wait_ge(s["ln_ready"], b - 1)
                            sc.activation(e8[:, :], c8[:, :], ACT.Exp, bias=sm[:, 0:1], accum_out=sm[:, 1:2]).then_inc(s["e8_ready"], 1)
                        if k == 6 and (has1 or end2):
                            act.wait_ge(s["xcT_ready"], b + 2)
                            lo, hi = 0 if has1 else H, H + E2 if end2 else H
                            last = sc.activation(xT[:, lo:hi], mb_[:, lo:hi], ACT.Copy)
                            last.then_inc(s["xcT_sb"], 1)
                        if has1 and k == 7:
                            act.wait_ge(s["qk_ready"], b + 2)
                            sc.activation(qk[:, :, :, :], mb_[:, :], ACT.Copy).then_inc(s["qk_sb"], 1)
                        if has1 and k == 8:
                            act.wait_ge(s["ka_ready"], b + 2)
                            sc.activation(ak[:, :], mb_[:, 0:H], ACT.Copy)
                            sc.activation(vv[1 - p][1][:, :, 0:HD], mb_[:, H:2 * H].rearrange("p (h d) -> p h d", d=HD), ACT.Copy).then_inc(s["ka_sb"], 1)
                        if has1 and k == 9:
                            act.wait_ge(s["v_ready"], b + 2)
                            sc.activation(vv[1 - p][0][:, :, 0:HD], mb_[:, 0:H].rearrange("p (h d) -> p h d", d=HD), ACT.Copy)
                            sc.activation(kT[:, 1, :, :], mb_[:, H:2 * H], ACT.Copy).then_inc(s["v_sb"], 1)
                        if has1 and k == 10:
                            act.wait_ge(s["qkT_ready"], b + 2)
                            sc.activation(qT[1 - p][:, :, :], mb_[:, 0:H], ACT.Copy, scale=float(HD) ** -0.5)
                            sc.activation(kT[:, 0, :, :], mb_[:, H:2 * H], ACT.Copy).then_inc(s["qkT_sb"], 1)
                        if end1 and k == 11:
                            act.wait_ge(s["aT_ready"], b)
                            sc.activation(atT[:, :, :], mb_[:, 0:H], ACT.Copy).then_inc(s["aT_sb"], 1)

                    def evacuate(b, w):
                        if w < NM:
                            act.wait_ge(s["tr_ready"], b * U + w + 1)
                            sc.activation(prT[w % 2][:, :, :], trp[:, :], ACT.Copy).then_inc(s["evac_main"], 1)

                    def outputs(b, w):
                        act.wait_ge(s["ot_ready"], b * 4 + w // 4 + 1)
                        sc.activation(ots[w // 4 % 2][:, :, :], otb[w // 4 % 2][:, :], ACT.Copy).then_inc(s["ot_sb"], 1)

                    def turn(b, p, has1, end1, end2, first=False):
                        for u in range(U):
                            if u >= 2:
                                evacuate(b, u - 2)
                            elif not first:
                                evacuate(b - 1, U + u - 2)
                            hook(u, b, p, has1, end1, end2)
                            act.wait_ge(s["nm_ready"], b * U + u + 1)
                            if u >= 4 or not first:
                                act.wait_ge(s["tr_ready"], b * U + u - 3)
                            for h in range(4):
                                last = sc.activation(pr[u % 4][:, h, :], score[u % 4][:, h * P:(h + 1) * P], ACT.Exp, bias=nm[:, u % 4, h:h + 1])
                            last.then_inc(s["p_ready"], 1)
                            if u == 3 and not first:
                                outputs(b - 1, 15)
                            if u in (7, 11, 15):
                                outputs(b, u - 4)

                    for k in range(U):
                        hook(k, -1, 1, True, False, False)
                    for b, has1, has2, end1, end2 in FIRST:
                        turn(b, b % 2, has1, end1, end2, b == 0)
                    with act.Fori(*LOOP) as b:
                        turn(b, 0, True, True, True)
                        turn(b + 1, 1, True, True, True)
                    for b, has1, has2, end1, end2 in LASTS:
                        turn(b, b % 2, has1, end1, end2)
                    outputs(B - 1, 15)
                    for b, has1, has2, end1, end2 in ENDS:
                        for k in range(U):
                            hook(k, b, b % 2, False, end1, end2)

                @block.vector
                def _(dve):
                    v, did = nc.vector, Count()
                    norm, end, att = Count(), Count(), Count()
                    for p in range(2):
                        for a in range(2):
                            v.memset(kd[p][a][:, :, :, :], 0.0).then_inc(s["kd_zero"], 1)
                    v.memset(before2[:, :], 0.0).then_inc(dve_done, did.one())
                    dve.wait_ge(s["buffers_made"], 1)
                    dve.wait_ge(hgate_made, 1)
                    dve.wait_ge(consts_in, CONSTS3)
                    dve.wait_ge(dve_done, did.n)

                    def batch(b):
                        return X[:, bass.ds(b, 1), :].rearrange("p a h -> p (a h)")

                    def normalise(i, a, done, count, dst, src):
                        dve.wait_ge(done, count.n)
                        y, w, t, half = rstd[:, a:a + 1], mvv[:, a:a + 1], rs_t[:, a:a + 1], rs_h[:, a:a + 1]
                        if i == 0:
                            v.bn_stats(st[:, a, :], src).then_inc(done, count.one())
                        if i == 1:
                            v.bn_aggr(mv[:, a, :], st[:, a, :]).then_inc(done, count.one())
                        if i == 2:
                            v.tensor_scalar(w, mv[:, a, 1:2], EPS, None, ALU.add).then_inc(done, count.one())
                        if i == 3:
                            v.tensor_scalar(t.bitcast(I32), w.bitcast(I32), 1, None, ALU.arith_shift_right).then_inc(done, count.one())
                        if i == 4:
                            v.tensor_scalar(y.bitcast(I32), t.bitcast(I32), -1.0, float(RSQRT_MAGIC), ALU.mult, ALU.add).then_inc(done, count.one())
                        if i in (5, 8, 11):
                            v.scalar_tensor_tensor(t, y, -0.5, y, ALU.mult, ALU.mult).then_inc(done, count.one())
                        if i in (6, 9, 12):
                            v.tensor_tensor(half, t, w, ALU.mult).then_inc(done, count.one())
                        if i in (7, 10, 13):
                            v.scalar_tensor_tensor(y, half, 1.5, y, ALU.add, ALU.mult).then_inc(done, count.one())
                        if i == 14:
                            v.tensor_scalar(dst, src, mv[:, a, 0:1], y, ALU.subtract, ALU.mult).then_inc(done, count.one())

                    def combined(b, slot):
                        if slot == 4:
                            dve.wait_ge(s["comb_ready"], b + 1)
                            v.scalar_tensor_tensor(batch(b), mb_[:, 0:H], tanh_g[:, 2:3], batch(b), ALU.mult, ALU.add).then_inc(s["norm_done"], norm.one())
                            dve.wait_ge(s["norm_done"], norm.n)
                            dve.sem_inc(s["comb_taken"], 1)
                        if 5 <= slot < 18:
                            normalise(slot - 5, 0, s["norm_done"], norm, xn[:, :], batch(b))
                        if slot == 17:
                            normalise(13, 0, s["norm_done"], norm, xn[:, :], batch(b))
                            normalise(14, 0, s["norm_done"], norm, xn[:, :], batch(b))
                            dve.wait_ge(s["norm_done"], norm.n)
                            dve.sem_inc(s["xc_ready"], 1)

                    def floor_mask(p, loads):
                        dve.wait_ge(ctx_in[p], loads)
                        v.tensor_scalar(mk[p][:, :], mk[p][:, :], F32_MIN, None, ALU.max).then_inc(dve_done, did.one())

                    def attended(b, slot):
                        if slot == 18:
                            dve.wait_ge(s["o_taken"], b * 4 + 4)
                            v.reciprocal(rr[:, :, :], oa[:, :, :, HD]).then_inc(s["att_done"], att.one())
                        if slot == 19:
                            dve.wait_ge(s["att_done"], att.n)
                            v.tensor_tensor(rr[:, 1, :], rr[:, 1, :], hg[:, :], ALU.mult).then_inc(s["att_done"], att.one())
                            v.tensor_tensor(at[:, :, :], oa[:, 0, :, 0:HD], rr[:, 0, :].unsqueeze(2).to_broadcast([P, NH, HD]), ALU.mult).then_inc(s["att_done"], att.one())
                        if slot == 22:
                            dve.wait_ge(s["att_done"], att.n)
                            v.tensor_tensor(at2[:, :, :], oa[:, 1, :, 0:HD], rr[:, 1, :].unsqueeze(2).to_broadcast([P, NH, HD]), ALU.mult).then_inc(s["att_done"], att.one())
                        if slot == 25:
                            dve.wait_ge(s["att_done"], att.n)
                            v.tensor_tensor(at[:, :, :], at[:, :, :], at2[:, :, :], ALU.add).then_inc(s["att_done"], att.one())
                            dve.wait_ge(s["att_done"], att.n)
                            dve.sem_inc(s["at_ready"], 1)

                    def projected(b, slot):
                        if slot == 40:
                            dve.wait_ge(s["wo_ready"], b + 1)
                            v.scalar_tensor_tensor(batch(b), mb_[:, 0:H], tanh_g[:, 1:2], batch(b), ALU.mult, ALU.add).then_inc(s["end_done"], end.one())
                            dve.wait_ge(s["end_done"], end.n)
                            dve.sem_inc(s["wo_taken"], 1)
                        if slot > 40:
                            normalise(slot - 41, 1, s["end_done"], end, None, batch(b))

                    def routed(b, p, slot):
                        if slot < 6:
                            normalise(slot + 7, 1, s["end_done"], end, xn4[p][:, :], batch(b))
                        if slot == 5:
                            normalise(13, 1, s["end_done"], end, xn4[p][:, :], batch(b))
                            dve.wait_ge(s["x4_free"], b + 1)
                            normalise(14, 1, s["end_done"], end, xn4[p][:, :], batch(b))
                            dve.wait_ge(s["end_done"], end.n)
                            dve.sem_inc(s["x4_ready"], 1)
                        if slot == 12:
                            dve.wait_ge(s["lg_ready"], b + 1)
                            v.tensor_copy(c8[:, :], mb_[:, 0:E2]).then_inc(s["end_done"], end.one())
                        if slot == 13:
                            dve.wait_ge(s["end_done"], end.n)
                            v.max(t8[:, :], c8[:, :]).then_inc(s["end_done"], end.one())
                        if slot == 14:
                            dve.wait_ge(s["end_done"], end.n)
                            v.tensor_scalar(sm[:, 0:1], t8[:, 0:1], -1.0, None, ALU.mult).then_inc(s["ln_ready"], 1)
                            v.max_index(i8[:, :], t8[:, :], c8[:, :]).then_inc(s["end_done"], end.one())
                        if slot == 15:
                            dve.wait_ge(s["end_done"], end.n)
                            v.tensor_copy(sm[:, 2:3], i8[:, 0:1]).then_inc(s["end_done"], end.one())
                        if slot == 16:
                            dve.wait_ge(s["end_done"], end.n)
                            v.tensor_scalar(m8[:, :], iota_e[:, 0:E2], sm[:, 2:3], None, ALU.is_equal).then_inc(s["end_done"], end.one())
                        if slot == 17:
                            dve.wait_ge(s["end_done"], end.n)
                            v.tensor_copy(m8b[:, :], m8[:, :]).then_inc(s["m_ready"], 1)
                        if slot == 18:
                            dve.wait_ge(s["e8_ready"], b + 1)
                            v.reciprocal(sm[:, 3:4], sm[:, 1:2]).then_inc(s["end_done"], end.one())
                        if slot == 20:
                            dve.wait_ge(s["end_done"], end.n)
                            v.scalar_tensor_tensor(pe8[:, :], e8[:, :], sm[:, 3:4], m8[:, :], ALU.mult, ALU.mult).then_inc(s["end_done"], end.one())
                        if slot == 21:
                            dve.wait_ge(s["xcT_sb"], b + 4)
                            v.tensor_tensor(n8[:, :], xT[:, H:H + E2], m8[:, :], ALU.mult).then_inc(s["end_done"], end.one())
                            v.tensor_tensor(before2[:, :], before2[:, :], m8b[:, :], ALU.add).then_inc(s["end_done"], end.one())
                        if slot == 23:
                            dve.wait_ge(s["end_done"], end.n)
                            v.tensor_reduce(sm[:, 4:5], pe8[:, :], axis=AX.X, op=ALU.add).then_inc(s["end_done"], end.one())
                            v.tensor_reduce(sm[:, 5:6], n8[:, :], axis=AX.X, op=ALU.add).then_inc(s["end_done"], end.one())
                        if slot == 24:
                            dve.wait_ge(s["end_done"], end.n)
                            v.tensor_scalar(sm[:, 6:7], sm[:, 5:6], float(CAP2), None, ALU.is_le).then_inc(s["end_done"], end.one())
                            v.scalar_tensor_tensor(sm[:, 8:9], sm[:, 2:3], float(CAP2), sm[:, 5:6], ALU.mult, ALU.add).then_inc(s["end_done"], end.one())
                        if slot == 26:
                            dve.wait_ge(s["end_done"], end.n)
                            v.tensor_tensor(wt2[:, bass.ds(b, 1)], sm[:, 4:5], sm[:, 6:7], ALU.mult).then_inc(s["end_done"], end.one())
                            v.tensor_scalar(sm[:, 7:8], sm[:, 6:7], -SKIP, SKIP - 1.0, ALU.mult, ALU.add).then_inc(s["end_done"], end.one())
                        if slot == 27:
                            dve.wait_ge(s["end_done"], end.n)
                            v.tensor_tensor(sm[:, 8:9], sm[:, 8:9], sm[:, 7:8], ALU.add).then_inc(s["end_done"], end.one())
                        if slot == 28:
                            dve.wait_ge(s["end_done"], end.n)
                            v.tensor_copy(sl[p][:, :], sm[:, 8:9]).then_inc(s["end_done"], end.one())
                            v.tensor_scalar(slot_g[:, bass.ds(b, 1)], sm[:, 8:9], float(SLOTS2), None, ALU.min).then_inc(s["end_done"], end.one())
                            dve.wait_ge(s["end_done"], end.n)
                            dve.sem_inc(s["sl_ready"], 1)

                    def small(slot, b, p, loads, has1, end1, end2):
                        if has1:
                            combined(b + 1, slot)
                        if end1:
                            attended(b - 1, slot)
                            projected(b - 1, slot)
                        if end2:
                            routed(b - 2, p, slot)
                        if has1 and slot == 36:
                            floor_mask(1 - p, loads)

                    def evacuate(b, w):
                        if w >= NM:
                            dve.wait_ge(s["tr_ready"], b * U + w + 1)
                            v.tensor_copy(prT[w % 2][:, :, :], trp[:, :]).then_inc(s["evac_ad"], 1)

                    def outputs(b, w):
                        a, half = w // 8, w // 4 % 2
                        dve.wait_ge(s["ob_ready"], b * 4 + w // 4 + 1)
                        v.tensor_copy(oa[:, a, 16 * half:16 * half + 16, :], otb[w // 4 % 2][:, :].rearrange("p (h d) -> p h d", d=32)[:, :, 0:HD + 1]).then_inc(s["o_taken"], 1)

                    def turn(b, p, loads, has1, end1, end2, first=False):
                        dve.wait_ge(dve_done, did.n)
                        for u in range(U):
                            dve.wait_ge(s["sc_ready"], b * U + u + 1)
                            sp4 = score[u % 4][:, :].rearrange("p (h t) -> p h t", h=4)
                            if u < NM:
                                v.tensor_tensor(sp4, sp4, mk[p][:, :].unsqueeze(1).to_broadcast([P, 4, P]), ALU.add).then_inc(dve_done, did.one())
                                small(3 * u, b, p, loads, has1, end1, end2)
                                dve.wait_ge(dve_done, did.n)
                            if u >= 4 or not first:
                                dve.wait_ge(s["p_ready"], b * U + u - 3)
                            v.tensor_reduce(nm[:, u % 4, :], sp4, axis=AX.X, op=ALU.max, negate=True).then_inc(s["nm_ready"], 1)
                            if u >= NM:
                                small(3 * u, b, p, loads, has1, end1, end2)
                            small(3 * u + 1, b, p, loads, has1, end1, end2)
                            if u >= 2:
                                evacuate(b, u - 2)
                            elif not first:
                                evacuate(b - 1, U + u - 2)
                            small(3 * u + 2, b, p, loads, has1, end1, end2)
                            if u == NM:
                                dve.wait_ge(dve_done, did.n)
                                dve.sem_inc(s["cin_free"], 1)
                            if u in (1, 5) and not first:
                                outputs(b - 1, 8 + 4 * (u // 4))
                            if u in (9, 13):
                                outputs(b, 4 * ((u - 9) // 4))

                    def restart():
                        for done, count in ((dve_done, did), (s["norm_done"], norm), (s["end_done"], end), (s["att_done"], att)):
                            dve.wait_ge(done, count.n)
                            dve.sem_inc(done, -count.restart())

                    for slot in range(3 * U):
                        small(slot, -1, 1, 32, True, False, False)
                    for b, has1, has2, end1, end2 in FIRST:
                        turn(b, b % 2, 32 * ((b + 1) // 2 + 1), has1, end1, end2, b == 0)
                    restart()
                    with dve.Fori(*LOOP) as b:
                        turn(b, 0, b * 16 + 32, True, True, True)
                        turn(b + 1, 1, b * 16 + 64, True, True, True)
                        restart()
                    for b, has1, has2, end1, end2 in LASTS:
                        turn(b, b % 2, 32 * ((b + 1) // 2 + 1), has1, end1, end2)
                    for w in (14, 15):
                        evacuate(B - 1, w)
                    outputs(B - 1, 8)
                    outputs(B - 1, 12)
                    for b, has1, has2, end1, end2 in ENDS:
                        for slot in range(3 * U):
                            small(slot, b, b % 2, 0, False, end1, end2)
                    restart()

                @block.tensor
                def _(pe):
                    t = nc.tensor
                    pe.wait_ge(consts_in, CONSTS3)
                    pe.wait_ge(s["buffers_made"], 1)

                    def combine(b, j0, j1):
                        if j0 == 0:
                            pe.wait_ge(s["one_ready"], b + 1)
                        for j in range(j0, j1):
                            for k in range(3):
                                last = t.matmul(mb_[:, 0:H], onehot[:, j, :], parts[:, j, k, :], start=j == 0 and k == 0, stop=j == N2 - 1 and k == 2)
                        if j1 == N2:
                            last.then_inc(s["comb_ready"], 1)

                    def hook(k, b, p, loads, has1, has2, end1, end2):
                        if has1 and k == 0:
                            combine(b + 1, 11, N2)
                        if end2 and k == 2:
                            if has1:
                                pe.wait_ge(s["comb_taken"], b + 2)
                            pe.wait_ge(s["x4_ready"], b - 1)
                            for c in range(HC):
                                last = t.transpose(mb_[:, c * P:(c + 1) * P], xn4[p][:, c * P:(c + 1) * P], idn[:, :])
                            last.then_inc(s["x4T_ready"], 1)
                        if end2 and k == 3:
                            pe.wait_ge(s["x4T_sb"], b - 1)
                            for c in range(HC):
                                last = t.matmul(mb_[:, 0:E2], x4T[:, c, :], g2w[:, c, :], start=c == 0, stop=c == HC - 1)
                            last.then_inc(s["lg_ready"], 1)
                        if k == 6 and (has1 or end2):
                            if end2:
                                pe.wait_ge(s["m_ready"], b - 1)
                                t.matmul(mb_[:, H:H + E2], upr[:, :], m8b[:, :], start=True, stop=False)
                                last = t.matmul(mb_[:, H:H + E2], ones_b[:, :], before2[:, :], start=False, stop=True)
                            if has1:
                                pe.wait_ge(s["xc_ready"], b + 2)
                                for c in range(HC):
                                    last = t.transpose(mb_[:, c * P:(c + 1) * P], xn[:, c * P:(c + 1) * P], idn[:, :])
                            last.then_inc(s["xcT_ready"], 1)
                        if has1 and k == 7:
                            pe.wait_ge(s["xcT_sb"], b + 2)
                            for c in range(HC):
                                last = t.matmul(mb_[:, :], xT[:, c * P:(c + 1) * P], wq[:, c, 0:2 * H], start=c == 0, stop=c == HC - 1)
                            last.then_inc(s["qk_ready"], 1)
                        if has1 and k == 8:
                            pe.wait_ge(s["qk_sb"], b + 2)
                            pe.wait_ge(ctx_in[1 - p], loads)
                            for c in range(HC):
                                last = t.matmul(mb_[:, :], cT[1 - p][:, c, :], wq[:, c, H:3 * H], start=c == 0, stop=c == HC - 1)
                            last.then_inc(s["ka_ready"], 1)
                        if has1 and k == 9:
                            pe.wait_ge(s["ka_sb"], b + 2)
                            for c in range(HC):
                                t.matmul(mb_[:, 0:H], xT[:, c * P:(c + 1) * P], wq[:, c, 2 * H:3 * H], start=c == 0, stop=c == HC - 1)
                            for c in range(HC):
                                last = t.transpose(mb_[:, H + c * P:H + (c + 1) * P], ak[:, c * P:(c + 1) * P], idn[:, :])
                            last.then_inc(s["v_ready"], 1)
                        if has1 and k == 10:
                            pe.wait_ge(s["v_sb"], b + 2)
                            pe.wait_ge(s["rope_ready"], b + 2)
                            for a in range(2):
                                for c in range(HC):
                                    src = qk[:, a, c * (NH // 2):(c + 1) * (NH // 2), :].rearrange("p h d -> p (h d)")
                                    last = t.transpose(mb_[:, a * H + c * P:a * H + (c + 1) * P], src, idn[:, :])
                            last.then_inc(s["qkT_ready"], 1)
                        if end1 and k == 11:
                            if has1:
                                pe.wait_ge(s["qkT_sb"], b + 2)
                            elif end2:
                                pe.wait_ge(s["xcT_sb"], b + 2)
                            pe.wait_ge(s["at_ready"], b)
                            for c in range(HC):
                                last = t.transpose(mb_[:, c * P:(c + 1) * P], at[:, c * (NH // 2):(c + 1) * (NH // 2), :].rearrange("p h d -> p (h d)"), idn[:, :])
                            last.then_inc(s["aT_ready"], 1)
                        if end1 and k == 12:
                            pe.wait_ge(s["aT_sb"], b)
                            for c in range(HC):
                                last = t.matmul(mb_[:, 0:H], atT[:, c, :], wo_sb[:, c, :], start=c == 0, stop=c == HC - 1)
                            last.then_inc(s["wo_ready"], 1)
                        if has2 and k == 14:
                            if end1:
                                pe.wait_ge(s["wo_taken"], b)
                            else:
                                pe.wait_ge(s["qkT_sb"], b + 2)
                            combine(b + 2, 0, 6)
                        if has2 and k == 15:
                            combine(b + 2, 6, 11)

                    def transposes(b, w, first=False):
                        pe.wait_ge(s["p_ready"], b * U + w + 1)
                        if w == 0 and not first:
                            pe.wait_ge(s["evac_ad"], b * NM)
                        if 1 <= w <= NM:
                            pe.wait_ge(s["evac_main"], b * NM + w)
                        if w > NM:
                            pe.wait_ge(s["evac_ad"], b * NM + w - NM)
                        for h in range(4):
                            last = t.transpose(trp[:, h * P:(h + 1) * P], pr[w % 4][:, h, :], idn[:, :])
                        last.then_inc(s["tr_ready"], 1)

                    def values(b, p, w, first=False):
                        if w < NM:
                            pe.wait_ge(s["evac_main"], b * NM + w + 1)
                        else:
                            pe.wait_ge(s["evac_ad"], b * NM + w - NM + 1)
                        if w % 4 == 0 and not (first and w < 8):
                            pe.wait_ge(s["o_taken"], b * 4 + w // 4 - 1)
                        for h in range(4):
                            last = t.matmul(otb[w // 4 % 2][32 * h:32 * h + 32, w % 4 * P:(w % 4 + 1) * P], vv[p][w // NM][:, 4 * (w % NM) + h, :],
                                            prT[w % 2][:, h, :], start=True, stop=True)
                        if w % 4 == 3:
                            last.then_inc(s["ot_ready"], 1)

                    def outputs(b, w):
                        pe.wait_ge(s["ot_sb"], b * 4 + w // 4 + 1)
                        for k in range(4):
                            last = t.transpose(otb[w // 4 % 2][:, k * P:(k + 1) * P], ots[w // 4 % 2][:, k, :], idn[:, :])
                        last.then_inc(s["ob_ready"], 1)

                    def turn(b, p, loads, spread, has1, has2, end1, end2, first=False):
                        pe.wait_ge(kd_in[p], spread)
                        for u in range(U):
                            if u >= 4 or not first:
                                pe.wait_ge(s["p_ready"], b * U + u - 3)
                            a, c, i = u // NM, u % NM // 4, u % 4
                            t.matmul(score[u % 4][:, :], qT[p][:, c, :], kd[p][a][:, c, 4 * i:4 * i + 4, :],
                                     start=True, stop=True).then_inc(s["sc_ready"], 1)
                            if u >= 2:
                                transposes(b, u - 2, first)
                            elif not first:
                                transposes(b - 1, U + u - 2)
                            if u >= 3:
                                values(b, p, u - 3, first)
                            elif not first:
                                values(b - 1, 1 - p, U + u - 3)
                            if u in (0, 4) and not first:
                                outputs(b - 1, 8 + u)
                            if u in (8, 12):
                                outputs(b, u - 8)
                            hook(u, b, p, loads, has1, has2, end1, end2)

                    combine(0, 0, 11)
                    for k in range(14):
                        hook(k, -1, 1, 32, True, True, False, False)
                    pe.wait_ge(s["qkT_sb"], 1)
                    combine(1, 0, 11)
                    for b, has1, has2, end1, end2 in FIRST:
                        turn(b, b % 2, 32 * ((b + 1) // 2 + 1), 128, has1, has2, end1, end2, b == 0)
                    with pe.Fori(*LOOP) as b:
                        turn(b, 0, b * 16 + 32, b * 64 + 128, True, True, True, True)
                        turn(b + 1, 1, b * 16 + 64, b * 64 + 128, True, True, True, True)
                    for b, has1, has2, end1, end2 in LASTS:
                        turn(b, b % 2, 32 * ((b + 1) // 2 + 1), 128 * (b // 2 + 1), has1, has2, end1, end2)
                    for w in (14, 15):
                        transposes(B - 1, w)
                        values(B - 1, 1, w - 1)
                    values(B - 1, 1, 15)
                    outputs(B - 1, 8)
                    outputs(B - 1, 12)
                    for b, has1, has2, end1, end2 in ENDS:
                        for k in range(U):
                            hook(k, b, b % 2, 0, has1, has2, end1, end2)

        NY = 8
        with ExitStack() as ph:
            xe = [sb(f"xe{q}", [P, 3, H], where=ph) for q in range(2)]
            xeT = [sb(f"xeT{q}", [P, HC, CAP2], where=ph) for q in range(2)]
            mid = [sb(f"mid{q}", [P, HC, CAP2], where=ph) for q in range(2)]
            ye = [sb(f"ye{q}", [P, 3, H], where=ph) for q in range(2)]
            sgc = [sb(f"sgc{q}", [P, 1], U32, where=ph) for q in range(NY)]
            yg = [sb(f"yg{q}", [P, H], where=ph) for q in range(NY)]
            wt2g = sb("wt2g", [P, B], where=ph)
            names = ["xt_ready", "xt_sb", "h_ready", "h_sb", "y_ready", "y_sb", "yg_free", "res_ready"]
            s = {n: sem("d_" + n) for n in names}
            rows_in = [sem(f"rows_in{q}") for q in range(2)]
            y_out = [sem(f"y_out{q}") for q in range(2)]
            yg_in = [sem(f"yg_in{q}") for q in range(NY)]
            res_out = sem("res_out")
            with nc.Block() as block:
                @block.sync
                def _(sp):
                    with sp.Fori(0, E2 // 2 - 1) as it:
                        for q in range(2):
                            e = it * 2 + q + 2
                            sp.wait_ge(s["h_ready"], it * 2 + q + 1)
                            sp.dma_start(w1s[q][:, :, :], w1[:, bass.ds(e, 1), :, :].rearrange("p a c n -> p (a c) n")).then_inc(w1_in[q], 16)
                            sp.wait_ge(s["y_ready"], it * 2 + q + 1)
                            sp.dma_start(w2s[q][:, :, :], w2[:, bass.ds(e, 1), :, :].rearrange("p a c n -> p (a c) n")).then_inc(w2_in[q], 16)

                @block.scalar
                def _(act):
                    sc = nc.scalar
                    for q in range(2):
                        act.sem_inc(y_out[q], 32)
                    with act.Fori(0, E2 // 2) as it:
                        for q in range(2):
                            n = it * 2 + q + 1
                            act.wait_ge(s["h_ready"], n)
                            for m in range(HC):
                                last = sc.activation(mid[q][:, m, :], pb[2 + 2 * q + m][:, 0:CAP2], ACT.Gelu)
                            last.then_inc(s["h_sb"], 1)
                            act.wait_ge(s["y_sb"], n + 1)
                            act.dma_start(youts[bass.ds((it * 2 + q) * CAP2, 2 * P), :].rearrange("(c p) n -> p c n", p=P), ye[q][:, 0:2, :]).then_inc(y_out[q], 16)
                            act.dma_start(youts[bass.ds((it * 2 + q) * CAP2 + 2 * P, 64), :], ye[q][0:64, 2, :]).then_inc(y_out[q], 16)
                    with act.Fori(0, B // 2) as it:
                        act.wait_ge(s["res_ready"], it * 2 + 2)
                        act.dma_start(out[:, bass.ds(it * 2, 2), :], X[:, bass.ds(it * 2, 2), :]).then_inc(res_out, 16)
                    act.wait_ge(res_out, 16 * (B // 2))

                @block.gpsimd
                def _(pool):
                    gp, did = nc.gpsimd, Count()

                    def load_rows(e, q):
                        pool.dma_start(xe[q][:, 0:2, :], rows2[bass.ds(e * CAP2, 2 * P), :].rearrange("(c p) n -> p c n", p=P)).then_inc(rows_in[q], 16)
                        pool.dma_start(xe[q][0:64, 2, :], rows2[bass.ds(e * CAP2 + 2 * P, 64), :]).then_inc(rows_in[q], 16)

                    for q in range(2):
                        load_rows(q, q)
                    with pool.Fori(0, E2 // 2 - 1) as it:
                        for q in range(2):
                            pool.wait_ge(s["xt_ready"], it * 2 + q + 1)
                            pool.sem_inc(pool_passed, 1)
                            load_rows(it * 2 + q + 2, q)
                    for q in range(2):
                        pool.wait_ge(y_out[q], 32 * (E2 // 2 + 1))
                    with pool.Fori(0, B // NY) as it:
                        for q in range(NY):
                            pool.wait_ge(s["yg_free"], it * NY + q + 1)
                            gp.tensor_copy(sgc[q][:, :], slot_g[:, bass.ds(it * NY + q, 1)]).then_inc(pool_done, did.one())
                            pool.wait_ge(pool_done, did.n)
                            pool.indirect_dma_start(yg[q][:, :], None, youts, bass.IndirectOffsetOnAxis(ap=sgc[q][:, :], axis=0),
                                                    bounds_check=SLOTS2, oob_is_err=False).then_inc(yg_in[q], 16)
                        pool.wait_ge(pool_done, did.n)
                        pool.sem_inc(pool_done, -did.restart())

                @block.vector
                def _(dve):
                    v, did = nc.vector, Count()
                    dve.sem_inc(s["y_sb"], 1)
                    for _ in range(NY):
                        dve.sem_inc(s["yg_free"], 1)
                    v.tensor_scalar(wt2g[:, :], wt2[:, :], tanh_g[:, 3:4], None, ALU.mult).then_inc(dve_done, did.one())

                    def transposed(n, q):
                        dve.wait_ge(s["xt_ready"], n)
                        for c in range(HC):
                            last = v.tensor_copy(xeT[q][:, c, :], pb[c][:, 0:CAP2])
                        last.then_inc(s["xt_sb"], 1)

                    def outputs(n, q, stored):
                        dve.wait_ge(s["y_ready"], n)
                        dve.wait_ge(y_out[q], stored)
                        v.tensor_copy(ye[q][:, 0:2, :], pb[6][:, :])
                        v.tensor_copy(ye[q][0:64, 2, :], pb[7][0:64, 0:H]).then_inc(s["y_sb"], 1)

                    for q in range(2):
                        transposed(q + 1, q)
                    with dve.Fori(0, E2 // 2 - 1) as it:
                        for q in range(2):
                            transposed(it * 2 + q + 3, q)
                            outputs(it * 2 + q + 1, q, it * 32 + 32)
                    for q in range(2):
                        outputs(E2 - 1 + q, q, 16 * E2)
                    dve.wait_ge(dve_done, did.n)
                    dve.sem_inc(dve_done, -did.restart())
                    with dve.Fori(0, B // NY) as it:
                        for q in range(NY):
                            dve.wait_ge(yg_in[q], it * 16 + 16)
                            xb = X[:, bass.ds(it * NY + q, 1), :].rearrange("p a h -> p (a h)")
                            v.scalar_tensor_tensor(xb, yg[q][:, :], wt2g[:, bass.ds(it * NY + q, 1)], xb, ALU.mult, ALU.add).then_inc(s["res_ready"], 1)
                            dve.wait_ge(s["res_ready"], it * NY + q + 1)
                            dve.sem_inc(s["yg_free"], 1)

                @block.tensor
                def _(pe):
                    t = nc.tensor

                    def transposes(q, rows):
                        pe.wait_ge(rows_in[q], rows)
                        for c in range(HC):
                            for o, m in CH2:
                                last = t.transpose(pb[c][:, o:o + m], xe[q][0:m, o // P, c * P:(c + 1) * P], idn[0:m, 0:m])
                        last.then_inc(s["xt_ready"], 1)

                    def hidden(n, q, weights):
                        pe.wait_ge(w1_in[q], weights)
                        pe.wait_ge(s["xt_sb"], n)
                        for m in range(HC):
                            for c in range(HC):
                                last = t.matmul(pb[2 + 2 * q + m][:, 0:CAP2], w1s[q][:, c, m * P:(m + 1) * P], xeT[q][:, c, :], start=c == 0, stop=c == HC - 1)
                        last.then_inc(s["h_ready"], 1)

                    def outputs(n, q, weights):
                        pe.wait_ge(w2_in[q], weights)
                        pe.wait_ge(s["y_sb"], n)
                        pe.wait_ge(s["h_sb"], n)
                        for j, (o, m) in enumerate(CH2):
                            for c in range(HC):
                                last = t.matmul(pb[6 + j // 2][0:m, (j % 2) * H:(j % 2) * H + H], mid[q][:, c, o:o + m], w2s[q][:, c, :], start=c == 0, stop=c == HC - 1)
                        last.then_inc(s["y_ready"], 1)

                    transposes(0, 32)
                    pe.wait_ge(s["xt_sb"], 1)
                    transposes(1, 32)
                    hidden(1, 0, 16)
                    with pe.Fori(0, E2 // 2 - 1) as it:
                        for q in range(2):
                            pe.wait_ge(s["xt_sb"], it * 2 + q + 2)
                            transposes(q, it * 32 + 64)
                            hidden(it * 2 + q + 2, 1 - q, it * 16 + 16 + 16 * q)
                            outputs(it * 2 + q + 1, q, it * 16 + 16)
                    hidden(E2, 1, 8 * E2)
                    for q in range(2):
                        outputs(E2 - 1 + q, q, 8 * E2)
        phase34.close()

def kernel(**a):
    import concourse.bacc as bacc
    from concourse import mybir as _mb
    from concourse.bass_utils import run_bass_kernel_spmd
    import ml_dtypes

    g = {k: np.asarray(v) for k, v in a.items()}
    f = np.float32
    inv = 1.0 / 10000.0 ** (np.arange(0, HD, 2, dtype=f) / HD)
    emb = np.outer(np.arange(S, dtype=f), inv)
    emb = np.concatenate([emb, emb], -1)
    cosv, sinv = np.cos(emb).astype(f), np.sin(emb).astype(f)
    sinv[:, :HD // 2] *= -1
    rows = np.arange(P)
    wgu = np.concatenate([g["L0_ffn_w_gate"], g["L0_ffn_w_up"]], -1)
    ins = {
        "x": g["x"].transpose(1, 0, 2), "ctx": g["ctx_2048"].transpose(1, 0, 2),
        "ctxT": g["ctx_2048"].transpose(0, 2, 1).reshape(B, HC, P, S).transpose(0, 2, 1, 3),
        "mask": g["mask_Bx1xSxS_fk0"][:, 0],
        "gates": np.concatenate([g["g_xattn"], g["g_ffn"]]),
        "theta_w": g["L0_xattn_theta_w"].T, "theta_b": g["L0_xattn_theta_b"][:, None],
        "phi_w": g["L0_xattn_phi_w"].T, "phi_b": g["L0_xattn_phi_b"][:, None],
        "g_w": g["L0_xattn_g_w"].T, "g_b": g["L0_xattn_g_b"],
        "gamma": g["L0_xattn_ln_gamma"], "beta": g["L0_xattn_ln_beta"],
        "out_w": g["L0_xattn_out_w"].T, "out_b": g["L0_xattn_out_b"][:, None],
        "gate1_w": g["L0_ffn_gate_w"].T.reshape(HC, P, E1).transpose(1, 0, 2),
        "w_gu": wgu.reshape(E1, HC, P, 2 * I1).transpose(2, 0, 1, 3),
        "w_d": g["L0_ffn_w_down"].reshape(E1, 2, I1H, H).transpose(2, 0, 1, 3),
        "sw_gu": np.concatenate([g["L0_ffn_sw_gate"], g["L0_ffn_sw_up"]], -1).reshape(HC, P, 2 * IS).transpose(1, 0, 2),
        "sw_d": g["L0_ffn_sw_down"],
        "wqkv": np.concatenate([g["L1_xattn_Wq"], g["L1_xattn_Wk"], g["L1_xattn_Wv"]], -1).reshape(HC, P, 3 * H).transpose(1, 0, 2),
        "wo": g["L1_xattn_Wo"].reshape(HC, P, H).transpose(1, 0, 2),
        "hgate": g["L1_xattn_gate"].reshape(NH),
        "gate2_w": g["L1_ffn_gate_weight"].T.reshape(HC, P, E2).transpose(1, 0, 2),
        "w1": g["L1_ffn_w1"].reshape(E2, HC, P, H).transpose(2, 0, 1, 3),
        "w2": g["L1_ffn_w2"].reshape(E2, HC, P, H).transpose(2, 0, 1, 3),
        "ident": np.eye(P, dtype=f), "upper": np.triu(np.ones((P, P), f)).astype(ml_dtypes.bfloat16),
        "cos": cosv, "sin": sinv,
        "group": (rows[:, None] % 32 // 8 == np.arange(4)).astype(f),
        "quarter": (rows[:, None] // 32 == np.arange(4)).astype(f),
    }
    nc = bacc.Bacc("TRN2", target_bir_lowering=False, num_devices=1)
    arrays, args = {}, []
    for name, v in ins.items():
        arrays[f"in_{name}"] = v = np.ascontiguousarray(v)
        args.append(nc.dram_tensor(f"in_{name}", v.shape, _mb.dt.from_np(v.dtype), kind="ExternalInput").ap())
    args.append(nc.dram_tensor("out_x", (P, B, H), _mb.dt.float32, kind="ExternalOutput").ap())
    build(nc, *args)
    r = run_bass_kernel_spmd(nc, [arrays], core_ids=[0])
    return r.results[0]["out_x"].transpose(1, 0, 2)
```

```python
import concourse.bass as bass
from concourse import mybir
from contextlib import ExitStack
import numpy as np

F32 = mybir.dt.float32
BF16 = mybir.dt.bfloat16
U32 = mybir.dt.uint32
I32 = mybir.dt.int32
ACT = mybir.ActivationFunctionType
ALU = mybir.AluOpType
AX = mybir.AxisListType

P = 128
B, S, H = 16, 128, 256
TOK = B * S
HC = H // P
LAT = 64
E1, K1, I1, CAP1 = 64, 6, 176, 32
SLOTS1 = E1 * CAP1
I1H = I1 // 2
IS = 352
ISC = [(0, 128), (128, 128), (256, 96)]
ROW = H + E1
NH, HD = 32, 8
E2, CAP2 = 8, 320
SLOTS2 = E2 * CAP2
CH2 = [(0, 128), (128, 128), (256, 64)]
EPS = 1e-5
RSQRT_MAGIC = 0x5F3759DF
F32_MIN = float(np.finfo(np.float32).min)
SKIP = 1.0e6

W1 = 4
R2 = 4


class Count:

    def __init__(self):
        self.n = 0

    def one(self):
        self.n += 1
        return 1

    def restart(self):
        n, self.n = self.n, 0
        return n


def rsqrt(nc, dve, done, count, y, v, half, t):
    vec = nc.vector
    vec.tensor_scalar(t.bitcast(I32), v.bitcast(I32), 1, None, ALU.arith_shift_right).then_inc(done, count.one())
    dve.wait_ge(done, count.n)
    vec.tensor_scalar(y.bitcast(I32), t.bitcast(I32), -1.0, float(RSQRT_MAGIC), ALU.mult, ALU.add).then_inc(done, count.one())
    dve.wait_ge(done, count.n)
    for _ in range(3):
        vec.scalar_tensor_tensor(t, y, -0.5, y, ALU.mult, ALU.mult).then_inc(done, count.one())
        dve.wait_ge(done, count.n)
        vec.tensor_tensor(half, t, v, ALU.mult).then_inc(done, count.one())
        dve.wait_ge(done, count.n)
        vec.scalar_tensor_tensor(y, half, 1.5, y, ALU.add, ALU.mult).then_inc(done, count.one())
        dve.wait_ge(done, count.n)


def build(nc, x, ctx, ctxT, mask, gates, theta_w, theta_b, phi_w, phi_b, g_w, g_b, gamma, beta, out_w, out_b,
          gate1_w, w_gu, w_d, sw_gu, sw_d, wqkv, wo, hgate, gate2_w, w1, w2, ident, upper, cos, sin, group, quarter,
          out):
    rows1 = nc.dram_tensor("rows1", [TOK + 1, ROW], F32, kind="Internal").ap()
    rows2 = nc.dram_tensor("rows2", [SLOTS2, H], F32, kind="Internal").ap()
    youts = nc.dram_tensor("youts", [SLOTS2 + 1, H], F32, kind="Internal").ap()

    with ExitStack() as whole:
        def sb(name, shape, dt=F32, where=whole):
            return where.enter_context(nc.sbuf_tensor(name, shape, dt))

        def sem(name):
            return whole.enter_context(nc.semaphore(name))

        pb = [whole.enter_context(nc.psum_tensor(f"bank{i}", [P, 512], F32)) for i in range(8)]

        X = sb("X", [P, B, H])
        idn = sb("idn", [P, P])
        upr = sb("upr", [P, P], BF16)
        ones_b = sb("ones_b", [P, P], BF16)
        tanh_g = sb("tanh_g", [P, 4])
        iota_e = sb("iota_e", [P, E1])
        idx1f = sb("idx1f", [P, B])
        idx1 = sb("idx1", [P, B], U32)
        rs_t, rs_h = sb("rs_t", [P, W1]), sb("rs_h", [P, W1])
        zrow = sb("zrow", [P, ROW])
        shared = sb("shared", [P, B * 3 * H], BF16)
        parts = shared[:, :].rearrange("p (j k h) -> p j k h", k=3, h=H)
        slot_g = sb("slot_g", [P, B], U32)
        wt2 = sb("wt2", [P, B])

        iota_t = sb("iota_t", [P, P])
        onehot = [sb(f"onehot{p}", [P, SLOTS1 // P, P], BF16) for p in range(2)]

        dve_done, pool_done = sem("dve_done"), sem("pool_done")
        one_ready = sem("one_ready")
        pe_passed, pool_passed = sem("pe_passed"), sem("pool_passed")
        consts_in, zero_made, zero_out = sem("consts_in"), sem("zero_made"), sem("zero_out")
        tanh_made, hgate_made, shared_in = sem("tanh_made"), sem("hgate_made"), sem("shared_in")

        def which_slots(nc, pool, count, p):
            for j in range(SLOTS1 // P):
                nc.gpsimd.tensor_scalar(onehot[p][:, j, :], iota_t[:, :], idx1f[:, j:j + 1], None, ALU.is_equal).then_inc(pool_done, count.one())
            pool.wait_ge(pool_done, count.n)
            nc.gpsimd.tensor_scalar(iota_t[:, :], iota_t[:, :], float(P), None, ALU.add).then_inc(pool_done, count.one())
            pool.wait_ge(pool_done, count.n)
            pool.sem_inc(one_ready, 1)

        phase12 = ExitStack()
        wgu_sb = [sb(f"wgu{r}", [P, 4, HC, 2 * I1], where=phase12) for r in range(R2)]
        wd_sb = [sb(f"wd{r}", [I1H, 4, 2, H], where=phase12) for r in range(R2)]
        experts_in = [sem(f"experts_in{r}") for r in range(R2)]
        down_in = [sem(f"down_in{r}") for r in range(R2)]

        CONSTS1 = 16 * 13

        with ExitStack() as ph:
            CX = shared[:, 0:2 * B * H].bitcast(F32).rearrange("p (b h) -> p b h", h=H)
            G = [shared[:, (2 * B + 8 * i) * H:(2 * B + 8 * i + 8) * H].rearrange("p (e c) -> p e c", c=CAP1) for i in range(2)]
            G += [sb(f"G{i}", [P, E1, CAP1], BF16, where=ph) for i in range(2, W1)]
            thw, phw, gw = (sb(n, [P, LAT], where=ph) for n in ("thw", "phw", "gw"))
            thb, phb = (sb(n, [LAT, 1], where=ph) for n in ("thb", "phb"))
            gb = sb("gb", [P, 2, LAT], where=ph)
            gam, bet = (sb(n, [LAT, H], where=ph) for n in ("gam", "bet"))
            ow, ob = sb("ow", [LAT, P], where=ph), sb("ob", [P, 1], where=ph)
            mean64 = sb("mean64", [LAT, LAT], where=ph)
            g1w = sb("g1w", [P, HC, E1], where=ph)
            sgu = sb("sgu", [P, HC, 2 * IS], where=ph)
            sdn = sb("sdn", [P, 3, H], where=ph)
            iota_c = sb("iota_c", [P, CAP1], BF16, where=ph)
            xn = [sb(f"xn{p}", [P, H], where=ph) for p in range(W1)]
            wx = [sb(f"wx{p}", [P, H], where=ph) for p in range(2)]
            th = [sb(f"th{p}", [LAT, 2 * H], where=ph) for p in range(W1)]
            gx = [sb(f"gx{p}", [P, 2, LAT], where=ph) for p in range(W1)]
            pr = [sb(f"pr{p}", [P, 2, H], where=ph) for p in range(W1)]
            prT = [sb(f"prT{p}", [P, 2, H], where=ph) for p in range(W1)]
            hh = [sb(f"hh{p}", [LAT, H], where=ph) for p in range(W1)]
            row = sb("row", [P, W1, ROW], where=ph)
            xT = [sb(f"xT{p}", [P, HC, P], where=ph) for p in range(W1)]
            sg = [sb(f"sg{p}", [P, 3, P], where=ph) for p in range(W1)]
            st = sb("st", [P, W1, 6], where=ph)
            mv = sb("mv", [P, W1, 2], where=ph)
            mvv = sb("mvv", [P, W1], where=ph)
            rstd = sb("rstd", [P, W1], where=ph)
            st2 = sb("st2", [LAT, W1, 2], where=ph)
            nmax = sb("nmax", [P, W1, 2], where=ph)
            psm = sb("psm", [P, W1, 2], where=ph)
            rin = sb("rin", [P, W1, 2], where=ph)
            t8 = sb("t8", [P, W1, 8], where=ph)
            i8 = sb("i8", [P, W1, 8], U32, where=ph)
            i8f = sb("i8f", [P, W1, 8], where=ph)
            ex = sb("ex", [P, W1, E1], where=ph)
            eq = sb("eq", [P, 2, K1, E1], where=ph)
            mf = sb("mf", [P, 2, E1], where=ph)
            mb = sb("mb", [P, W1, E1], BF16, where=ph)
            before = sb("before", [P, W1 + 1, E1], BF16, where=ph)
            cumc = sb("cumc", [P, W1, E1], BF16, where=ph)

            names = ["x_in", "xn_ready", "pt_ready", "gxp_ready", "pt_sb", "gx_sb", "sc_ready", "nm_ready",
                     "p_ready", "rin_ready", "pn_ready", "ptr_ready", "prT_sb", "tx_ready", "st2_ready", "mu_ready",
                     "hn_ready", "h_ready", "w_ready", "xn2_ready", "xt_ready", "xT_sb", "lg_ready", "gu_ready",
                     "lnm_ready", "e_ready", "mb_ready", "cum_ready", "G_ready", "ix_ready", "sg_ready",
                     "hs_ready", "dn_ready", "banks_free", "row_ready"]
            s = {n: sem(n) for n in names}
            row_out = [sem(f"row_out{p}") for p in range(W1)]
            bank_a = [pb[2 * p] for p in range(W1)]
            bank_b = [pb[2 * p + 1] for p in range(W1)]
            NIT = B // W1

            with nc.Block() as block:
                @block.sync
                def _(sp):
                    def load_batches(it):
                        sp.dma_start(X[:, bass.ds(it * W1, W1), :], x[:, bass.ds(it * W1, W1), :]).then_inc(s["x_in"], 16)
                        sp.dma_start(CX[:, bass.ds(it * W1, W1), :], ctx[:, bass.ds(it * W1, W1), :]).then_inc(s["x_in"], 16)

                    load_batches(0)
                    for dst, src in ((phw, phi_w), (thw, theta_w), (gw, g_w), (thb, theta_b), (phb, phi_b), (idn, ident),
                                     (gam, gamma), (bet, beta), (ow, out_w), (ob, out_b), (upr, upper)):
                        sp.dma_start(dst[:, :], src).then_inc(consts_in, 16)
                    sp.dma_start(gb[:, :, :], g_b.rearrange("(a c l) -> a c l", a=1, c=1).to_broadcast([P, 2, LAT])).then_inc(consts_in, 16)
                    sp.dma_start(tanh_g[:, :], gates.rearrange("(a n) -> a n", a=1).to_broadcast([P, 4])).then_inc(consts_in, 16)
                    sp.wait_ge(s["x_in"], 32)
                    load_batches(1)
                    sp.dma_start(g1w[:, :, :], gate1_w).then_inc(shared_in, 16)
                    sp.dma_start(sgu[:, :, :], sw_gu).then_inc(shared_in, 16)
                    sp.dma_start(sdn[:, 0:2, :], sw_d[0:2 * P, :].rearrange("(c p) n -> p c n", p=P)).then_inc(shared_in, 16)
                    sp.dma_start(sdn[0:IS - 2 * P, 2, :], sw_d[2 * P:IS, :]).then_inc(shared_in, 16)

                    def store_rows(it):
                        for p in range(W1):
                            sp.wait_ge(s["row_ready"], it * W1 + p + 1)
                            sp.dma_start(rows1[bass.ds((it * W1 + p) * P, P), :], row[:, p, :]).then_inc(row_out[p], 16)

                    for p in range(W1):
                        sp.sem_inc(row_out[p], 16)
                    for r in range(R2):
                        sp.dma_start(wgu_sb[r][:, :, :, :], w_gu[:, 4 * r:4 * r + 4, :, :]).then_inc(experts_in[r], 16)
                        sp.dma_start(wd_sb[r][:, :, :, :], w_d[:, 4 * r:4 * r + 4, :, :]).then_inc(down_in[r], 16)
                    with sp.Fori(0, NIT - 2) as it:
                        sp.wait_ge(s["x_in"], it * 32 + 64)
                        load_batches(it + 2)
                        store_rows(it)
                    store_rows(NIT - 2)
                    sp.wait_ge(zero_made, 2)
                    sp.dma_start(rows1[TOK:TOK + 1, :], zrow[0:1, :]).then_inc(zero_out, 16)
                    sp.dma_start(youts[SLOTS2:SLOTS2 + 1, :], zrow[0:1, 0:H]).then_inc(zero_out, 16)
                    for c in range(SLOTS2 // P):
                        sp.dma_start(rows2[c * P:(c + 1) * P, :], zrow[:, 0:H]).then_inc(zero_out, 16)
                    store_rows(NIT - 1)
                    sp.wait_ge(zero_out, 16 * (2 + SLOTS2 // P))
                    for p in range(W1):
                        sp.wait_ge(row_out[p], 16 * (NIT + 1))

                @block.gpsimd
                def _(pool):
                    gp, did = nc.gpsimd, Count()
                    gp.memset(zrow[:, :], 0.0).then_inc(zero_made, 1)
                    gp.iota(iota_e[:, :], [[1, E1]], base=0, channel_multiplier=0, allow_small_or_imprecise_dtypes=True).then_inc(pool_done, did.one())
                    pool.wait_ge(pool_done, did.n)
                    gp.iota(iota_c[:, :], [[1, CAP1]], base=0, channel_multiplier=0, allow_small_or_imprecise_dtypes=True).then_inc(pool_done, did.one())
                    pool.wait_ge(pool_done, did.n)
                    gp.iota(iota_t[:, :], [[1, P]], base=0, channel_multiplier=0, allow_small_or_imprecise_dtypes=True).then_inc(pool_done, did.one())
                    pool.wait_ge(pool_done, did.n)
                    gp.memset(mean64[:, :], 1.0 / LAT).then_inc(pool_done, did.one())
                    pool.wait_ge(pool_done, did.n)
                    gp.memset(ones_b[:, :], 1.0).then_inc(pool_done, did.one())
                    pool.wait_ge(pool_done, did.n)
                    pool.sem_inc(zero_made, 1)
                    pool.sem_inc(pool_done, -did.restart())

                @block.scalar
                def _(act):
                    sc = nc.scalar
                    act.wait_ge(consts_in, CONSTS1)
                    sc.activation(tanh_g[:, :], tanh_g[:, :], ACT.Tanh).then_inc(tanh_made, 1)

                    def over_sum(it, p):
                        act.wait_ge(s["rin_ready"], it * W1 + p + 1)
                        for c in range(2):
                            last = sc.activation(pr[p][:, c, :], pr[p][:, c, :], ACT.Copy, scale=rin[:, p, c:c + 1])
                        last.then_inc(s["pn_ready"], 1)

                    with act.Fori(0, NIT) as it:
                        for p in range(W1):
                            act.wait_ge(s["pt_ready"], it * W1 + p + 1)
                            sc.activation(th[p][:, 0:H], bank_a[p][0:LAT, 0:H], ACT.Identity, bias=phb[:, 0:1])
                            sc.activation(th[p][:, H:2 * H], bank_a[p][0:LAT, H:2 * H], ACT.Identity, bias=thb[:, 0:1]).then_inc(s["pt_sb"], 1)
                        for p in range(W1):
                            act.wait_ge(s["nm_ready"], it * W1 + p + 1)
                            for c in range(2):
                                last = sc.activation(pr[p][:, c, :], bank_a[p][:, c * H:(c + 1) * H], ACT.Exp,
                                                     bias=nmax[:, p, c:c + 1], accum_out=psm[:, p, c:c + 1])
                            last.then_inc(s["p_ready"], 1)
                            if p:
                                over_sum(it, p - 1)
                        over_sum(it, W1 - 1)
                        for p in range(W1):
                            act.wait_ge(s["ptr_ready"], it * W1 + p + 1)
                            sc.activation(prT[p][:, :, :], bank_b[p][:, :], ACT.Copy).then_inc(s["prT_sb"], 1)
                        for p in range(W1):
                            act.wait_ge(s["hn_ready"], it * W1 + p + 1)
                            sc.activation(hh[p][:, :], hh[p][:, :], ACT.Relu).then_inc(s["h_ready"], 1)
                        for p in range(W1):
                            act.wait_ge(s["xt_ready"], it * W1 + p + 1)
                            sc.activation(xT[p][:, :, :], bank_a[p][:, 0:H], ACT.Copy).then_inc(s["xT_sb"], 1)
                        for p in range(W1):
                            act.wait_ge(s["lnm_ready"], it * W1 + p + 1)
                            sc.activation(ex[:, p, :], bank_b[p][:, 448:512], ACT.Exp, bias=nmax[:, p, 0:1],
                                          accum_out=psm[:, p, 0:1]).then_inc(s["e_ready"], 1)
                        for p in range(W1):
                            act.wait_ge(s["gu_ready"], it * W1 + p + 1)
                            sc.activation(sg[p][:, 0:2, :], bank_a[p][:, 0:256], ACT.Silu)
                            sc.activation(sg[p][0:96, 2, :], bank_a[p][0:96, 256:384], ACT.Silu).then_inc(s["sg_ready"], 1)

                @block.vector
                def _(dve):
                    v, did = nc.vector, Count()

                    def variances():
                        dve.wait_ge(dve_done, did.n)
                        for p in range(W1):
                            v.bn_aggr(mv[:, p, :], st[:, p, :]).then_inc(dve_done, did.one())
                        dve.wait_ge(dve_done, did.n)
                        v.tensor_scalar(mvv[:, :], mv[:, :, 1], EPS, None, ALU.add).then_inc(dve_done, did.one())
                        dve.wait_ge(dve_done, did.n)
                        rsqrt(nc, dve, dve_done, did, rstd[:, :], mvv[:, :], rs_h[:, :], rs_t[:, :])

                    v.memset(idx1f[:, :], 0.0).then_inc(dve_done, did.one())
                    dve.wait_ge(dve_done, did.n)
                    v.memset(cumc[:, :, :], 2.0 * CAP1).then_inc(dve_done, did.one())
                    dve.wait_ge(dve_done, did.n)
                    v.memset(before[:, 0, :], 0.0).then_inc(dve_done, did.one())
                    dve.wait_ge(dve_done, did.n)
                    for _ in range(W1):
                        dve.sem_inc(s["banks_free"], 1)
                    dve.wait_ge(zero_made, 2)
                    dve.wait_ge(dve_done, did.n)
                    dve.sem_inc(dve_done, -did.restart())

                    def norm_x(it):
                        dve.wait_ge(s["x_in"], it * 32 + 32)
                        for p in range(W1):
                            v.bn_stats(st[:, p, :], X[:, bass.ds(it * W1 + p, 1), :]).then_inc(dve_done, did.one())
                        variances()
                        for p in range(W1):
                            v.tensor_scalar(xn[p][:, :], X[:, bass.ds(it * W1 + p, 1), :], mv[:, p, 0:1], rstd[:, p:p + 1],
                                            ALU.subtract, ALU.mult).then_inc(s["xn_ready"], 1)

                    def slots_of(it, p):
                        v.tensor_tensor(G[p][:, :, :], cumc[:, p, :].unsqueeze(2).to_broadcast([P, E1, CAP1]),
                                        iota_c[:, :].unsqueeze(1).to_broadcast([P, E1, CAP1]), ALU.is_le).then_inc(s["G_ready"], 1)

                    def add_slots(it, p):
                        dve.wait_ge(s["ix_ready"], it * W1 + p + 1)
                        dve.wait_ge(dve_done, did.n)
                        v.tensor_tensor(idx1f[:, :], idx1f[:, :], bank_b[p][:, 384:400], ALU.add).then_inc(dve_done, did.one())

                    def gated(it, p):
                        xb = X[:, bass.ds(it * W1 + p, 1), :].rearrange("p a h -> p (a h)")
                        v.scalar_tensor_tensor(xb, wx[p % 2][:, :], tanh_g[:, 0:1], xb, ALU.mult, ALU.add).then_inc(dve_done, did.one())

                    def step(it, more):
                        for p in range(W1):
                            dve.wait_ge(s["gxp_ready"], it * W1 + p + 1)
                            v.tensor_tensor(gx[p][:, :, :], bank_b[p][:, 0:2 * LAT].rearrange("p (c l) -> p c l", c=2), gb[:, :, :], ALU.add).then_inc(s["gx_sb"], 1)
                            if p >= 2:
                                slots_of(it, p)
                        for p in range(W1):
                            dve.wait_ge(s["sc_ready"], it * W1 + p + 1)
                            v.tensor_reduce(nmax[:, p, :], bank_a[p][:, :].rearrange("p (c t) -> p c t", c=2), axis=AX.X, op=ALU.max, negate=True).then_inc(s["nm_ready"], 1)
                            add_slots(it, p)
                        for p in range(W1):
                            dve.wait_ge(s["p_ready"], it * W1 + p + 1)
                            v.reciprocal(rin[:, p, :], psm[:, p, :]).then_inc(s["rin_ready"], 1)
                        if more:
                            norm_x(it + 1)
                        for p in range(W1):
                            dve.wait_ge(s["tx_ready"], it * W1 + p + 1)
                            v.bn_stats(st[0:LAT, p, :], bank_a[p][0:LAT, 0:H]).then_inc(dve_done, did.one())
                        dve.wait_ge(dve_done, did.n)
                        for p in range(W1):
                            v.bn_aggr(st2[:, p, :], st[0:LAT, p, :]).then_inc(dve_done, did.one())
                        dve.wait_ge(dve_done, did.n)
                        v.tensor_tensor(mvv[0:LAT, :], st2[:, :, 0], st2[:, :, 0], ALU.mult).then_inc(dve_done, did.one())
                        dve.wait_ge(dve_done, did.n)
                        v.tensor_tensor(st2[:, :, 1], mvv[0:LAT, :], st2[:, :, 1], ALU.add).then_inc(s["st2_ready"], 1)
                        dve.wait_ge(s["mu_ready"], it + 1)
                        v.tensor_copy(mv[0:LAT, :, :], bank_b[0][0:LAT, 0:2 * W1].rearrange("p (w t) -> p w t", t=2)).then_inc(dve_done, did.one())
                        dve.wait_ge(dve_done, did.n)
                        v.tensor_tensor(mvv[0:LAT, :], mv[0:LAT, :, 0], mv[0:LAT, :, 0], ALU.mult).then_inc(dve_done, did.one())
                        dve.wait_ge(dve_done, did.n)
                        v.scalar_tensor_tensor(mvv[0:LAT, :], mv[0:LAT, :, 1], EPS, mvv[0:LAT, :], ALU.add, ALU.subtract).then_inc(dve_done, did.one())
                        dve.wait_ge(dve_done, did.n)
                        rsqrt(nc, dve, dve_done, did, rstd[0:LAT, :], mvv[0:LAT, :], rs_h[0:LAT, :], rs_t[0:LAT, :])
                        for p in range(W1):
                            v.scalar_tensor_tensor(hh[p][:, :], bank_a[p][0:LAT, 0:H], mv[0:LAT, p, 0:1], gam[:, :], ALU.subtract, ALU.mult).then_inc(dve_done, did.one())
                            if p:
                                v.scalar_tensor_tensor(hh[p - 1][:, :], hh[p - 1][:, :], rstd[0:LAT, p - 1:p], bet[:, :], ALU.mult, ALU.add).then_inc(s["hn_ready"], 1)
                            dve.wait_ge(dve_done, did.n)
                        v.scalar_tensor_tensor(hh[W1 - 1][:, :], hh[W1 - 1][:, :], rstd[0:LAT, W1 - 1:W1], bet[:, :], ALU.mult, ALU.add).then_inc(s["hn_ready"], 1)
                        for p in range(W1):
                            dve.wait_ge(s["w_ready"], it * W1 + p + 1)
                            v.scalar_tensor_tensor(wx[p % 2][:, :], bank_b[p][:, 0:H], ob[:, 0:1], CX[:, bass.ds(it * W1 + p, 1), :].rearrange("p a h -> p (a h)"), ALU.add, ALU.add).then_inc(dve_done, did.one())
                            if p:
                                gated(it, p - 1)
                            dve.wait_ge(dve_done, did.n)
                        gated(it, W1 - 1)
                        dve.wait_ge(dve_done, did.n)
                        for p in range(W1):
                            v.bn_stats(st[:, p, :], X[:, bass.ds(it * W1 + p, 1), :]).then_inc(dve_done, did.one())
                        variances()
                        for p in range(W1):
                            dve.wait_ge(row_out[p], it * 16 + 16)
                            v.tensor_scalar(row[:, p, 0:H], X[:, bass.ds(it * W1 + p, 1), :], mv[:, p, 0:1], rstd[:, p:p + 1],
                                                    ALU.subtract, ALU.mult).then_inc(s["xn2_ready"], 1)
                        for p in range(W1):
                            dve.wait_ge(s["lg_ready"], it * W1 + p + 1)
                            v.tensor_reduce(nmax[:, p, 0:1], bank_b[p][:, 448:512], axis=AX.X, op=ALU.max, negate=True).then_inc(s["lnm_ready"], 1)
                        for p in range(0, W1, 2):
                            two = slice(p, p + 2)
                            dve.wait_ge(s["e_ready"], it * W1 + p + 2)
                            v.reciprocal(rin[:, two, 0], psm[:, two, 0]).then_inc(dve_done, did.one())
                            dve.wait_ge(dve_done, did.n)
                            v.tensor_tensor(ex[:, two, :], ex[:, two, :], rin[:, two, 0:1].to_broadcast([P, 2, E1]), ALU.mult).then_inc(dve_done, did.one())
                            dve.wait_ge(dve_done, did.n)
                            v.max(t8[:, p, :], ex[:, p, :]).then_inc(dve_done, did.one())
                            v.max(t8[:, p + 1, :], ex[:, p + 1, :]).then_inc(dve_done, did.one())
                            dve.wait_ge(dve_done, did.n)
                            v.max_index(i8[:, p, :], t8[:, p, :], ex[:, p, :]).then_inc(dve_done, did.one())
                            v.max_index(i8[:, p + 1, :], t8[:, p + 1, :], ex[:, p + 1, :]).then_inc(dve_done, did.one())
                            dve.wait_ge(dve_done, did.n)
                            v.tensor_copy(i8f[:, two, :], i8[:, two, :]).then_inc(dve_done, did.one())
                            dve.wait_ge(dve_done, did.n)
                            for q in range(2):
                                v.tensor_tensor(eq[:, q, :, :], iota_e[:, :].unsqueeze(1).to_broadcast([P, K1, E1]),
                                                i8f[:, p + q, 0:K1].unsqueeze(2).to_broadcast([P, K1, E1]), ALU.is_equal).then_inc(dve_done, did.one())
                            dve.wait_ge(dve_done, did.n)
                            v.tensor_reduce(mf[:, :, :], eq[:, :, :, :].rearrange("p q k e -> p q e k"), axis=AX.X, op=ALU.add).then_inc(dve_done, did.one())
                            dve.wait_ge(dve_done, did.n)
                            v.tensor_tensor(row[:, two, H:ROW], ex[:, two, :], mf[:, :, :], ALU.mult).then_inc(dve_done, did.one())
                            v.tensor_copy(mb[:, two, :], mf[:, :, :]).then_inc(dve_done, did.one())
                            dve.wait_ge(dve_done, did.n)
                            for q in range(p, p + 2):
                                v.tensor_tensor(before[:, q + 1, :], before[:, q, :], mb[:, q, :], ALU.add).then_inc(dve_done, did.one())
                                dve.wait_ge(dve_done, did.n)
                            dve.sem_inc(s["mb_ready"], 2)
                            dve.sem_inc(s["row_ready"], 2)
                        for p in range(W1):
                            dve.wait_ge(s["sg_ready"], it * W1 + p + 1)
                            v.tensor_tensor(sg[p][:, 0:2, :], sg[p][:, 0:2, :], bank_b[p][:, 0:256].rearrange("p (c t) -> p c t", c=2), ALU.mult).then_inc(dve_done, did.one())
                            v.tensor_tensor(sg[p][0:96, 2, :], sg[p][0:96, 2, :], bank_b[p][0:96, 256:384], ALU.mult).then_inc(dve_done, did.one())
                            dve.wait_ge(dve_done, did.n)
                            dve.sem_inc(s["hs_ready"], 1)
                        for p in range(W1):
                            dve.wait_ge(s["cum_ready"], it * W1 + p + 1)
                            v.tensor_scalar(cumc[:, p, :], bank_b[p][:, 448:512], 2.0 * CAP1, None, ALU.min).then_inc(dve_done, did.one())
                            if 1 <= p <= 2:
                                dve.wait_ge(dve_done, did.n)
                                slots_of(it + 1, p - 1)
                        v.tensor_copy(before[:, 0, :], before[:, W1, :]).then_inc(dve_done, did.one())
                        for p in range(W1):
                            dve.wait_ge(s["dn_ready"], it * W1 + p + 1)
                            xb = X[:, bass.ds(it * W1 + p, 1), :].rearrange("p a h -> p (a h)")
                            v.scalar_tensor_tensor(xb, bank_a[p][:, 0:H], tanh_g[:, 2:3], xb, ALU.mult, ALU.add).then_inc(dve_done, did.one())
                            dve.wait_ge(dve_done, did.n)
                            dve.sem_inc(s["banks_free"], 1)
                        dve.wait_ge(dve_done, did.n)
                        dve.sem_inc(dve_done, -did.restart())

                    for p in range(2):
                        slots_of(0, p)
                    norm_x(0)
                    dve.wait_ge(tanh_made, 1)
                    dve.wait_ge(consts_in, CONSTS1)
                    dve.wait_ge(dve_done, did.n)
                    dve.sem_inc(dve_done, -did.restart())
                    with dve.Fori(0, NIT - 1) as it:
                        step(it, True)
                    step(NIT - 1, False)
                    for p in range(2, W1):
                        slots_of(NIT, p)
                    for p in range(W1):
                        add_slots(NIT, p)
                    dve.wait_ge(dve_done, did.n)
                    v.tensor_copy(idx1[:, :], idx1f[:, :]).then_inc(dve_done, did.one())
                    dve.wait_ge(dve_done, did.n)
                    dve.wait_ge(dve_done, did.n)
                    dve.sem_inc(dve_done, -did.restart())

                @block.tensor
                def _(pe):
                    t = nc.tensor
                    pe.wait_ge(consts_in, CONSTS1)
                    pe.wait_ge(zero_made, 2)

                    def slots(it, p):
                        pe.wait_ge(s["G_ready"], it * W1 + p + 1)
                        gf = G[p][:, :, :].rearrange("p e c -> p (e c)")
                        for j in range(SLOTS1 // P):
                            last = t.matmul(bank_b[p][:, 384 + j:385 + j], gf[:, j * P:(j + 1) * P], ones_b[:, 0:1], start=True, stop=True)
                        last.then_inc(s["ix_ready"], 1)

                    with pe.Fori(0, NIT) as it:
                        for p in range(W1):
                            pe.wait_ge(s["banks_free"], it * W1 + p + 1)
                            pe.wait_ge(s["xn_ready"], it * W1 + p + 1)
                            t.matmul(bank_a[p][0:LAT, 0:H], phw[:, :], xn[p][:, :], start=True, stop=True)
                            t.matmul(bank_a[p][0:LAT, H:2 * H], thw[:, :], CX[:, bass.ds(it * W1 + p, 1), :].rearrange("p a h -> p (a h)"),
                                     start=True, stop=True).then_inc(s["pt_ready"], 1)
                            for c in range(2):
                                last = t.matmul(bank_b[p][:, c * LAT:(c + 1) * LAT], xn[p][:, c * P:(c + 1) * P], gw[:, :], start=True, stop=True)
                            last.then_inc(s["gxp_ready"], 1)
                        for p in range(W1):
                            pe.wait_ge(s["pt_sb"], it * W1 + p + 1)
                            for c in range(2):
                                last = t.matmul(bank_a[p][:, c * H:(c + 1) * H], th[p][:, H + c * P:H + (c + 1) * P], th[p][:, 0:H], start=True, stop=True)
                            last.then_inc(s["sc_ready"], 1)
                        for p in range(W1):
                            pe.wait_ge(s["gx_sb"], it * W1 + p + 1)
                            slots(it, p)
                        for p in range(W1):
                            pe.wait_ge(s["pn_ready"], it * W1 + p + 1)
                            for c in range(2):
                                for tc in range(2):
                                    last = t.transpose(bank_b[p][:, c * H + tc * P:c * H + (tc + 1) * P], pr[p][:, tc, c * P:(c + 1) * P], idn[:, :])
                            last.then_inc(s["ptr_ready"], 1)
                        for p in range(W1):
                            pe.wait_ge(s["prT_sb"], it * W1 + p + 1)
                            for c in range(2):
                                last = t.matmul(bank_a[p][0:LAT, 0:H], gx[p][:, c, :], prT[p][:, c, :], start=c == 0, stop=c == 1)
                            last.then_inc(s["tx_ready"], 1)
                        pe.wait_ge(s["st2_ready"], it + 1)
                        pe.sem_inc(pe_passed, 1)
                        t.matmul(bank_b[0][0:LAT, 0:2 * W1], mean64[:, :], st2[:, :, :].rearrange("p w t -> p (w t)"), start=True, stop=True).then_inc(s["mu_ready"], 1)
                        for p in range(W1):
                            pe.wait_ge(s["h_ready"], it * W1 + p + 1)
                            t.matmul(bank_b[p][:, 0:H], ow[:, :], hh[p][:, :], start=True, stop=True).then_inc(s["w_ready"], 1)
                        for p in range(W1):
                            pe.wait_ge(s["xn2_ready"], it * W1 + p + 1)
                            for c in range(HC):
                                last = t.transpose(bank_a[p][:, c * P:(c + 1) * P], row[:, p, c * P:(c + 1) * P], idn[:, :])
                            last.then_inc(s["xt_ready"], 1)
                        pe.wait_ge(shared_in, 16 * 4)
                        for p in range(W1):
                            pe.wait_ge(s["xT_sb"], it * W1 + p + 1)
                            for c in range(HC):
                                last = t.matmul(bank_b[p][:, 448:512], xT[p][:, c, :], g1w[:, c, :], start=c == 0, stop=c == HC - 1)
                            last.then_inc(s["lg_ready"], 1)
                        for k, banks in enumerate((bank_a, bank_b)):
                            for p in range(W1):
                                if k == 1:
                                    pe.wait_ge(s["e_ready"], it * W1 + p + 1)
                                for j, (o, m) in enumerate(ISC):
                                    for c in range(HC):
                                        last = t.matmul(banks[p][0:m, j * P:(j + 1) * P], sgu[:, c, k * IS + o:k * IS + o + m], xT[p][:, c, :],
                                                        start=c == 0, stop=c == HC - 1)
                                if k == 1:
                                    last.then_inc(s["gu_ready"], 1)
                        for p in range(W1):
                            pe.wait_ge(s["hs_ready"], it * W1 + p + 1)
                            pe.wait_ge(s["mb_ready"], it * W1 + p + 1)
                            t.matmul(bank_b[p][:, 448:512], upr[:, :], mb[:, p, :], start=True, stop=False)
                            t.matmul(bank_b[p][:, 448:512], ones_b[:, :], before[:, p, :], start=False, stop=True).then_inc(s["cum_ready"], 1)
                            for j, (o, m) in enumerate(ISC):
                                last = t.matmul(bank_a[p][:, 0:H], sg[p][0:m, j, :], sdn[0:m, j, :], start=j == 0, stop=j == 2)
                            last.then_inc(s["dn_ready"], 1)
                    for p in range(W1):
                        slots(NIT, p)

        N2 = SLOTS1 // P
        with ExitStack() as ph:
            qrt = sb("qrt", [P, 4], where=ph)
            idxc = [sb(f"idxc{r}", [P, 1], U32, where=ph) for r in range(R2)]
            xs = [sb(f"xs{r}", [P, ROW], where=ph) for r in range(R2)]
            xsT = [sb(f"xsT{q}", [P, HC, P], where=ph) for q in range(2)]
            hm = [sb(f"hm{q}", [P, I1], where=ph) for q in range(2)]
            hT = [sb(f"hT{q}", [I1H, 2, P], where=ph) for q in range(2)]
            w4 = sb("w4", [P, 2, 4], where=ph)
            ws = sb("ws", [P, 2], where=ph)
            yy = [sb(f"yy{q}", [P, H], where=ph) for q in range(2)]
            slots_in = [sem(f"slots_in{r}") for r in range(R2)]
            names = ["slots_free", "st_ready", "xsT_sb", "ug_ready", "silu_ready", "hm_ready", "ht_ready", "hT_sb", "y_ready", "y_taken"]
            s = {n: sem("e_" + n) for n in names}
            NIT = N2 // R2

            def steps(eng, step):
                with eng.Fori(0, NIT - 1) as it:
                    for r in range(R2):
                        step(it, r, True, True)
                for r in range(R2):
                    step(NIT - 1, r, r < R2 - 1, r < R2 - 2)

            with nc.Block() as block:
                @block.sync
                def _(sp):
                    sp.dma_start(qrt[:, :], quarter).then_inc(consts_in, 16)
                    with sp.Fori(1, NIT) as it:
                        for r in range(R2):
                            sp.wait_ge(s["ug_ready"], (it - 1) * R2 + r + 1)
                            sp.dma_start(wgu_sb[r][:, :, :, :], w_gu[:, bass.ds((it * R2 + r) * 4, 4), :, :]).then_inc(experts_in[r], 16)
                            sp.wait_ge(s["y_ready"], (it - 1) * R2 + r + 1)
                            sp.dma_start(wd_sb[r][:, :, :, :], w_d[:, bass.ds((it * R2 + r) * 4, 4), :, :]).then_inc(down_in[r], 16)

                @block.gpsimd
                def _(pool):
                    gp, did = nc.gpsimd, Count()
                    for _ in range(R2):
                        pool.sem_inc(s["slots_free"], 1)
                    with pool.Fori(0, NIT) as it:
                        for r in range(R2):
                            pool.wait_ge(s["slots_free"], it * R2 + r + 1)
                            gp.tensor_copy(idxc[r][:, :], idx1[:, bass.ds(it * R2 + r, 1)]).then_inc(pool_done, did.one())
                            pool.wait_ge(pool_done, did.n)
                            pool.indirect_dma_start(xs[r][:, :], None, rows1, bass.IndirectOffsetOnAxis(ap=idxc[r][:, :], axis=0),
                                                    bounds_check=TOK, oob_is_err=False).then_inc(slots_in[r], 16)
                        pool.wait_ge(pool_done, did.n)
                        pool.sem_inc(pool_done, -did.restart())
                    for p in range(2):
                        which_slots(nc, pool, did, p)
                    pool.wait_ge(pool_done, did.n)
                    pool.sem_inc(pool_done, -did.restart())

                @block.scalar
                def _(act):
                    sc = nc.scalar

                    def rows(n, q):
                        act.wait_ge(s["st_ready"], n)
                        sc.activation(xsT[q][:, :, :], pb[q][:, 0:H], ACT.Copy).then_inc(s["xsT_sb"], 1)

                    def gates(n, q):
                        act.wait_ge(s["ug_ready"], n)
                        sc.activation(hm[q][:, :], pb[2 + q][:, 0:I1], ACT.Silu).then_inc(s["silu_ready"], 1)

                    def step(it, r, has1, has2):
                        q, n = r % 2, it * R2 + r + 1
                        if has1:
                            gates(n + 1, 1 - q)
                        act.wait_ge(s["ht_ready"], n)
                        sc.activation(hT[q][:, :, :], pb[4 + q][0:I1H, 0:2 * P], ACT.Copy).then_inc(s["hT_sb"], 1)
                        if has2:
                            rows(n + 2, q)

                    rows(1, 0)
                    rows(2, 1)
                    gates(1, 0)
                    steps(act, step)

                @block.vector
                def _(dve):
                    v, did = nc.vector, Count()
                    for _ in range(2):
                        dve.sem_inc(s["y_taken"], 1)
                    dve.wait_ge(consts_in, CONSTS1 + 16)

                    def hidden(j, r, loads):
                        q = r % 2
                        dve.wait_ge(slots_in[r], loads)
                        v.tensor_tensor(w4[:, q, :], xs[r][:, bass.ds(H + j * 4, 4)], qrt[:, :], ALU.mult).then_inc(dve_done, did.one())
                        dve.wait_ge(dve_done, did.n)
                        v.tensor_reduce(ws[:, q:q + 1], w4[:, q, :], axis=AX.X, op=ALU.add).then_inc(dve_done, did.one())
                        dve.wait_ge(s["st_ready"], j + 1)
                        dve.sem_inc(s["slots_free"], 1)
                        dve.wait_ge(s["silu_ready"], j + 1)
                        v.tensor_tensor(hm[q][:, :], hm[q][:, :], pb[2 + q][:, I1:2 * I1], ALU.mult).then_inc(s["hm_ready"], 1)

                    def step(it, r, has1, has2):
                        q, j = r % 2, it * R2 + r
                        if has1:
                            hidden(j + 1, (r + 1) % R2, it * 16 + 16 + 16 * ((r + 1) // R2))
                        dve.wait_ge(s["y_ready"], j + 1)
                        v.tensor_scalar(yy[q][:, :], pb[6 + q][:, 0:H], ws[:, q:q + 1], None, ALU.mult).then_inc(dve_done, did.one())
                        dve.wait_ge(dve_done, did.n)
                        dve.sem_inc(s["y_taken"], 1)
                        part = [parts[:, bass.ds(j, 1), k, :].rearrange("p a h -> p (a h)") for k in range(3)]
                        v.tensor_copy(part[0], yy[q][:, :]).then_inc(dve_done, did.one())
                        dve.wait_ge(dve_done, did.n)
                        v.tensor_tensor(yy[q][:, :], yy[q][:, :], part[0], ALU.subtract).then_inc(dve_done, did.one())
                        dve.wait_ge(dve_done, did.n)
                        v.tensor_copy(part[1], yy[q][:, :]).then_inc(dve_done, did.one())
                        dve.wait_ge(dve_done, did.n)
                        v.tensor_tensor(part[2], yy[q][:, :], part[1], ALU.subtract).then_inc(dve_done, did.one())
                        if r == R2 - 1:
                            dve.wait_ge(dve_done, did.n)
                            dve.sem_inc(dve_done, -did.restart())

                    hidden(0, 0, 16)
                    dve.wait_ge(dve_done, did.n)
                    dve.sem_inc(dve_done, -did.restart())
                    steps(dve, step)

                @block.tensor
                def _(pe):
                    t = nc.tensor

                    def rows(r, loads):
                        q = r % 2
                        pe.wait_ge(slots_in[r], loads)
                        for c in range(HC):
                            last = t.transpose(pb[q][:, c * P:(c + 1) * P], xs[r][:, c * P:(c + 1) * P], idn[:, :])
                        last.then_inc(s["st_ready"], 1)

                    def gates(n, r, loads):
                        q = r % 2
                        pe.wait_ge(experts_in[r], loads)
                        pe.wait_ge(s["xsT_sb"], n)
                        for c in range(HC):
                            for e in range(4):
                                last = t.matmul(pb[2 + q][32 * e:32 * e + 32, 0:2 * I1], xsT[q][:, c, 32 * e:32 * e + 32],
                                                wgu_sb[r][:, e, c, :], start=c == 0, stop=c == HC - 1)
                        last.then_inc(s["ug_ready"], 1)

                    def step(it, r, has1, has2):
                        q, n = r % 2, it * R2 + r + 1
                        if has1:
                            gates(n + 1, (r + 1) % R2, it * 16 + 16 + 16 * ((r + 1) // R2))
                        pe.wait_ge(s["hm_ready"], n)
                        for c in range(2):
                            last = t.transpose(pb[4 + q][0:I1H, c * P:(c + 1) * P], hm[q][:, c * I1H:(c + 1) * I1H], idn[:, :])
                        last.then_inc(s["ht_ready"], 1)
                        if has2:
                            rows((r + 2) % R2, it * 16 + 16 + 16 * ((r + 2) // R2))
                        pe.wait_ge(down_in[r], it * 16 + 16)
                        pe.wait_ge(s["y_taken"], n)
                        pe.wait_ge(s["hT_sb"], n)
                        for c in range(2):
                            for e in range(4):
                                last = t.matmul(pb[6 + q][32 * e:32 * e + 32, 0:H], hT[q][:, c, 32 * e:32 * e + 32],
                                                wd_sb[r][:, e, c, :], start=c == 0, stop=c == 1)
                        last.then_inc(s["y_ready"], 1)

                    rows(0, 16)
                    rows(1, 16)
                    gates(1, 0, 16)
                    steps(pe, step)
        phase12.close()
        phase34 = ExitStack()
        w1s = [sb(f"w1s{q}", [P, HC, H], where=phase34) for q in range(2)]
        w2s = [sb(f"w2s{q}", [P, HC, H], where=phase34) for q in range(2)]
        w1_in, w2_in = [sem(f"w1_in{q}") for q in range(2)], [sem(f"w2_in{q}") for q in range(2)]

        with ExitStack() as ph:
            wq = sb("wq", [P, HC, 3 * H], where=ph)
            wo_sb = sb("wo_sb", [P, HC, H], where=ph)
            g2w = sb("g2w", [P, HC, E2], where=ph)
            cosv, sinv = (sb(n, [P, HD], where=ph) for n in ("cosv", "sinv"))
            grp = sb("grp", [P, 4], where=ph)
            hg = sb("hg", [P, NH], where=ph)
            cT = [sb(f"cT{p}", [P, HC, P], where=ph) for p in range(2)]
            mk = [sb(f"mk{p}", [P, P], where=ph) for p in range(2)]
            xn = sb("xc", [P, H], where=ph)
            xT = sb("xcT", [P, H + E2], where=ph)
            qk = sb("qk", [P, 2, NH, HD], where=ph)
            rot = sb("rot", [P, 2, NH, HD], where=ph)
            ak = sb("ak", [P, H], where=ph)
            kT = sb("kT", [P, 2, HC, P], where=ph)
            vv = [[sb(f"vv{p}{a}", [P, NH, 32], where=ph) for a in range(2)] for p in range(2)]
            qT = [sb(f"qT{p}", [P, HC, P], where=ph) for p in range(2)]
            kb = [sb(f"kb{a}", [P, HC, 4, P], where=ph) for a in range(2)]
            kd = [[sb(f"kd{p}{a}", [P, HC, 16, P], where=ph) for a in range(2)] for p in range(2)]
            pr = [sb(f"pc{i}", [P, 4, P], where=ph) for i in range(3)] + [sb("pc3", [P, 4, P], where=ph)]
            prT = [sb(f"pcT{i}", [P, 4, P], where=ph) for i in range(2)]
            ots = [sb(f"ots{i}", [P, 4, P], where=ph) for i in range(2)]
            nm = sb("nm", [P, 4, 4], where=ph)
            oa = sb("oa", [P, 2, NH, HD + 1], where=ph)
            rr = sb("rr", [P, 2, NH], where=ph)
            at = sb("at", [P, NH, HD], where=ph)
            at2 = sb("at2", [P, NH, HD], where=ph)
            atT = sb("atT", [P, HC, P], where=ph)
            xn4 = [sb(f"xn4{p}", [P, H], where=ph) for p in range(2)]
            x4T = sb("x4T", [P, HC, P], where=ph)
            st = sb("stc", [P, 2, 6], where=ph)
            mv = sb("mvc", [P, 2, 2], where=ph)
            mvv, rstd = sb("mvvc", [P, 2], where=ph), sb("rstdc", [P, 2], where=ph)
            t8 = sb("t8c", [P, 8], where=ph)
            i8 = sb("i8c", [P, 8], U32, where=ph)
            sm = sb("sm", [P, 16], where=ph)
            e8, m8, c8, pe8, n8 = (sb(n, [P, E2], where=ph) for n in ("e8", "m8", "c8", "pe8", "n8"))
            m8b = sb("m8b", [P, E2], BF16, where=ph)
            before2 = sb("before2", [P, E2], BF16, where=ph)
            sl = [sb(f"sl{p}", [P, 1], U32, where=ph) for p in range(2)]
            names = ["comb_ready", "comb_taken", "xc_ready", "xcT_ready", "xcT_sb", "qk_ready", "qk_sb", "ka_ready",
                     "ka_sb", "v_ready", "v_sb", "rope_ready", "qkT_ready", "qkT_sb", "kb_ready", "kd_zero", "at_ready", "aT_ready", "aT_sb",
                     "wo_ready", "wo_taken", "x4_ready", "x4T_ready", "x4T_sb", "lg_ready", "ln_ready", "e8_ready", "m_ready",
                     "sl_ready", "cin_free", "x4_free", "buffers_made",
                     "norm_done", "end_done", "att_done",
                     "sc_ready", "nm_ready", "p_ready", "tr_ready", "evac_main", "evac_ad", "pv_done",
                     "ot_ready", "ot_sb", "ob_ready", "o_taken"]
            s = {n: sem("c_" + n) for n in names}
            ctx_in = [sem(f"ctx_in{p}") for p in range(2)]
            xn4_out = [sem(f"xn4_out{p}") for p in range(2)]
            kd_in = [sem(f"kd_in{p}") for p in range(2)]
            score = pb[0:4]
            trp, otb, mb_ = pb[4], pb[5:7], pb[7]
            U, NM = 16, 8
            CONSTS3 = CONSTS1 + 16 * 8

            FIRST = [(0, True, True, False, False), (1, True, True, True, False)]
            LASTS = [(14, True, False, True, True), (15, False, False, True, True)]
            ENDS = [(16, False, False, True, True), (17, False, False, False, True)]
            LOOP = (2, 14, 2)

            with nc.Block() as block:
                @block.sync
                def _(sp):
                    for dst, src in ((wq, wqkv), (wo_sb, wo), (g2w, gate2_w)):
                        sp.dma_start(dst[:, :, :], src).then_inc(consts_in, 16)
                    for dst, src in ((cosv, cos), (sinv, sin), (grp, group)):
                        sp.dma_start(dst[:, :], src).then_inc(consts_in, 16)
                    sp.dma_start(hg[:, :], hgate.rearrange("(a n) -> a n", a=1).to_broadcast([P, NH])).then_inc(consts_in, 16)
                    for p in range(2):
                        sp.sem_inc(s["cin_free"], 1)

                    def load(b, p):
                        sp.wait_ge(s["cin_free"], b + 1)
                        sp.dma_start(cT[p][:, :, :], ctxT[bass.ds(b, 1), :, :, :].rearrange("a p c t -> p (a c) t")).then_inc(ctx_in[p], 16)
                        sp.dma_start(mk[p][:, :], mask[bass.ds(b, 1), :, :].rearrange("a p k -> p (a k)")).then_inc(ctx_in[p], 16)

                    def spread_keys(b, p):
                        for a in (1, 0):
                            sp.wait_ge(s["kb_ready"], b * 2 + 2 - a)
                            for g in range(4):
                                sp.dma_start(kd[p][a][32 * g:32 * g + 32, :, 4 * g:4 * g + 4, :], kb[a][32 * g:32 * g + 32, :, :, :]).then_inc(kd_in[p], 16)

                    load(0, 0)
                    load(1, 1)
                    for q in range(2):
                        sp.dma_start(w1s[q][:, :, :], w1[:, q, :, :]).then_inc(w1_in[q], 16)
                        sp.dma_start(w2s[q][:, :, :], w2[:, q, :, :]).then_inc(w2_in[q], 16)
                    sp.wait_ge(s["kd_zero"], 2)
                    spread_keys(0, 0)
                    sp.wait_ge(s["kd_zero"], 4)
                    with sp.Fori(1, B // 2) as it:
                        load(it * 2, 0)
                        spread_keys(it * 2 - 1, 1)
                        load(it * 2 + 1, 1)
                        spread_keys(it * 2, 0)
                    spread_keys(B - 1, 1)

                @block.gpsimd
                def _(pool):
                    gp, did = nc.gpsimd, Count()
                    for p in range(2):
                        for a in range(2):
                            gp.memset(vv[p][a][:, :, :], 0.0).then_inc(pool_done, did.one())
                    pool.wait_ge(pool_done, did.n)
                    for p in range(2):
                        for a in range(2):
                            gp.memset(vv[p][a][:, :, HD:HD + 1], 1.0).then_inc(pool_done, did.one())
                        pool.sem_inc(s["x4_free"], 1)
                    pool.wait_ge(pool_done, did.n)
                    pool.sem_inc(s["buffers_made"], 1)
                    pool.wait_ge(consts_in, CONSTS3)

                    def rope(b):
                        pool.wait_ge(s["qk_sb"], b + 1)
                        q4 = qk[:, :, :, :].rearrange("p a h d -> p (a h) d")
                        r4 = rot[:, :, :, :].rearrange("p a h d -> p (a h) d")
                        hf = HD // 2
                        gp.tensor_tensor(r4[:, :, 0:hf], q4[:, :, hf:HD], sinv[:, 0:hf].unsqueeze(1).to_broadcast([P, 2 * NH, hf]), ALU.mult).then_inc(pool_done, did.one())
                        gp.tensor_tensor(r4[:, :, hf:HD], q4[:, :, 0:hf], sinv[:, hf:HD].unsqueeze(1).to_broadcast([P, 2 * NH, hf]), ALU.mult).then_inc(pool_done, did.one())
                        pool.wait_ge(pool_done, did.n)
                        gp.tensor_tensor(q4, q4, cosv[:, :].unsqueeze(1).to_broadcast([P, 2 * NH, HD]), ALU.mult).then_inc(pool_done, did.one())
                        pool.wait_ge(pool_done, did.n)
                        gp.tensor_tensor(q4, q4, r4, ALU.add).then_inc(pool_done, did.one())
                        pool.wait_ge(pool_done, did.n)
                        pool.sem_inc(s["rope_ready"], 1)
                    def keys(b, a, spread):
                        if a == 0:
                            pool.wait_ge(s["qkT_sb"], b + 1)
                        else:
                            pool.wait_ge(s["v_sb"], b + 1)
                            pool.sem_inc(pool_passed, 1)
                            for p, n in spread:
                                pool.wait_ge(kd_in[p], n)
                        for c in range(HC):
                            gp.tensor_tensor(kb[a][:, c, :, :], kT[:, a, c, :].unsqueeze(1).to_broadcast([P, 4, P]),
                                             grp[:, :].unsqueeze(2).to_broadcast([P, 4, P]), ALU.mult).then_inc(pool_done, did.one())
                        pool.wait_ge(pool_done, did.n)
                        pool.sem_inc(s["kb_ready"], 1)

                    def scatter(b, p):
                        pool.wait_ge(s["sl_ready"], b + 1)
                        pool.sem_inc(pool_passed, 1)
                        pool.indirect_dma_start(rows2, bass.IndirectOffsetOnAxis(ap=sl[p][:, :], axis=0), xn4[p][:, :], None,
                                                bounds_check=SLOTS2 - 1, oob_is_err=False).then_inc(xn4_out[p], 16)

                    def turn(b, p, has1, has2, end2, scattered, spread):
                        if has2:
                            pool.wait_ge(s["comb_ready"], b + 1)
                            pool.sem_inc(pool_passed, 1)
                            which_slots(nc, pool, did, p)
                        if has1:
                            rope(b + 1)
                        if end2:
                            scatter(b - 2, p)
                        if has1:
                            keys(b + 1, 1, [(p, spread)])
                            keys(b + 1, 0, [])
                        if end2:
                            pool.wait_ge(xn4_out[p], scattered)
                            pool.sem_inc(s["x4_free"], 1)

                    rope(0)
                    keys(0, 1, [])
                    keys(0, 0, [])
                    for b, has1, has2, end1, end2 in FIRST:
                        turn(b, b % 2, has1, has2, end2, 0, 128)
                    pool.wait_ge(pool_done, did.n)
                    pool.sem_inc(pool_done, -did.restart())
                    with pool.Fori(*LOOP) as b:
                        turn(b, 0, True, True, True, b * 8, b * 64 + 128)
                        turn(b + 1, 1, True, True, True, b * 8, b * 64 + 128)
                        pool.wait_ge(pool_done, did.n)
                        pool.sem_inc(pool_done, -did.restart())
                    for b, has1, has2, end1, end2 in LASTS + ENDS:
                        turn(b, b % 2, has1, has2, end2, 16 * (b // 2), 128 * (b // 2 + 1))
                    pool.wait_ge(pool_done, did.n)
                    pool.sem_inc(pool_done, -did.restart())

                @block.scalar
                def _(act):
                    sc = nc.scalar
                    act.wait_ge(consts_in, CONSTS3)
                    sc.activation(hg[:, :], hg[:, :], ACT.Tanh).then_inc(hgate_made, 1)
                    act.wait_ge(s["buffers_made"], 1)

                    def hook(k, b, p, has1, end1, end2):
                        if end2 and k == 2:
                            act.wait_ge(s["x4T_ready"], b - 1)
                            sc.activation(x4T[:, :, :], mb_[:, 0:H], ACT.Copy).then_inc(s["x4T_sb"], 1)
                        if end2 and k == 5:
                            act.wait_ge(s["ln_ready"], b - 1)
                            sc.activation(e8[:, :], c8[:, :], ACT.Exp, bias=sm[:, 0:1], accum_out=sm[:, 1:2]).then_inc(s["e8_ready"], 1)
                        if k == 6 and (has1 or end2):
                            act.wait_ge(s["xcT_ready"], b + 2)
                            lo, hi = 0 if has1 else H, H + E2 if end2 else H
                            last = sc.activation(xT[:, lo:hi], mb_[:, lo:hi], ACT.Copy)
                            last.then_inc(s["xcT_sb"], 1)
                        if has1 and k == 7:
                            act.wait_ge(s["qk_ready"], b + 2)
                            sc.activation(qk[:, :, :, :], mb_[:, :], ACT.Copy).then_inc(s["qk_sb"], 1)
                        if has1 and k == 8:
                            act.wait_ge(s["ka_ready"], b + 2)
                            sc.activation(ak[:, :], mb_[:, 0:H], ACT.Copy)
                            sc.activation(vv[1 - p][1][:, :, 0:HD], mb_[:, H:2 * H].rearrange("p (h d) -> p h d", d=HD), ACT.Copy).then_inc(s["ka_sb"], 1)
                        if has1 and k == 9:
                            act.wait_ge(s["v_ready"], b + 2)
                            sc.activation(vv[1 - p][0][:, :, 0:HD], mb_[:, 0:H].rearrange("p (h d) -> p h d", d=HD), ACT.Copy)
                            sc.activation(kT[:, 1, :, :], mb_[:, H:2 * H], ACT.Copy).then_inc(s["v_sb"], 1)
                        if has1 and k == 10:
                            act.wait_ge(s["qkT_ready"], b + 2)
                            sc.activation(qT[1 - p][:, :, :], mb_[:, 0:H], ACT.Copy, scale=float(HD) ** -0.5)
                            sc.activation(kT[:, 0, :, :], mb_[:, H:2 * H], ACT.Copy).then_inc(s["qkT_sb"], 1)
                        if end1 and k == 11:
                            act.wait_ge(s["aT_ready"], b)
                            sc.activation(atT[:, :, :], mb_[:, 0:H], ACT.Copy).then_inc(s["aT_sb"], 1)

                    def evacuate(b, w):
                        if w < NM:
                            act.wait_ge(s["tr_ready"], b * U + w + 1)
                            sc.activation(prT[w % 2][:, :, :], trp[:, :], ACT.Copy).then_inc(s["evac_main"], 1)

                    def outputs(b, w):
                        act.wait_ge(s["ot_ready"], b * 4 + w // 4 + 1)
                        sc.activation(ots[w // 4 % 2][:, :, :], otb[w // 4 % 2][:, :], ACT.Copy).then_inc(s["ot_sb"], 1)

                    def turn(b, p, has1, end1, end2, first=False):
                        for u in range(U):
                            if u >= 3:
                                evacuate(b, u - 3)
                            elif not first:
                                evacuate(b - 1, U + u - 3)
                            hook(u, b, p, has1, end1, end2)
                            act.wait_ge(s["nm_ready"], b * U + u + 1)
                            if u >= 4 or not first:
                                act.wait_ge(s["tr_ready"], b * U + u - 3)
                            for h in range(4):
                                last = sc.activation(pr[u % 4][:, h, :], score[u % 4][:, h * P:(h + 1) * P], ACT.Exp, bias=nm[:, u % 4, h:h + 1])
                            last.then_inc(s["p_ready"], 1)
                            if u in (0, 4) and not first:
                                outputs(b - 1, 11 + u)
                            if u in (8, 12):
                                outputs(b, u - 5)

                    for k in range(U):
                        hook(k, -1, 1, True, False, False)
                    for b, has1, has2, end1, end2 in FIRST:
                        turn(b, b % 2, has1, end1, end2, b == 0)
                    with act.Fori(*LOOP) as b:
                        turn(b, 0, True, True, True)
                        turn(b + 1, 1, True, True, True)
                    for b, has1, has2, end1, end2 in LASTS:
                        turn(b, b % 2, has1, end1, end2)
                    outputs(B - 1, 11)
                    outputs(B - 1, 15)
                    for b, has1, has2, end1, end2 in ENDS:
                        for k in range(U):
                            hook(k, b, b % 2, False, end1, end2)

                @block.vector
                def _(dve):
                    v, did = nc.vector, Count()
                    norm, end, att = Count(), Count(), Count()
                    for a in (1, 0):
                        v.memset(kd[0][a][:, :, :, :], 0.0).then_inc(s["kd_zero"], 1)
                    v.memset(before2[:, :], 0.0).then_inc(dve_done, did.one())
                    dve.wait_ge(dve_done, did.n)

                    def batch(b):
                        return X[:, bass.ds(b, 1), :].rearrange("p a h -> p (a h)")

                    def normalise(i, a, done, count, dst, src):
                        dve.wait_ge(done, count.n)
                        y, w, t, half = rstd[:, a:a + 1], mvv[:, a:a + 1], rs_t[:, a:a + 1], rs_h[:, a:a + 1]
                        if i == 0:
                            v.bn_stats(st[:, a, :], src).then_inc(done, count.one())
                        if i == 1:
                            v.bn_aggr(mv[:, a, :], st[:, a, :]).then_inc(done, count.one())
                        if i == 2:
                            v.tensor_scalar(w, mv[:, a, 1:2], EPS, None, ALU.add).then_inc(done, count.one())
                        if i == 3:
                            v.tensor_scalar(t.bitcast(I32), w.bitcast(I32), 1, None, ALU.arith_shift_right).then_inc(done, count.one())
                        if i == 4:
                            v.tensor_scalar(y.bitcast(I32), t.bitcast(I32), -1.0, float(RSQRT_MAGIC), ALU.mult, ALU.add).then_inc(done, count.one())
                        if i in (5, 8, 11):
                            v.scalar_tensor_tensor(t, y, -0.5, y, ALU.mult, ALU.mult).then_inc(done, count.one())
                        if i in (6, 9, 12):
                            v.tensor_tensor(half, t, w, ALU.mult).then_inc(done, count.one())
                        if i in (7, 10, 13):
                            v.scalar_tensor_tensor(y, half, 1.5, y, ALU.add, ALU.mult).then_inc(done, count.one())
                        if i == 14:
                            v.tensor_scalar(dst, src, mv[:, a, 0:1], y, ALU.subtract, ALU.mult).then_inc(done, count.one())

                    def combined(b, slot):
                        if slot == 4:
                            dve.wait_ge(s["comb_ready"], b + 1)
                            v.scalar_tensor_tensor(batch(b), mb_[:, 0:H], tanh_g[:, 2:3], batch(b), ALU.mult, ALU.add).then_inc(s["norm_done"], norm.one())
                            dve.wait_ge(s["norm_done"], norm.n)
                            dve.sem_inc(s["comb_taken"], 1)
                        if 5 <= slot < 18:
                            normalise(slot - 5, 0, s["norm_done"], norm, xn[:, :], batch(b))
                        if slot == 17:
                            normalise(13, 0, s["norm_done"], norm, xn[:, :], batch(b))
                            normalise(14, 0, s["norm_done"], norm, xn[:, :], batch(b))
                            dve.wait_ge(s["norm_done"], norm.n)
                            dve.sem_inc(s["xc_ready"], 1)

                    def floor_mask(p, loads):
                        dve.wait_ge(ctx_in[p], loads)
                        v.tensor_scalar(mk[p][:, :], mk[p][:, :], F32_MIN, None, ALU.max).then_inc(dve_done, did.one())

                    def attended(b, slot):
                        if slot == 21:
                            dve.wait_ge(s["o_taken"], b * 4 + 4)
                            v.reciprocal(rr[:, :, :], oa[:, :, :, HD]).then_inc(s["att_done"], att.one())
                        if slot == 22:
                            dve.wait_ge(s["att_done"], att.n)
                            v.tensor_tensor(rr[:, 1, :], rr[:, 1, :], hg[:, :], ALU.mult).then_inc(s["att_done"], att.one())
                            v.tensor_tensor(at[:, :, :], oa[:, 0, :, 0:HD], rr[:, 0, :].unsqueeze(2).to_broadcast([P, NH, HD]), ALU.mult).then_inc(s["att_done"], att.one())
                        if slot == 25:
                            dve.wait_ge(s["att_done"], att.n)
                            v.tensor_tensor(at2[:, :, :], oa[:, 1, :, 0:HD], rr[:, 1, :].unsqueeze(2).to_broadcast([P, NH, HD]), ALU.mult).then_inc(s["att_done"], att.one())
                        if slot == 28:
                            dve.wait_ge(s["att_done"], att.n)
                            v.tensor_tensor(at[:, :, :], at[:, :, :], at2[:, :, :], ALU.add).then_inc(s["att_done"], att.one())
                            dve.wait_ge(s["att_done"], att.n)
                            dve.sem_inc(s["at_ready"], 1)

                    def projected(b, slot):
                        if slot == 40:
                            dve.wait_ge(s["wo_ready"], b + 1)
                            v.scalar_tensor_tensor(batch(b), mb_[:, 0:H], tanh_g[:, 1:2], batch(b), ALU.mult, ALU.add).then_inc(s["end_done"], end.one())
                            dve.wait_ge(s["end_done"], end.n)
                            dve.sem_inc(s["wo_taken"], 1)
                        if slot > 40:
                            normalise(slot - 41, 1, s["end_done"], end, None, batch(b))

                    def routed(b, p, slot):
                        if slot < 6:
                            normalise(slot + 7, 1, s["end_done"], end, xn4[p][:, :], batch(b))
                        if slot == 5:
                            normalise(13, 1, s["end_done"], end, xn4[p][:, :], batch(b))
                            dve.wait_ge(s["x4_free"], b + 1)
                            normalise(14, 1, s["end_done"], end, xn4[p][:, :], batch(b))
                            dve.wait_ge(s["end_done"], end.n)
                            dve.sem_inc(s["x4_ready"], 1)
                        if slot == 12:
                            dve.wait_ge(s["lg_ready"], b + 1)
                            v.tensor_copy(c8[:, :], mb_[:, 0:E2]).then_inc(s["end_done"], end.one())
                        if slot == 13:
                            dve.wait_ge(s["end_done"], end.n)
                            v.max(t8[:, :], c8[:, :]).then_inc(s["end_done"], end.one())
                        if slot == 14:
                            dve.wait_ge(s["end_done"], end.n)
                            v.tensor_scalar(sm[:, 0:1], t8[:, 0:1], -1.0, None, ALU.mult).then_inc(s["ln_ready"], 1)
                            v.max_index(i8[:, :], t8[:, :], c8[:, :]).then_inc(s["end_done"], end.one())
                        if slot == 15:
                            dve.wait_ge(s["end_done"], end.n)
                            v.tensor_copy(sm[:, 2:3], i8[:, 0:1]).then_inc(s["end_done"], end.one())
                        if slot == 16:
                            dve.wait_ge(s["end_done"], end.n)
                            v.tensor_scalar(m8[:, :], iota_e[:, 0:E2], sm[:, 2:3], None, ALU.is_equal).then_inc(s["end_done"], end.one())
                        if slot == 17:
                            dve.wait_ge(s["end_done"], end.n)
                            v.tensor_copy(m8b[:, :], m8[:, :]).then_inc(s["m_ready"], 1)
                        if slot == 18:
                            dve.wait_ge(s["e8_ready"], b + 1)
                            v.reciprocal(sm[:, 3:4], sm[:, 1:2]).then_inc(s["end_done"], end.one())
                        if slot == 20:
                            dve.wait_ge(s["end_done"], end.n)
                            v.scalar_tensor_tensor(pe8[:, :], e8[:, :], sm[:, 3:4], m8[:, :], ALU.mult, ALU.mult).then_inc(s["end_done"], end.one())
                        if slot == 21:
                            dve.wait_ge(s["xcT_sb"], b + 4)
                            v.tensor_tensor(n8[:, :], xT[:, H:H + E2], m8[:, :], ALU.mult).then_inc(s["end_done"], end.one())
                            v.tensor_tensor(before2[:, :], before2[:, :], m8b[:, :], ALU.add).then_inc(s["end_done"], end.one())
                        if slot == 23:
                            dve.wait_ge(s["end_done"], end.n)
                            v.tensor_reduce(sm[:, 4:5], pe8[:, :], axis=AX.X, op=ALU.add).then_inc(s["end_done"], end.one())
                            v.tensor_reduce(sm[:, 5:6], n8[:, :], axis=AX.X, op=ALU.add).then_inc(s["end_done"], end.one())
                        if slot == 24:
                            dve.wait_ge(s["end_done"], end.n)
                            v.tensor_scalar(sm[:, 6:7], sm[:, 5:6], float(CAP2), None, ALU.is_le).then_inc(s["end_done"], end.one())
                            v.scalar_tensor_tensor(sm[:, 8:9], sm[:, 2:3], float(CAP2), sm[:, 5:6], ALU.mult, ALU.add).then_inc(s["end_done"], end.one())
                        if slot == 26:
                            dve.wait_ge(s["end_done"], end.n)
                            v.tensor_tensor(wt2[:, bass.ds(b, 1)], sm[:, 4:5], sm[:, 6:7], ALU.mult).then_inc(s["end_done"], end.one())
                            v.tensor_scalar(sm[:, 7:8], sm[:, 6:7], -SKIP, SKIP - 1.0, ALU.mult, ALU.add).then_inc(s["end_done"], end.one())
                        if slot == 27:
                            dve.wait_ge(s["end_done"], end.n)
                            v.tensor_tensor(sm[:, 8:9], sm[:, 8:9], sm[:, 7:8], ALU.add).then_inc(s["end_done"], end.one())
                        if slot == 28:
                            dve.wait_ge(s["end_done"], end.n)
                            v.tensor_copy(sl[p][:, :], sm[:, 8:9]).then_inc(s["end_done"], end.one())
                            v.tensor_scalar(slot_g[:, bass.ds(b, 1)], sm[:, 8:9], float(SLOTS2), None, ALU.min).then_inc(s["end_done"], end.one())
                            dve.wait_ge(s["end_done"], end.n)
                            dve.sem_inc(s["sl_ready"], 1)

                    def small(slot, b, p, loads, has1, end1, end2):
                        if has1:
                            combined(b + 1, slot)
                        if end1:
                            attended(b - 1, slot)
                            projected(b - 1, slot)
                        if end2:
                            routed(b - 2, p, slot)
                        if has1 and slot == 36:
                            floor_mask(1 - p, loads)

                    def evacuate(b, w):
                        if w >= NM:
                            dve.wait_ge(s["tr_ready"], b * U + w + 1)
                            v.tensor_copy(prT[w % 2][:, :, :], trp[:, :]).then_inc(s["evac_ad"], 1)

                    def outputs(b, w):
                        a, half = w // 8, w // 4 % 2
                        dve.wait_ge(s["ob_ready"], b * 4 + w // 4 + 1)
                        v.tensor_copy(oa[:, a, 16 * half:16 * half + 16, :], otb[w // 4 % 2][:, :].rearrange("p (h d) -> p h d", d=32)[:, :, 0:HD + 1]).then_inc(s["o_taken"], 1)

                    def turn(b, p, loads, has1, end1, end2, first=False):
                        dve.wait_ge(dve_done, did.n)
                        for u in range(U):
                            dve.wait_ge(s["sc_ready"], b * U + u + 1)
                            sp4 = score[u % 4][:, :].rearrange("p (h t) -> p h t", h=4)
                            if u < NM:
                                v.tensor_tensor(sp4, sp4, mk[p][:, :].unsqueeze(1).to_broadcast([P, 4, P]), ALU.add).then_inc(dve_done, did.one())
                                small(3 * u, b, p, loads, has1, end1, end2)
                                dve.wait_ge(dve_done, did.n)
                            if u >= 4 or not first:
                                dve.wait_ge(s["p_ready"], b * U + u - 3)
                            v.tensor_reduce(nm[:, u % 4, :], sp4, axis=AX.X, op=ALU.max, negate=True).then_inc(s["nm_ready"], 1)
                            if u >= NM:
                                small(3 * u, b, p, loads, has1, end1, end2)
                            small(3 * u + 1, b, p, loads, has1, end1, end2)
                            if u >= 3:
                                evacuate(b, u - 3)
                            elif not first:
                                evacuate(b - 1, U + u - 3)
                            small(3 * u + 2, b, p, loads, has1, end1, end2)
                            if u == NM:
                                dve.wait_ge(dve_done, did.n)
                                dve.sem_inc(s["cin_free"], 1)
                            if u in (2, 6) and not first:
                                outputs(b - 1, 8 + 4 * (u // 4))
                            if u in (10, 14):
                                outputs(b, 4 * ((u - 10) // 4))

                    def restart():
                        for done, count in ((dve_done, did), (s["norm_done"], norm), (s["end_done"], end), (s["att_done"], att)):
                            dve.wait_ge(done, count.n)
                            dve.sem_inc(done, -count.restart())

                    for slot in range(3 * U):
                        small(slot, -1, 1, 32, True, False, False)
                    for a in (1, 0):
                        v.memset(kd[1][a][:, :, :, :], 0.0).then_inc(s["kd_zero"], 1)
                    dve.wait_ge(hgate_made, 1)
                    dve.wait_ge(consts_in, CONSTS3)
                    for b, has1, has2, end1, end2 in FIRST:
                        turn(b, b % 2, 32 * ((b + 1) // 2 + 1), has1, end1, end2, b == 0)
                    restart()
                    with dve.Fori(*LOOP) as b:
                        turn(b, 0, b * 16 + 32, True, True, True)
                        turn(b + 1, 1, b * 16 + 64, True, True, True)
                        restart()
                    for b, has1, has2, end1, end2 in LASTS:
                        turn(b, b % 2, 32 * ((b + 1) // 2 + 1), has1, end1, end2)
                    for w in (13, 14, 15):
                        evacuate(B - 1, w)
                    outputs(B - 1, 8)
                    outputs(B - 1, 12)
                    for b, has1, has2, end1, end2 in ENDS:
                        for slot in range(3 * U):
                            small(slot, b, b % 2, 0, False, end1, end2)
                    restart()

                @block.tensor
                def _(pe):
                    t = nc.tensor

                    def combine(b, p, j0, j1):
                        if j0 == 0:
                            pe.wait_ge(one_ready, b + 1)
                        for j in range(j0, j1):
                            for k in range(3):
                                last = t.matmul(mb_[:, 0:H], onehot[p][:, j, :], parts[:, j, k, :], start=j == 0 and k == 0, stop=j == N2 - 1 and k == 2)
                        if j1 == N2:
                            last.then_inc(s["comb_ready"], 1)

                    def hook(k, b, p, loads, has1, has2, end1, end2):
                        if has1 and k == 0:
                            combine(b + 1, 1 - p, 11, N2)
                        if end2 and k == 2:
                            if has1:
                                pe.wait_ge(s["comb_taken"], b + 2)
                            pe.wait_ge(s["x4_ready"], b - 1)
                            for c in range(HC):
                                last = t.transpose(mb_[:, c * P:(c + 1) * P], xn4[p][:, c * P:(c + 1) * P], idn[:, :])
                            last.then_inc(s["x4T_ready"], 1)
                        if end2 and k == 3:
                            pe.wait_ge(s["x4T_sb"], b - 1)
                            for c in range(HC):
                                last = t.matmul(mb_[:, 0:E2], x4T[:, c, :], g2w[:, c, :], start=c == 0, stop=c == HC - 1)
                            last.then_inc(s["lg_ready"], 1)
                        if k == 6 and (has1 or end2):
                            if end2:
                                pe.wait_ge(s["m_ready"], b - 1)
                                t.matmul(mb_[:, H:H + E2], upr[:, :], m8b[:, :], start=True, stop=False)
                                last = t.matmul(mb_[:, H:H + E2], ones_b[:, :], before2[:, :], start=False, stop=True)
                            if has1:
                                pe.wait_ge(s["xc_ready"], b + 2)
                                for c in range(HC):
                                    last = t.transpose(mb_[:, c * P:(c + 1) * P], xn[:, c * P:(c + 1) * P], idn[:, :])
                            last.then_inc(s["xcT_ready"], 1)
                        if has1 and k == 7:
                            pe.wait_ge(s["xcT_sb"], b + 2)
                            for c in range(HC):
                                last = t.matmul(mb_[:, :], xT[:, c * P:(c + 1) * P], wq[:, c, 0:2 * H], start=c == 0, stop=c == HC - 1)
                            last.then_inc(s["qk_ready"], 1)
                        if has1 and k == 8:
                            pe.wait_ge(s["qk_sb"], b + 2)
                            pe.wait_ge(ctx_in[1 - p], loads)
                            for c in range(HC):
                                last = t.matmul(mb_[:, :], cT[1 - p][:, c, :], wq[:, c, H:3 * H], start=c == 0, stop=c == HC - 1)
                            last.then_inc(s["ka_ready"], 1)
                        if has1 and k == 9:
                            pe.wait_ge(s["ka_sb"], b + 2)
                            for c in range(HC):
                                t.matmul(mb_[:, 0:H], xT[:, c * P:(c + 1) * P], wq[:, c, 2 * H:3 * H], start=c == 0, stop=c == HC - 1)
                            for c in range(HC):
                                last = t.transpose(mb_[:, H + c * P:H + (c + 1) * P], ak[:, c * P:(c + 1) * P], idn[:, :])
                            last.then_inc(s["v_ready"], 1)
                        if has1 and k == 10:
                            pe.wait_ge(s["v_sb"], b + 2)
                            pe.wait_ge(s["rope_ready"], b + 2)
                            for a in range(2):
                                for c in range(HC):
                                    src = qk[:, a, c * (NH // 2):(c + 1) * (NH // 2), :].rearrange("p h d -> p (h d)")
                                    last = t.transpose(mb_[:, a * H + c * P:a * H + (c + 1) * P], src, idn[:, :])
                            last.then_inc(s["qkT_ready"], 1)
                        if end1 and k == 11:
                            if has1:
                                pe.wait_ge(s["qkT_sb"], b + 2)
                            elif end2:
                                pe.wait_ge(s["xcT_sb"], b + 2)
                            pe.wait_ge(s["at_ready"], b)
                            for c in range(HC):
                                last = t.transpose(mb_[:, c * P:(c + 1) * P], at[:, c * (NH // 2):(c + 1) * (NH // 2), :].rearrange("p h d -> p (h d)"), idn[:, :])
                            last.then_inc(s["aT_ready"], 1)
                        if end1 and k == 12:
                            pe.wait_ge(s["aT_sb"], b)
                            for c in range(HC):
                                last = t.matmul(mb_[:, 0:H], atT[:, c, :], wo_sb[:, c, :], start=c == 0, stop=c == HC - 1)
                            last.then_inc(s["wo_ready"], 1)
                        if has2 and k == 14:
                            if end1:
                                pe.wait_ge(s["wo_taken"], b)
                            else:
                                pe.wait_ge(s["qkT_sb"], b + 2)
                            combine(b + 2, p, 0, 6)
                        if has2 and k == 15:
                            combine(b + 2, p, 6, 11)

                    def transposes(b, w, first=False):
                        pe.wait_ge(s["p_ready"], b * U + w + 1)
                        if w == 0 and not first:
                            pe.wait_ge(s["evac_ad"], b * NM)
                        if 1 <= w <= NM:
                            pe.wait_ge(s["evac_main"], b * NM + w)
                        if w > NM:
                            pe.wait_ge(s["evac_ad"], b * NM + w - NM)
                        for h in range(4):
                            last = t.transpose(trp[:, h * P:(h + 1) * P], pr[w % 4][:, h, :], idn[:, :])
                        last.then_inc(s["tr_ready"], 1)

                    def values(b, p, w, first=False):
                        if w < NM:
                            pe.wait_ge(s["evac_main"], b * NM + w + 1)
                        else:
                            pe.wait_ge(s["evac_ad"], b * NM + w - NM + 1)
                        if w % 4 == 0 and not (first and w < 8):
                            pe.wait_ge(s["o_taken"], b * 4 + w // 4 - 1)
                        for h in range(4):
                            last = t.matmul(otb[w // 4 % 2][32 * h:32 * h + 32, w % 4 * P:(w % 4 + 1) * P], vv[p][w // NM][:, 4 * (w % NM) + h, :],
                                            prT[w % 2][:, h, :], start=True, stop=True)
                        if w % 4 == 3:
                            last.then_inc(s["ot_ready"], 1)

                    def outputs(b, w):
                        pe.wait_ge(s["ot_sb"], b * 4 + w // 4 + 1)
                        for k in range(4):
                            last = t.transpose(otb[w // 4 % 2][:, k * P:(k + 1) * P], ots[w // 4 % 2][:, k, :], idn[:, :])
                        last.then_inc(s["ob_ready"], 1)

                    def turn(b, p, loads, spread, has1, has2, end1, end2, first=False):
                        pe.wait_ge(kd_in[p], spread)
                        for u in range(U):
                            if u >= 4 or not first:
                                pe.wait_ge(s["p_ready"], b * U + u - 3)
                            a, c, i = u // NM, u % NM // 4, u % 4
                            t.matmul(score[u % 4][:, :], qT[p][:, c, :], kd[p][a][:, c, 4 * i:4 * i + 4, :],
                                     start=True, stop=True).then_inc(s["sc_ready"], 1)
                            if u >= 3:
                                transposes(b, u - 3, first)
                            elif not first:
                                transposes(b - 1, U + u - 3)
                            hook(u, b, p, loads, has1, has2, end1, end2)
                            if u >= 4:
                                values(b, p, u - 4, first)
                            elif not first:
                                values(b - 1, 1 - p, U + u - 4)
                            if u in (1, 5) and not first:
                                outputs(b - 1, 7 + u)
                            if u in (9, 13):
                                outputs(b, u - 9)

                    combine(0, 0, 0, 11)
                    hook(0, -1, 1, 32, True, True, False, False)
                    pe.wait_ge(consts_in, CONSTS3)
                    for k in range(1, 14):
                        hook(k, -1, 1, 32, True, True, False, False)
                    pe.wait_ge(s["buffers_made"], 1)
                    pe.wait_ge(s["qkT_sb"], 1)
                    combine(1, 1, 0, 11)
                    for b, has1, has2, end1, end2 in FIRST:
                        turn(b, b % 2, 32 * ((b + 1) // 2 + 1), 128, has1, has2, end1, end2, b == 0)
                    with pe.Fori(*LOOP) as b:
                        turn(b, 0, b * 16 + 32, b * 64 + 128, True, True, True, True)
                        turn(b + 1, 1, b * 16 + 64, b * 64 + 128, True, True, True, True)
                    for b, has1, has2, end1, end2 in LASTS:
                        turn(b, b % 2, 32 * ((b + 1) // 2 + 1), 128 * (b // 2 + 1), has1, has2, end1, end2)
                    for w in (13, 14, 15):
                        transposes(B - 1, w)
                        values(B - 1, 1, w - 1)
                    values(B - 1, 1, 15)
                    outputs(B - 1, 8)
                    outputs(B - 1, 12)
                    for b, has1, has2, end1, end2 in ENDS:
                        for k in range(U):
                            hook(k, b, b % 2, 0, has1, has2, end1, end2)

        with ExitStack() as ph:
            xe = [sb(f"xe{q}", [P, 3, H], where=ph) for q in range(2)]
            xeT = [sb(f"xeT{q}", [P, HC, CAP2], where=ph) for q in range(2)]
            mid = [sb(f"mid{q}", [P, HC, CAP2], where=ph) for q in range(2)]
            ye = [sb(f"ye{q}", [P, 3, H], where=ph) for q in range(2)]
            yg = sb("yg", [P, B, H], where=ph)
            wt2g = sb("wt2g", [P, B], where=ph)
            names = ["xt_ready", "xt_sb", "h_ready", "h_sb", "y_ready", "y_sb", "res_ready"]
            s = {n: sem("d_" + n) for n in names}
            rows_in = [sem(f"rows_in{q}") for q in range(2)]
            y_out = [sem(f"y_out{q}") for q in range(2)]
            yg_in = [sem(f"yg_in{b}") for b in range(B)]
            res_out = sem("res_out")
            with nc.Block() as block:
                @block.sync
                def _(sp):
                    with sp.Fori(0, E2 // 2 - 1) as it:
                        for q in range(2):
                            e = it * 2 + q + 2
                            sp.wait_ge(s["h_ready"], it * 2 + q + 1)
                            sp.dma_start(w1s[q][:, :, :], w1[:, bass.ds(e, 1), :, :].rearrange("p a c n -> p (a c) n")).then_inc(w1_in[q], 16)
                            sp.wait_ge(s["y_ready"], it * 2 + q + 1)
                            sp.dma_start(w2s[q][:, :, :], w2[:, bass.ds(e, 1), :, :].rearrange("p a c n -> p (a c) n")).then_inc(w2_in[q], 16)

                @block.scalar
                def _(act):
                    sc = nc.scalar
                    for q in range(2):
                        act.sem_inc(y_out[q], 32)

                    def gelu(n, q):
                        act.wait_ge(s["h_ready"], n)
                        for m in range(HC):
                            last = sc.activation(mid[q][:, m, :], pb[2 + 2 * q + m][:, 0:CAP2], ACT.Gelu)
                        last.then_inc(s["h_sb"], 1)

                    def store(e, q):
                        act.wait_ge(s["y_sb"], e + 2)
                        act.dma_start(youts[bass.ds(e * CAP2, 2 * P), :].rearrange("(c p) n -> p c n", p=P), ye[q][:, 0:2, :]).then_inc(y_out[q], 16)
                        act.dma_start(youts[bass.ds(e * CAP2 + 2 * P, 64), :], ye[q][0:64, 2, :]).then_inc(y_out[q], 16)

                    gelu(1, 0)
                    gelu(2, 1)
                    with act.Fori(0, E2 // 2 - 1) as it:
                        for q in range(2):
                            store(it * 2 + q, q)
                            gelu(it * 2 + q + 3, q)
                    for q in range(2):
                        store(E2 - 2 + q, q)
                    with act.Fori(0, B // 2) as it:
                        act.wait_ge(s["res_ready"], it * 2 + 2)
                        act.dma_start(out[:, bass.ds(it * 2, 2), :], X[:, bass.ds(it * 2, 2), :]).then_inc(res_out, 16)
                    act.wait_ge(res_out, 16 * (B // 2))

                @block.gpsimd
                def _(pool):
                    gp = nc.gpsimd

                    def load_rows(e, q):
                        pool.dma_start(xe[q][:, 0:2, :], rows2[bass.ds(e * CAP2, 2 * P), :].rearrange("(c p) n -> p c n", p=P)).then_inc(rows_in[q], 16)
                        pool.dma_start(xe[q][0:64, 2, :], rows2[bass.ds(e * CAP2 + 2 * P, 64), :]).then_inc(rows_in[q], 16)

                    for q in range(2):
                        load_rows(q, q)
                    with pool.Fori(0, E2 // 2 - 1) as it:
                        for q in range(2):
                            pool.wait_ge(s["xt_ready"], it * 2 + q + 1)
                            pool.sem_inc(pool_passed, 1)
                            load_rows(it * 2 + q + 2, q)
                    for q in range(2):
                        pool.wait_ge(y_out[q], 32 * (E2 // 2 + 1))
                    for b in range(B):
                        pool.indirect_dma_start(yg[:, b, :], None, youts, bass.IndirectOffsetOnAxis(ap=slot_g[:, b:b + 1], axis=0),
                                                bounds_check=SLOTS2, oob_is_err=False).then_inc(yg_in[b], 16)

                @block.vector
                def _(dve):
                    v, did = nc.vector, Count()
                    dve.sem_inc(s["y_sb"], 1)
                    v.tensor_scalar(wt2g[:, :], wt2[:, :], tanh_g[:, 3:4], None, ALU.mult).then_inc(dve_done, did.one())

                    def transposed(n, q):
                        dve.wait_ge(s["xt_ready"], n)
                        for c in range(HC):
                            last = v.tensor_copy(xeT[q][:, c, :], pb[c][:, 0:CAP2])
                        last.then_inc(s["xt_sb"], 1)

                    def outputs(n, q, stored):
                        dve.wait_ge(s["y_ready"], n)
                        dve.wait_ge(y_out[q], stored)
                        v.tensor_copy(ye[q][:, 0:2, :], pb[6][:, :])
                        v.tensor_copy(ye[q][0:64, 2, :], pb[7][0:64, 0:H]).then_inc(s["y_sb"], 1)

                    for q in range(2):
                        transposed(q + 1, q)
                    with dve.Fori(0, E2 // 2 - 1) as it:
                        for q in range(2):
                            transposed(it * 2 + q + 3, q)
                            outputs(it * 2 + q + 1, q, it * 32 + 32)
                    for q in range(2):
                        outputs(E2 - 1 + q, q, 16 * E2)
                    dve.wait_ge(dve_done, did.n)
                    dve.sem_inc(dve_done, -did.restart())
                    for b in range(B):
                        dve.wait_ge(yg_in[b], 16)
                        v.scalar_tensor_tensor(X[:, b, :], yg[:, b, :], wt2g[:, b:b + 1], X[:, b, :], ALU.mult, ALU.add).then_inc(s["res_ready"], 1)

                @block.tensor
                def _(pe):
                    t = nc.tensor

                    def transposes(q, rows):
                        pe.wait_ge(rows_in[q], rows)
                        for c in range(HC):
                            for o, m in CH2:
                                last = t.transpose(pb[c][:, o:o + m], xe[q][0:m, o // P, c * P:(c + 1) * P], idn[0:m, 0:m])
                        last.then_inc(s["xt_ready"], 1)

                    def hidden(n, q, weights):
                        pe.wait_ge(w1_in[q], weights)
                        pe.wait_ge(s["xt_sb"], n)
                        for m in range(HC):
                            for c in range(HC):
                                last = t.matmul(pb[2 + 2 * q + m][:, 0:CAP2], w1s[q][:, c, m * P:(m + 1) * P], xeT[q][:, c, :], start=c == 0, stop=c == HC - 1)
                        last.then_inc(s["h_ready"], 1)

                    def outputs(n, q, weights):
                        pe.wait_ge(w2_in[q], weights)
                        pe.wait_ge(s["y_sb"], n)
                        pe.wait_ge(s["h_sb"], n)
                        for j, (o, m) in enumerate(CH2):
                            for c in range(HC):
                                last = t.matmul(pb[6 + j // 2][0:m, (j % 2) * H:(j % 2) * H + H], mid[q][:, c, o:o + m], w2s[q][:, c, :], start=c == 0, stop=c == HC - 1)
                        last.then_inc(s["y_ready"], 1)

                    transposes(0, 32)
                    pe.wait_ge(s["xt_sb"], 1)
                    transposes(1, 32)
                    hidden(1, 0, 16)
                    with pe.Fori(0, E2 // 2 - 1) as it:
                        for q in range(2):
                            pe.wait_ge(s["xt_sb"], it * 2 + q + 2)
                            transposes(q, it * 32 + 64)
                            hidden(it * 2 + q + 2, 1 - q, it * 16 + 16 + 16 * q)
                            outputs(it * 2 + q + 1, q, it * 16 + 16)
                    hidden(E2, 1, 8 * E2)
                    for q in range(2):
                        outputs(E2 - 1 + q, q, 8 * E2)
        phase34.close()

def kernel(**a):
    import concourse.bacc as bacc
    from concourse import mybir as _mb
    from concourse.bass_utils import run_bass_kernel_spmd
    import ml_dtypes

    g = {k: np.asarray(v) for k, v in a.items()}
    f = np.float32
    inv = 1.0 / 10000.0 ** (np.arange(0, HD, 2, dtype=f) / HD)
    emb = np.outer(np.arange(S, dtype=f), inv)
    emb = np.concatenate([emb, emb], -1)
    cosv, sinv = np.cos(emb).astype(f), np.sin(emb).astype(f)
    sinv[:, :HD // 2] *= -1
    rows = np.arange(P)
    wgu = np.concatenate([g["L0_ffn_w_gate"], g["L0_ffn_w_up"]], -1)
    ins = {
        "x": g["x"].transpose(1, 0, 2), "ctx": g["ctx_2048"].transpose(1, 0, 2),
        "ctxT": g["ctx_2048"].transpose(0, 2, 1).reshape(B, HC, P, S).transpose(0, 2, 1, 3),
        "mask": g["mask_Bx1xSxS_fk0"][:, 0],
        "gates": np.concatenate([g["g_xattn"], g["g_ffn"]]),
        "theta_w": g["L0_xattn_theta_w"].T, "theta_b": g["L0_xattn_theta_b"][:, None],
        "phi_w": g["L0_xattn_phi_w"].T, "phi_b": g["L0_xattn_phi_b"][:, None],
        "g_w": g["L0_xattn_g_w"].T, "g_b": g["L0_xattn_g_b"],
        "gamma": g["L0_xattn_ln_gamma"], "beta": g["L0_xattn_ln_beta"],
        "out_w": g["L0_xattn_out_w"].T, "out_b": g["L0_xattn_out_b"][:, None],
        "gate1_w": g["L0_ffn_gate_w"].T.reshape(HC, P, E1).transpose(1, 0, 2),
        "w_gu": wgu.reshape(E1, HC, P, 2 * I1).transpose(2, 0, 1, 3),
        "w_d": g["L0_ffn_w_down"].reshape(E1, 2, I1H, H).transpose(2, 0, 1, 3),
        "sw_gu": np.concatenate([g["L0_ffn_sw_gate"], g["L0_ffn_sw_up"]], -1).reshape(HC, P, 2 * IS).transpose(1, 0, 2),
        "sw_d": g["L0_ffn_sw_down"],
        "wqkv": np.concatenate([g["L1_xattn_Wq"], g["L1_xattn_Wk"], g["L1_xattn_Wv"]], -1).reshape(HC, P, 3 * H).transpose(1, 0, 2),
        "wo": g["L1_xattn_Wo"].reshape(HC, P, H).transpose(1, 0, 2),
        "hgate": g["L1_xattn_gate"].reshape(NH),
        "gate2_w": g["L1_ffn_gate_weight"].T.reshape(HC, P, E2).transpose(1, 0, 2),
        "w1": g["L1_ffn_w1"].reshape(E2, HC, P, H).transpose(2, 0, 1, 3),
        "w2": g["L1_ffn_w2"].reshape(E2, HC, P, H).transpose(2, 0, 1, 3),
        "ident": np.eye(P, dtype=f), "upper": np.triu(np.ones((P, P), f)).astype(ml_dtypes.bfloat16),
        "cos": cosv, "sin": sinv,
        "group": (rows[:, None] % 32 // 8 == np.arange(4)).astype(f),
        "quarter": (rows[:, None] // 32 == np.arange(4)).astype(f),
    }
    nc = bacc.Bacc("TRN2", target_bir_lowering=False, num_devices=1)
    arrays, args = {}, []
    for name, v in ins.items():
        arrays[f"in_{name}"] = v = np.ascontiguousarray(v)
        args.append(nc.dram_tensor(f"in_{name}", v.shape, _mb.dt.from_np(v.dtype), kind="ExternalInput").ap())
    args.append(nc.dram_tensor("out_x", (P, B, H), _mb.dt.float32, kind="ExternalOutput").ap())
    build(nc, *args)
    r = run_bass_kernel_spmd(nc, [arrays], core_ids=[0])
    return r.results[0]["out_x"].transpose(1, 0, 2)
```
